# Optimizing a Trainium2 kernel written in Bass

```python
import numpy as np
import jax
import jax.numpy as jnp

def _softmax(x, axis=-1):
    return jax.nn.softmax(x, axis=axis)

def _gelu(x):
    return jax.nn.gelu(x, approximate=True)

def _silu(x):
    return jax.nn.silu(x)

def _sigmoid(x):
    return jax.nn.sigmoid(x)

def _layernorm(x, axis=-1, eps=1e-05):
    m = jnp.mean(x, axis=axis, keepdims=True)
    v = jnp.var(x, axis=axis, keepdims=True)
    return (x - m) / jnp.sqrt(v + eps)

def _scatter_add(tgt, idx, src, axis=0):
    return tgt.at[idx].add(src)

def _segment_sum(src, seg, n):
    return jax.ops.segment_sum(src, seg, n)
kernel_name = 'mk_vit_tower_postln_d1_tok_img768_r4_f451af'

def setup_inputs(seed: int=0):
    np.random.seed(seed)
    _w = jnp.asarray

    def _rec_inputs():
        import jax
        import jax.numpy as jnp
        _rk = jax.random.key(seed)
        x = 7.57192e-06 + 1.00007 * jax.random.normal(jax.random.fold_in(_rk, 1), (64, 3, 112, 112), jnp.float32)
        return x
    x = _rec_inputs()

    def _L0_tok_setup():
        import jax, jax.numpy as jnp
        import numpy as np
        PATCH = 16
        EPS = 1e-05

        def _conv_offsets(x, offset_w, offset_b):
            off = jax.lax.conv_general_dilated(x, offset_w, window_strides=(PATCH, PATCH), padding='VALID', dimension_numbers=('NCHW', 'OIHW', 'NCHW'))
            return off + offset_b[None, :, None, None]

        def _deform_conv(x, offset_w, offset_b, dconv_w):
            B, C, H, W = x.shape
            kh = kw = PATCH
            K = kh * kw
            Ho, Wo = (H // PATCH, W // PATCH)
            off = _conv_offsets(x, offset_w, offset_b)
            off = off.reshape(B, K, 2, Ho, Wo)
            dy = off[:, :, 0].transpose(0, 2, 3, 1)
            dx = off[:, :, 1].transpose(0, 2, 3, 1)
            ii, jj = jnp.meshgrid(jnp.arange(kh), jnp.arange(kw), indexing='ij')
            ki = ii.reshape(-1).astype(x.dtype)
            kj = jj.reshape(-1).astype(x.dtype)
            base_y = (jnp.arange(Ho, dtype=x.dtype) * PATCH)[:, None] + ki[None, :]
            base_x = (jnp.arange(Wo, dtype=x.dtype) * PATCH)[:, None] + kj[None, :]
            py = base_y[None, :, None, :] + dy
            px = base_x[None, None, :, :] + dx
            y0 = jnp.floor(py)
            x0 = jnp.floor(px)
            wy1 = py - y0
            wx1 = px - x0
            wy0 = 1.0 - wy1
            wx0 = 1.0 - wx1
            y0i = y0.astype(jnp.int32)
            x0i = x0.astype(jnp.int32)
            y1i = y0i + 1
            x1i = x0i + 1
            xt = x.transpose(0, 2, 3, 1)
            bidx = jnp.arange(B)[:, None, None, None]

            def gather(yi, xi):
                ok = ((yi >= 0) & (yi < H) & (xi >= 0) & (xi < W)).astype(x.dtype)
                v = xt[bidx, jnp.clip(yi, 0, H - 1), jnp.clip(xi, 0, W - 1)]
                return v * ok[..., None]
            sampled = gather(y0i, x0i) * (wy0 * wx0)[..., None] + gather(y0i, x1i) * (wy0 * wx1)[..., None] + gather(y1i, x0i) * (wy1 * wx0)[..., None] + gather(y1i, x1i) * (wy1 * wx1)[..., None]
            Wk = dconv_w.reshape(dconv_w.shape[0], C, K)
            out = jnp.einsum('bhwkc,ock->bohw', sampled, Wk)
            return out
        key = jax.random.key(seed)
        ks = jax.random.split(key, 3)
        B, C, H, W = (64, 3, 224, 224)
        O = 192
        x = jax.random.normal(ks[0], (B, C, H, W), jnp.float32)
        offset_w = jax.random.normal(ks[1], (2 * PATCH * PATCH, C, PATCH, PATCH), jnp.float32) * 0.01
        offset_b = jnp.zeros((2 * PATCH * PATCH,), jnp.float32)
        dconv_w = jax.random.normal(ks[2], (O, C, PATCH, PATCH), jnp.float32) * 0.02
        bn_gamma = jnp.ones((O,), jnp.float32)
        bn_beta = jnp.zeros((O,), jnp.float32)
        return {'x': x, 'offset_w': offset_w, 'offset_b': offset_b, 'dconv_w': dconv_w, 'bn_gamma': bn_gamma, 'bn_beta': bn_beta}
    _L0_tok_all = _L0_tok_setup()
    _L0_tok_in = {k: v for k, v in _L0_tok_all.items() if k in ('offset_w', 'offset_b', 'dconv_w', 'bn_gamma', 'bn_beta')}
    del _L0_tok_all

    def _L0_attn_setup():
        import jax, jax.numpy as jnp
        import numpy as np
        DIM = 192
        NUM_HEADS = 12
        EFF_HEADS = NUM_HEADS // 2
        HEAD_DIM = DIM // NUM_HEADS
        LAMBDA_INIT = 0.8
        EPS = 1e-05
        key = jax.random.key(seed)
        ks = jax.random.split(key, 12)
        B, N = (4, 512)
        s = 1.0 / np.sqrt(DIM)
        return {'x': jax.random.normal(ks[0], (B, N, DIM), dtype=jnp.float32), 'Wq': jax.random.normal(ks[1], (DIM, DIM), dtype=jnp.float32) * s, 'bq': jnp.zeros((DIM,), dtype=jnp.float32), 'Wk': jax.random.normal(ks[2], (DIM, DIM), dtype=jnp.float32) * s, 'bk': jnp.zeros((DIM,), dtype=jnp.float32), 'Wv': jax.random.normal(ks[3], (DIM, DIM), dtype=jnp.float32) * s, 'bv': jnp.zeros((DIM,), dtype=jnp.float32), 'Wo': jax.random.normal(ks[4], (DIM, DIM), dtype=jnp.float32) * s, 'bo': jnp.zeros((DIM,), dtype=jnp.float32), 'lambda_q1': jax.random.normal(ks[5], (HEAD_DIM,), dtype=jnp.float32) * 0.1, 'lambda_k1': jax.random.normal(ks[6], (HEAD_DIM,), dtype=jnp.float32) * 0.1, 'lambda_q2': jax.random.normal(ks[7], (HEAD_DIM,), dtype=jnp.float32) * 0.1, 'lambda_k2': jax.random.normal(ks[8], (HEAD_DIM,), dtype=jnp.float32) * 0.1, 'norm_weight': jnp.ones((2 * HEAD_DIM,), dtype=jnp.float32)}
    _L0_attn_all = _L0_attn_setup()
    _L0_attn_in = {k: v for k, v in _L0_attn_all.items() if k in ('Wq', 'bq', 'Wk', 'bk', 'Wv', 'bv', 'Wo', 'bo', 'lambda_q1', 'lambda_k1', 'lambda_q2', 'lambda_k2', 'norm_weight')}
    del _L0_attn_all

    def _L0_ffn_setup():
        import jax, jax.numpy as jnp
        import numpy as np
        B, T, C, H, E, TOPK, DR = (2, 512, 192, 768, 8, 2, 24)

        def _normalize(v, axis=-1, eps=1e-12):
            return v / jnp.maximum(jnp.linalg.norm(v, axis=axis, keepdims=True), eps)
        key = jax.random.key(seed)
        ks = jax.random.split(key, 16)
        std = 0.02
        n = lambda k, shape, s=std: (s * jax.random.normal(k, shape)).astype(jnp.float32)
        emb = jax.random.normal(ks[3], (E, DR), dtype=jnp.float32)
        emb = emb / (jnp.linalg.norm(emb, axis=-1, keepdims=True) + 1e-08)
        return {'x': jax.random.normal(ks[0], (B, T, C), dtype=jnp.float32), 'router_w': n(ks[1], (E, C)), 'probe_w': n(ks[2], (DR, C)), 'router_emb': emb, 'fatigue': jnp.zeros((E,), jnp.float32), 'energy': jnp.ones((E,), jnp.float32), 'w_fast1': n(ks[4], (E, C, H)), 'w_slow1': n(ks[5], (E, C, H)), 'h_fast1': n(ks[6], (E, C, H), 0.005), 'm_gate1': jax.random.uniform(ks[7], (E,), dtype=jnp.float32), 'b1': jnp.zeros((E, H), jnp.float32), 'w_fast2': n(ks[8], (E, H, C)), 'w_slow2': n(ks[9], (E, H, C)), 'h_fast2': n(ks[10], (E, H, C), 0.005), 'm_gate2': jax.random.uniform(ks[11], (E,), dtype=jnp.float32), 'b2': jnp.zeros((E, C), jnp.float32)}
    _L0_ffn_all = _L0_ffn_setup()
    _L0_ffn_in = {k: v for k, v in _L0_ffn_all.items() if k in ('router_w', 'probe_w', 'router_emb', 'fatigue', 'energy', 'w_fast1', 'w_slow1', 'h_fast1', 'm_gate1', 'b1', 'w_fast2', 'w_slow2', 'h_fast2', 'm_gate2', 'b2')}
    del _L0_ffn_all
    return {'x': x, 'L0_tok_offset_w': _L0_tok_in['offset_w'], 'L0_tok_offset_b': _L0_tok_in['offset_b'], 'L0_tok_dconv_w': _L0_tok_in['dconv_w'], 'L0_tok_bn_gamma': _L0_tok_in['bn_gamma'], 'L0_tok_bn_beta': _L0_tok_in['bn_beta'], 'L0_attn_Wq': _L0_attn_in['Wq'], 'L0_attn_bq': _L0_attn_in['bq'], 'L0_attn_Wk': _L0_attn_in['Wk'], 'L0_attn_bk': _L0_attn_in['bk'], 'L0_attn_Wv': _L0_attn_in['Wv'], 'L0_attn_bv': _L0_attn_in['bv'], 'L0_attn_Wo': _L0_attn_in['Wo'], 'L0_attn_bo': _L0_attn_in['bo'], 'L0_attn_lambda_q1': _L0_attn_in['lambda_q1'], 'L0_attn_lambda_k1': _L0_attn_in['lambda_k1'], 'L0_attn_lambda_q2': _L0_attn_in['lambda_q2'], 'L0_attn_lambda_k2': _L0_attn_in['lambda_k2'], 'L0_attn_norm_weight': _L0_attn_in['norm_weight'], 'L0_ffn_router_w': _L0_ffn_in['router_w'], 'L0_ffn_probe_w': _L0_ffn_in['probe_w'], 'L0_ffn_router_emb': _L0_ffn_in['router_emb'], 'L0_ffn_fatigue': _L0_ffn_in['fatigue'], 'L0_ffn_energy': _L0_ffn_in['energy'], 'L0_ffn_w_fast1': _L0_ffn_in['w_fast1'], 'L0_ffn_w_slow1': _L0_ffn_in['w_slow1'], 'L0_ffn_h_fast1': _L0_ffn_in['h_fast1'], 'L0_ffn_m_gate1': _L0_ffn_in['m_gate1'], 'L0_ffn_b1': _L0_ffn_in['b1'], 'L0_ffn_w_fast2': _L0_ffn_in['w_fast2'], 'L0_ffn_w_slow2': _L0_ffn_in['w_slow2'], 'L0_ffn_h_fast2': _L0_ffn_in['h_fast2'], 'L0_ffn_m_gate2': _L0_ffn_in['m_gate2'], 'L0_ffn_b2': _L0_ffn_in['b2']}

def reference(x, L0_tok_offset_w, L0_tok_offset_b, L0_tok_dconv_w, L0_tok_bn_gamma, L0_tok_bn_beta, L0_attn_Wq, L0_attn_bq, L0_attn_Wk, L0_attn_bk, L0_attn_Wv, L0_attn_bv, L0_attn_Wo, L0_attn_bo, L0_attn_lambda_q1, L0_attn_lambda_k1, L0_attn_lambda_q2, L0_attn_lambda_k2, L0_attn_norm_weight, L0_ffn_router_w, L0_ffn_probe_w, L0_ffn_router_emb, L0_ffn_fatigue, L0_ffn_energy, L0_ffn_w_fast1, L0_ffn_w_slow1, L0_ffn_h_fast1, L0_ffn_m_gate1, L0_ffn_b1, L0_ffn_w_fast2, L0_ffn_w_slow2, L0_ffn_h_fast2, L0_ffn_m_gate2, L0_ffn_b2):
    import jax
    import jax.numpy as jnp

    def _L0_tok_ref(x, offset_w, offset_b, dconv_w, bn_gamma, bn_beta):
        import jax, jax.numpy as jnp
        import numpy as np
        PATCH = 16
        EPS = 1e-05

        def _conv_offsets(x, offset_w, offset_b):
            off = jax.lax.conv_general_dilated(x, offset_w, window_strides=(PATCH, PATCH), padding='VALID', dimension_numbers=('NCHW', 'OIHW', 'NCHW'))
            return off + offset_b[None, :, None, None]

        def _deform_conv(x, offset_w, offset_b, dconv_w):
            B, C, H, W = x.shape
            kh = kw = PATCH
            K = kh * kw
            Ho, Wo = (H // PATCH, W // PATCH)
            off = _conv_offsets(x, offset_w, offset_b)
            off = off.reshape(B, K, 2, Ho, Wo)
            dy = off[:, :, 0].transpose(0, 2, 3, 1)
            dx = off[:, :, 1].transpose(0, 2, 3, 1)
            ii, jj = jnp.meshgrid(jnp.arange(kh), jnp.arange(kw), indexing='ij')
            ki = ii.reshape(-1).astype(x.dtype)
            kj = jj.reshape(-1).astype(x.dtype)
            base_y = (jnp.arange(Ho, dtype=x.dtype) * PATCH)[:, None] + ki[None, :]
            base_x = (jnp.arange(Wo, dtype=x.dtype) * PATCH)[:, None] + kj[None, :]
            py = base_y[None, :, None, :] + dy
            px = base_x[None, None, :, :] + dx
            y0 = jnp.floor(py)
            x0 = jnp.floor(px)
            wy1 = py - y0
            wx1 = px - x0
            wy0 = 1.0 - wy1
            wx0 = 1.0 - wx1
            y0i = y0.astype(jnp.int32)
            x0i = x0.astype(jnp.int32)
            y1i = y0i + 1
            x1i = x0i + 1
            xt = x.transpose(0, 2, 3, 1)
            bidx = jnp.arange(B)[:, None, None, None]

            def gather(yi, xi):
                ok = ((yi >= 0) & (yi < H) & (xi >= 0) & (xi < W)).astype(x.dtype)
                v = xt[bidx, jnp.clip(yi, 0, H - 1), jnp.clip(xi, 0, W - 1)]
                return v * ok[..., None]
            sampled = gather(y0i, x0i) * (wy0 * wx0)[..., None] + gather(y0i, x1i) * (wy0 * wx1)[..., None] + gather(y1i, x0i) * (wy1 * wx0)[..., None] + gather(y1i, x1i) * (wy1 * wx1)[..., None]
            Wk = dconv_w.reshape(dconv_w.shape[0], C, K)
            out = jnp.einsum('bhwkc,ock->bohw', sampled, Wk)
            return out
        B = x.shape[0]
        y = _deform_conv(x, offset_w, offset_b, dconv_w)
        mean = jnp.mean(y, axis=(0, 2, 3), keepdims=True)
        var = jnp.mean((y - mean) ** 2, axis=(0, 2, 3), keepdims=True)
        yn = (y - mean) * jax.lax.rsqrt(var + EPS)
        yn = yn * bn_gamma[None, :, None, None] + bn_beta[None, :, None, None]
        ya = jax.nn.gelu(yn, approximate=False)
        O, Ho, Wo = (ya.shape[1], ya.shape[2], ya.shape[3])
        return ya.reshape(B, O, Ho * Wo).transpose(0, 2, 1)

    def _L0_attn_ref(x, Wq, bq, Wk, bk, Wv, bv, Wo, bo, lambda_q1, lambda_k1, lambda_q2, lambda_k2, norm_weight):
        import jax, jax.numpy as jnp
        import numpy as np
        DIM = 192
        NUM_HEADS = 12
        EFF_HEADS = NUM_HEADS // 2
        HEAD_DIM = DIM // NUM_HEADS
        LAMBDA_INIT = 0.8
        EPS = 1e-05
        B, N, _ = x.shape
        scaling = HEAD_DIM ** (-0.5)
        q = x @ Wq + bq
        k = x @ Wk + bk
        v = x @ Wv + bv
        q = q.reshape(B, N, 2 * EFF_HEADS, HEAD_DIM).transpose(0, 2, 1, 3) * scaling
        k = k.reshape(B, N, 2 * EFF_HEADS, HEAD_DIM).transpose(0, 2, 1, 3)
        v = v.reshape(B, N, EFF_HEADS, 2 * HEAD_DIM).transpose(0, 2, 1, 3)
        scores = jnp.einsum('bhqd,bhkd->bhqk', q, k)
        probs = jax.nn.softmax(scores, axis=-1)
        probs = probs.reshape(B, EFF_HEADS, 2, N, N)
        lam1 = jnp.exp(jnp.sum(lambda_q1 * lambda_k1))
        lam2 = jnp.exp(jnp.sum(lambda_q2 * lambda_k2))
        lam = lam1 - lam2 + LAMBDA_INIT
        diff = probs[:, :, 0] - lam * probs[:, :, 1]
        out = jnp.einsum('bhqk,bhkd->bhqd', diff, v)
        rms = jax.lax.rsqrt(jnp.mean(out * out, axis=-1, keepdims=True) + EPS)
        out = out * rms * norm_weight * (1.0 - LAMBDA_INIT)
        out = out.transpose(0, 2, 1, 3).reshape(B, N, DIM)
        return out @ Wo + bo

    def _L0_ffn_ref(x, router_w, probe_w, router_emb, fatigue, energy, w_fast1, w_slow1, h_fast1, m_gate1, b1, w_fast2, w_slow2, h_fast2, m_gate2, b2):
        import jax, jax.numpy as jnp
        import numpy as np
        B, T, C, H, E, TOPK, DR = (2, 512, 192, 768, 8, 2, 24)

        def _normalize(v, axis=-1, eps=1e-12):
            return v / jnp.maximum(jnp.linalg.norm(v, axis=axis, keepdims=True), eps)
        Bd, Td, Cd = x.shape
        logits = jnp.einsum('btc,ec->bte', x, router_w)
        tok_proxy = x.mean(axis=-1, keepdims=True)
        router_gain = jnp.linalg.norm(router_emb, axis=-1)
        base_bias = 0.02 * tok_proxy
        gain_bias = 0.02 * tok_proxy * router_gain
        tok_unit = _normalize(jnp.einsum('btc,dc->btd', x, probe_w))
        align_bias = 0.02 * jnp.einsum('btd,ed->bte', tok_unit, _normalize(router_emb))
        logits = logits + base_bias + gain_bias + align_bias + 0.1 * energy - 0.1 * fatigue
        g, idx = jax.lax.top_k(logits, TOPK)
        gates = jax.nn.softmax(g, axis=-1)
        N = Bd * Td
        gates_full = jnp.zeros((N, E), x.dtype).at[jnp.arange(N)[:, None], idx.reshape(N, TOPK)].set(gates.reshape(N, TOPK))
        flat_x = x.reshape(N, Cd)

        def body(acc, p):
            wf1, ws1, hf1, mg1, bb1, wf2, ws2, hf2, mg2, bb2, ge = p
            W1 = wf1 + mg1 * ws1 + hf1
            h = jnp.square(jnp.maximum(flat_x @ W1 + bb1, 0.0))
            W2 = wf2 + mg2 * ws2 + hf2
            y = h @ W2 + bb2
            return (acc + ge[:, None] * y, None)
        out, _ = jax.lax.scan(body, jnp.zeros((N, Cd), x.dtype), (w_fast1, w_slow1, h_fast1, m_gate1, b1, w_fast2, w_slow2, h_fast2, m_gate2, b2, gates_full.T))
        return out.reshape(Bd, Td, Cd)
    h = _L0_tok_ref(x, L0_tok_offset_w, L0_tok_offset_b, L0_tok_dconv_w, L0_tok_bn_gamma, L0_tok_bn_beta)
    h = _layernorm(h + _L0_attn_ref(h, L0_attn_Wq, L0_attn_bq, L0_attn_Wk, L0_attn_bk, L0_attn_Wv, L0_attn_bv, L0_attn_Wo, L0_attn_bo, L0_attn_lambda_q1, L0_attn_lambda_k1, L0_attn_lambda_q2, L0_attn_lambda_k2, L0_attn_norm_weight), axis=-1)
    h = _layernorm(h + _L0_ffn_ref(h, L0_ffn_router_w, L0_ffn_probe_w, L0_ffn_router_emb, L0_ffn_fatigue, L0_ffn_energy, L0_ffn_w_fast1, L0_ffn_w_slow1, L0_ffn_h_fast1, L0_ffn_m_gate1, L0_ffn_b1, L0_ffn_w_fast2, L0_ffn_w_slow2, L0_ffn_h_fast2, L0_ffn_m_gate2, L0_ffn_b2), axis=-1)
    return h

_drawn_inputs = setup_inputs


def setup_inputs(seed=0):
    import zlib

    import numpy as np

    out = dict(_drawn_inputs(seed))
    spreads = {'L0_tok_offset_b': (0.0, 0.1),
     'L0_tok_bn_gamma': (1.0, 0.2),
     'L0_tok_bn_beta': (0.0, 0.1),
     'L0_attn_bq': (0.0, 0.1),
     'L0_attn_bk': (0.0, 0.8),
     'L0_attn_bv': (0.0, 0.1),
     'L0_attn_bo': (0.0, 0.1),
     'L0_attn_norm_weight': (1.0, 0.2),
     'L0_ffn_fatigue': (0.0, 0.46),
     'L0_ffn_energy': (1.0, 0.6),
     'L0_ffn_b1': (0.0, 0.348),
     'L0_ffn_b2': (0.0, 0.1)}
    factors = {'L0_attn_lambda_q1': 4.355,
     'L0_attn_lambda_q2': 2.696,
     'L0_ffn_probe_w': 5.944,
     'L0_ffn_router_emb': 5.608,
     'L0_ffn_h_fast1': 3.633,
     'L0_ffn_m_gate1': 2.971,
     'L0_ffn_h_fast2': 4.364,
     'L0_ffn_m_gate2': 3.728}
    for name, (base, spread) in spreads.items():
        noise = np.random.default_rng([zlib.crc32(name.encode()), seed]).standard_normal(out[name].shape)
        drawn = base * np.exp(spread * noise) if base else spread * noise
        out[name] = jnp.asarray(drawn.astype(out[name].dtype))
    for name, factor in factors.items():
        out[name] = (out[name] * factor).astype(out[name].dtype)
    return out
```

```python
from contextlib import ExitStack

import concourse.bass as bass
from concourse import mybir

F32 = mybir.dt.float32
I32 = mybir.dt.int32
U32 = mybir.dt.uint32
ALU = mybir.AluOpType
ACT = mybir.ActivationFunctionType
AX = mybir.AxisListType

B, C, IMG = 64, 3, 112
PT = 16
NP = IMG // PT
K = PT * PT
O = 192
HO = O // 2
BG = 16
STR = NP * BG
G = B // BG
U = G * NP
N = NP * NP
T = B * N
EPS = 1e-5
TP = T + 16
PAIRS = B // 2
HD = 16
SCALE = HD ** -0.5
LAMBDA_INIT = 0.8
E, H, DR = 8, 768, 24
RC = 2 * E + DR
RT = 128
TILES = -(-(2 * T) // RT) + E - 1
SLOTS = TILES * RT
YRING = 8
PICKED = 21
AGGREGATED = 50

R = 2
TAPS = 2 * R + 1
XR, XC = PT + 2 * R, IMG + 2 * R
FAR_ROWS = FAR_COLS = IMG
BLK = 2 * C
NPROD = TAPS * C
PRING = 5
POOL_PRODS = (6, 13)
DVE_PRODS = tuple(n for n in range(NPROD) if n not in POOL_PRODS)
NDVE, NPOOL = len(DVE_PRODS), len(POOL_PRODS)
XDMA = NP * C


def strided(view, offset, dims):
    return bass.AP(tensor=view.tensor, offset=view.offset + offset, ap=[list(view.ap[0])] + [list(d) for d in dims])


def tokenizer(nc, d, YT, dwT, far, ident, ones):
    with ExitStack() as ctx:
        def sb(name, shape, dt=F32):
            return ctx.enter_context(nc.sbuf_tensor(name, shape, dt))

        def sem(name):
            return ctx.enter_context(nc.semaphore(name))

        def ps(name, banks):
            return ctx.enter_context(nc.psum_tensor(name, [128, banks * 512], F32))

        xs = [sb(f"xs{s}", [STR, C, XR, XC]) for s in range(2)]
        prods = [sb(f"prod{s}", [STR, TAPS, K]) for s in range(PRING)]
        wts = [sb(f"wts{i}", [STR, TAPS, K]) for i in range(TAPS)]
        hats = [sb(f"hats{s}", [STR, 2, TAPS, K]) for s in range(2)]
        dist = sb("dist", [STR, 2, TAPS, K])
        patch = [sb(f"patch{s}", [STR, C, K]) for s in range(2)]
        xT = [sb(f"xT{s}", [128, BLK, STR]) for s in range(2)]
        smpT = [sb(f"smpT{s}", [128, BLK, STR]) for s in range(2)]
        off = [sb(f"off{s}", [STR, 2, K]) for s in range(2)]
        owT = sb("owT", [128, BLK, 2, K])
        obias = sb("obias", [1, 2 * K])
        tapb = sb("tapb", [STR, TAPS])
        reach = sb("reach", [STR, 1])
        beyond = sb("beyond", [STR, 2, 2, K])
        excess = sb("excess", [STR, U])
        worst = sb("worst", [STR, 1])
        ow_raw = [prods[t][:, :, :] for t in range(4)]

        psT = ps("psT", 2)
        psO = ps("psO", 1)
        psS = [ps(f"psS{s}", 2) for s in range(2)]
        psY = ps("psY", 1)

        w_in = sem("w_in")
        w_turned = sem("w_turned")
        w_copied = sem("w_copied")
        consts = sem("consts")
        halo_zero = sem("halo_zero")
        xs_in = [sem(f"xs_in{s}") for s in range(2)]
        patch_ready = sem("patch_ready")
        patch_free = sem("patch_free")
        turned = sem("turned")
        xT_ready = sem("xT_ready")
        offs_done = sem("offs_done")
        off_ready = sem("off_ready")
        off_stored = [sem(f"off_stored{s}") for s in range(2)]
        dist_ready = sem("dist_ready")
        hats_ready = sem("hats_ready")
        wts_ready = sem("wts_ready")
        wts_free = sem("wts_free")
        prod_dve = sem("prod_dve")
        prod_pool = sem("prod_pool")
        prod_free = sem("prod_free")
        summed = sem("summed")
        smp_ready = sem("smp_ready")
        y_done = sem("y_done")
        y_ready = sem("y_ready")
        checked = sem("checked")
        worst_ready = sem("worst_ready")
        worst_summed = sem("worst_summed")
        far_ready = sem("far_ready")

        def block_cols(psum, blk, rows=128, cols=STR):
            at = blk * STR if blk < 4 else 512 + (blk - 4) * STR
            return psum[0:rows, at:at + cols]

        def two_banks(psum):
            return ((psum[:, 0:4 * STR].rearrange("p (b t) -> p b t", b=4), 0, 4),
                    (psum[:, 512:512 + 2 * STR].rearrange("p (b t) -> p b t", b=2), 4, 6))

        def product(eng, n, pw, slot):
            i, c = divmod(n, C)
            view = xs[slot][:, :, :, :]
            pixels = strided(view, (c * XR + i) * XC + pw * PT, [[1, TAPS], [XC, PT], [1, PT]])
            shape = "p j (r w) -> p j r w"
            return eng.tensor_tensor(prods[n % PRING][:, :, :].rearrange(shape, r=PT), pixels,
                                     wts[i][:, :, :].rearrange(shape, r=PT), ALU.mult)

        with nc.Block() as block:
            @block.sync
            def _(sp):
                for t in range(4):
                    raw = bass.AP(tensor=prods[t][:, :, :].tensor, offset=0, ap=[[TAPS * K, STR], [1, C * K]])
                    sp.dma_start(raw, d["offset_w"].rearrange("o c h w -> o (c h w)")[t * STR:(t + 1) * STR, :]).then_inc(w_in, 16)
                raw = bass.AP(tensor=prods[4][:, :, :].tensor, offset=0, ap=[[TAPS * K, 64], [1, C * K]])
                sp.dma_start(raw, d["offset_w"].rearrange("o c h w -> o (c h w)")[4 * STR:512, :]).then_inc(w_in, 16)
                for t in range(2):
                    raw = bass.AP(tensor=wts[t][:, :, :].tensor, offset=0, ap=[[TAPS * K, HO], [1, C * K]])
                    sp.dma_start(raw, d["dconv_w"].rearrange("o c h w -> o (c h w)")[t * HO:(t + 1) * HO, :]).then_inc(w_in, 16)
                sp.dma_start(obias[:, :], d["offset_b"].rearrange("(a n) -> a n", a=1)).then_inc(w_in, 16)

                def load_strips(g):
                    s = g % 2
                    images = d["x"][g * BG:(g + 1) * BG]
                    if g < 2:
                        sp.wait_ge(halo_zero, g + 1)
                    else:
                        done = (g - 1) * NP
                        sp.wait_ge(prod_dve, NDVE * done)
                        sp.wait_ge(prod_pool, NPOOL * done)
                        sp.wait_ge(patch_ready, done)
                    for q in range(NP):
                        r0, r1 = max(q * PT - R, 0), min((q + 1) * PT + R, IMG)
                        top = r0 - (q * PT - R)
                        for c in range(C):
                            sp.dma_start(xs[s][q * BG:(q + 1) * BG, c, top:top + r1 - r0, R:R + IMG],
                                         images[:, c, r0:r1, :]).then_inc(xs_in[s], 16)

                load_strips(0)
                load_strips(1)
                for u in range(U):
                    sp.wait_ge(off_ready, u + 1)
                    sp.dma_start(d["off_all"][u // NP, :, u % NP, :], off[u % 2][:, :, :].rearrange("p a k -> p (a k)"))\
                        .then_inc(off_stored[u % 2], 16)
                    if u % NP == 2 and NP < u < (G - 1) * NP:
                        load_strips(u // NP + 1)
                for s in range(2):
                    sp.wait_ge(off_stored[s], 16 * (U // 2))

            @block.gpsimd
            def _(pool):
                pool.memset(ident[:, :], 0.0).then_inc(consts, 1)
                pool.memset(ones[:, :], 1.0).then_inc(consts, 1)
                pool.memset(tapb[:, 0:1], float(R))
                pool.memset(reach[:, :], -2.0 * R)
                for j in range(1, TAPS):
                    last = pool.memset(tapb[:, j:j + 1], float(R - j))
                last.then_inc(consts, 1)
                pool.wait_ge(consts, 3)
                pool.affine_select(out=ident[:, :], in_=ident[:, :], compare_op=ALU.not_equal, fill=1.0, base=0,
                                   pattern=[[-1, 128]], channel_multiplier=1).then_inc(consts, 1)
                pool.wait_ge(w_copied, 6 + 3)
                with pool.Fori(0, 2) as it:
                    for k in range(U // 2):
                        s, slot = k % 2, (k // NP) % 2
                        if k % NP == 0:
                            pool.wait_ge(xs_in[slot], (it + 1) * (16 * XDMA))
                        pool.wait_ge(hats_ready, it * (U // 2) + (k + 1))
                        n = 0
                        for i in range(TAPS):
                            pool.wait_ge(wts_free, it * (TAPS * U // 2) + (TAPS * k + i + 1))
                            pool.tensor_tensor(wts[i][:, :, :],
                                               strided(hats[s][:, :, :, :], i * K, [[0, TAPS], [1, K]]),
                                               hats[s][:, 1, :, :], ALU.mult).then_inc(wts_ready, 1)
                            for c in range(C):
                                n = C * i + c
                                if n in POOL_PRODS:
                                    pool.wait_ge(wts_ready, it * (TAPS * U // 2) + (TAPS * k + i + 1))
                                    pool.wait_ge(prod_free, it * (NPROD * U // 2) + (NPROD * k + n + 1))
                                    product(pool, n, k % NP, slot).then_inc(prod_pool, 1)

            @block.vector
            def _(dve):
                for s in range(2):
                    dve.memset(xs[s][:, :, :, 0:R], 0.0)
                    dve.memset(xs[s][:, :, :, XC - R:XC], 0.0)
                    dve.memset(xs[s][0:BG, :, 0:R, R:R + IMG], 0.0)
                    dve.memset(xs[s][STR - BG:STR, :, XR - R:XR, R:R + IMG], 0.0).then_inc(halo_zero, 1)
                dve.memset(YT[:, :, T:TP], 0.0)
                with dve.Fori(0, 2) as it:
                    for k in range(U // 2):
                        g2, pw = divmod(k, NP)
                        if pw == 0:
                            dve.wait_ge(xs_in[g2], (it + 1) * (16 * XDMA))
                        for n in DVE_PRODS:
                            if n % C == 0 or n == DVE_PRODS[0]:
                                dve.wait_ge(wts_ready, it * (TAPS * U // 2) + (TAPS * k + n // C + 1))
                            elif (n - 1) in POOL_PRODS and (n - 1) % C == 0:
                                dve.wait_ge(wts_ready, it * (TAPS * U // 2) + (TAPS * k + n // C + 1))
                            dve.wait_ge(prod_free, it * (NPROD * U // 2) + (NPROD * k + n + 1))
                            product(dve, n, pw, g2).then_inc(prod_dve, 1)
                        dve.wait_ge(y_done, it * (U // 2) + (k + 1))
                        place = YT[:, :, bass.ds(it * (2 * BG * N) + (g2 * BG * N), BG * N)]\
                            .rearrange("c h (b q w) -> c h q b w", b=BG, q=NP)[:, :, :, :, pw]
                        dve.tensor_scalar(place, psY[0:HO, 0:2 * STR].rearrange("c (h q b) -> c h q b", h=2, q=NP),
                                          1.0, None, ALU.mult).then_inc(y_ready, 1)
                dve.wait_ge(checked, U)
                dve.tensor_reduce(worst[:, :], excess[:, :], AX.X, ALU.max).then_inc(worst_ready, 1)
                dve.wait_ge(worst_summed, 1)
                dve.tensor_scalar(far[:, :], psT[0:1, 0:1], 0.0, None, ALU.is_gt).then_inc(far_ready, 1)
                dve.wait_ge(far_ready, 1)

            @block.scalar
            def _(act):
                for blk in range(BLK):
                    act.wait_ge(w_turned, blk + 1)
                    act.activation(owT[:, blk, :, :].rearrange("p t k -> p k t"),
                                   (psO if blk % 2 == 0 else psY)[:, 0:512].rearrange("p (k t) -> p k t", t=2),
                                   ACT.Copy).then_inc(w_copied, 1)
                for t in range(3):
                    act.wait_ge(w_turned, BLK + t + 1)
                    act.activation(dwT[:, 2 * t:2 * t + 2, :],
                                   (psO if t % 2 == 0 else psY)[:, 0:2 * O].rearrange("p (b o) -> p b o", b=2),
                                   ACT.Copy).then_inc(w_copied, 1)

                def copy_patch(u):
                    g, pw = divmod(u, NP)
                    act.wait_ge(xs_in[g % 2], 16 * XDMA * (g // 2 + 1))
                    act.wait_ge(patch_free, u + 1)
                    act.activation(patch[u % 2][:, :, :].rearrange("p c (r w) -> p c r w", r=PT),
                                   xs[g % 2][:, :, R:R + PT, R + pw * PT:R + (pw + 1) * PT],
                                   ACT.Copy).then_inc(patch_ready, 1)

                def copy_xT(u):
                    act.wait_ge(turned, u + 1)
                    if u >= 2:
                        act.wait_ge(offs_done, u - 1)
                    for view, a, b in two_banks(psT):
                        last = act.activation(xT[u % 2][:, a:b, :], view, ACT.Copy)
                    last.then_inc(xT_ready, 1)

                def copy_off(u):
                    act.wait_ge(offs_done, u + 1)
                    if u >= 2:
                        act.wait_ge(off_stored[u % 2], 16 * (u // 2))
                    act.activation(off[u % 2][:, :, :].rearrange("p a k -> p (a k)"), psO[0:STR, :],
                                   ACT.Copy).then_inc(off_ready, 1)

                def make_hats(u):
                    act.wait_ge(off_ready, u + 1)
                    if u >= 1:
                        act.wait_ge(hats_ready, u)
                        act.wait_ge(checked, u)
                    for j in range(TAPS):
                        last = act.activation(dist[:, :, j, :], off[u % 2][:, :, :], ACT.Abs, bias=tapb[:, j:j + 1])
                    last.then_inc(dist_ready, 1)
                    act.wait_ge(dist_ready, u + 1)
                    if u >= 2:
                        act.wait_ge(wts_ready, TAPS * (u - 1))
                    act.activation(hats[u % 2][:, :, :, :], dist[:, :, :, :], ACT.Relu, bias=ones[0:STR, 0:1],
                                   scale=-1.0).then_inc(hats_ready, 1)
                    act.activation(beyond[:, :, :, :], strided(dist[:, :, :, :], 0, [[TAPS * K, 2], [(TAPS - 1) * K, 2], [1, K]]), ACT.Relu, bias=reach[:, 0:1],
                                   accum_out=excess[:, u:u + 1]).then_inc(checked, 1)

                def copy_sampled(u):
                    act.wait_ge(summed, u + 1)
                    if u >= 2:
                        act.wait_ge(y_done, u - 1)
                    for view, a, b in two_banks(psS[u % 2]):
                        last = act.activation(smpT[u % 2][:, a:b, :], view, ACT.Copy)
                    last.then_inc(smp_ready, 1)

                act.wait_ge(consts, 4)
                copy_patch(0)
                copy_patch(1)
                for u in range(2):
                    copy_xT(u)
                    copy_off(u)
                    make_hats(u)
                copy_patch(2)
                copy_xT(2)
                for u in range(U):
                    if u + 3 < U:
                        copy_patch(u + 3)
                    copy_sampled(u)
                    if u + 2 < U:
                        copy_off(u + 2)
                    if u + 3 < U:
                        copy_xT(u + 3)
                    if u + 2 < U:
                        make_hats(u + 2)

            @block.tensor
            def _(pe):
                pe.wait_ge(consts, 4)
                pe.wait_ge(w_in, 16 * 8)
                for blk in range(BLK):
                    if blk >= 2:
                        pe.wait_ge(w_copied, blk - 1)
                    for t in range(5):
                        rows = STR if t < 4 else 64
                        raw = bass.AP(tensor=prods[t][:, :, :].tensor, offset=blk * 128, ap=[[TAPS * K, rows], [1, 128]])
                        last = pe.transpose((psO if blk % 2 == 0 else psY)[:, t * STR:t * STR + rows], raw,
                                            ident[0:rows, 0:rows])
                    last.then_inc(w_turned, 1)
                for t in range(3):
                    pe.wait_ge(w_copied, BLK - 1 + t)
                    for b in range(2):
                        for h in range(2):
                            raw = bass.AP(tensor=wts[h][:, :, :].tensor, offset=(2 * t + b) * 128,
                                          ap=[[TAPS * K, HO], [1, 128]])
                            last = pe.transpose((psO if t % 2 == 0 else psY)[:, b * O + h * HO:b * O + (h + 1) * HO],
                                                raw, ident[0:HO, 0:HO])
                    last.then_inc(w_turned, 1)
                pe.wait_ge(w_copied, BLK + 3)
                pe.sem_inc(patch_free, 2)
                pe.sem_inc(wts_free, TAPS)
                pe.sem_inc(prod_free, PRING)

                def turn_patch(u, s, first=False):
                    pe.wait_ge(patch_ready, u + 1)
                    if not first:
                        pe.wait_ge(xT_ready, u)
                    for blk in range(BLK):
                        c, h = divmod(blk, 2)
                        last = pe.transpose(block_cols(psT, blk), patch[s][:, c, h * 128:(h + 1) * 128],
                                            ident[0:STR, 0:STR])
                    last.then_inc(turned, 1)
                    pe.wait_ge(turned, u + 1)
                    pe.sem_inc(patch_free, 1)

                def offsets(u, s, first=False):
                    pe.wait_ge(xT_ready, u + 1)
                    if not first:
                        pe.wait_ge(off_ready, u)
                    pe.matmul(psO[0:STR, :], ones[0:1, 0:STR], obias[:, :].rearrange("p (k t) -> p t k", t=2),
                              start=True, stop=False)
                    for blk in range(BLK):
                        last = pe.matmul(psO[0:STR, :], xT[s][:, blk, :],
                                         owT[:, blk, :, :].rearrange("p a k -> p (a k)"),
                                         start=False, stop=(blk == BLK - 1))
                    last.then_inc(offs_done, 1)

                def sum_taps(u, s):
                    for n in range(NPROD):
                        if n in POOL_PRODS:
                            pe.wait_ge(prod_pool, u * NPOOL + (POOL_PRODS.index(n) + 1))
                        else:
                            pe.wait_ge(prod_dve, u * NDVE + (DVE_PRODS.index(n) + 1))
                        i, c = divmod(n, C)
                        for j in range(TAPS):
                            for h in range(2):
                                blk = 2 * c + h
                                last = pe.matmul(block_cols(psS[s], blk), prods[n % PRING][:, j, h * 128:(h + 1) * 128],
                                                 ident[0:STR, 0:STR], is_transpose=True,
                                                 start=(i == 0 and j == 0 and blk in (0, 4)),
                                                 stop=(i == TAPS - 1 and j == TAPS - 1), skip_group_check=True)
                                if j == TAPS - 1 and h == 0 and c == C - 1:
                                    last.then_inc(wts_free, 1)
                                if n == NPROD - 1 and j == TAPS - 2 and h == 1:
                                    last.then_inc(prod_free, 1)
                        last.then_inc(summed if n == NPROD - 1 else prod_free, 1)

                def project(u, s, first=False):
                    pe.wait_ge(smp_ready, u + 1)
                    if not first:
                        pe.wait_ge(y_ready, u)
                    for h in range(2):
                        for blk in range(BLK):
                            last = pe.matmul(psY[0:HO, h * STR:(h + 1) * STR], dwT[:, blk, h * HO:(h + 1) * HO],
                                             smpT[s][:, blk, :], start=(blk == 0), stop=(blk == BLK - 1))
                    last.then_inc(y_done, 1)

                turn_patch(0, 0, first=True)
                offsets(0, 0, first=True)
                turn_patch(1, 1)
                offsets(1, 1)
                turn_patch(2, 0)
                sum_taps(0, 0)
                offsets(2, 0)
                turn_patch(3, 1)
                project(0, 0, first=True)
                with pe.Fori(0, (U - 4) // 2) as m:
                    for e in range(1, 3):
                        u, s = m * 2 + e, e % 2
                        sum_taps(u, s)
                        offsets(u + 2, s)
                        turn_patch(u + 3, 1 - s)
                        project(u, s)
                for u in range(U - 3, U):
                    sum_taps(u, u % 2)
                    if u + 2 < U:
                        offsets(u + 2, u % 2)
                    if u + 3 < U:
                        turn_patch(u + 3, (u + 3) % 2)
                    project(u, u % 2)
                pe.wait_ge(worst_ready, 1)
                pe.matmul(psT[0:1, 0:1], worst[:, 0:1], ones[0:STR, 0:1], start=True, stop=True).then_inc(worst_summed, 1)


def far_taps(nc, d, YT, dwT, far, ident, ones):
    with ExitStack() as ctx:
        def sb(name, shape, dt=F32):
            return ctx.enter_context(nc.sbuf_tensor(name, shape, dt))

        def sem(name):
            return ctx.enter_context(nc.semaphore(name))

        image = sb("image", [STR, IMG * IMG])
        off = sb("far_off", [STR, NP, 2, K])
        pos = sb("pos", [STR, 2, NP, K])
        base_i = sb("base_i", [STR, 2, NP, K], I32)
        strip_i = sb("strip_i", [STR, 1], I32)
        strip_y = sb("strip_y", [STR, 1])
        base = sb("base", [STR, 2, NP, K])
        tap = sb("tap", [STR, 2])
        dist = sb("far_dist", [STR, NP * K])
        row_w = sb("row_w", [STR, NP * K])
        tap_w = sb("tap_w", [STR, NP * K])
        smp = [sb(f"smp{c}", [STR, NP * K]) for c in range(C)]
        smpT = sb("far_smpT", [128, BLK, STR])
        psT = ctx.enter_context(nc.psum_tensor("far_psT", [128, 1024], F32))
        psY = ctx.enter_context(nc.psum_tensor("far_psY", [128, 512], F32))

        grid = sem("far_grid")
        off_in = sem("far_off_in")
        image_in = sem("image_in")
        off_read = sem("far_off_read")
        image_read = sem("image_read")
        setup = sem("far_setup")
        group_ready = sem("group_ready")
        turned = sem("far_turned")
        smpT_ready = sem("far_smpT_ready")
        y_done = sem("far_y_done")
        y_ready = sem("far_y_ready")

        def is_far(eng):
            return eng.value_load(far[0:1, 0:1], min_val=0, max_val=1) > 0

        with nc.Block() as block:
            @block.sync
            def _(sp):
                with sp.If(is_far(sp)):
                    for g in range(G):
                        if g >= 1:
                            sp.wait_ge(off_read, g)
                        sp.dma_start(off[:, :, :, :].rearrange("p w a k -> p (w a k)"),
                                     d["off_all"][g].rearrange("p w k -> p (w k)")).then_inc(off_in, 16)
                        for c in range(C):
                            if g + c >= 1:
                                sp.wait_ge(image_read, g * C + c)
                            for q in range(NP):
                                sp.dma_start(image[q * BG:(q + 1) * BG, :],
                                             d["x"][g * BG:(g + 1) * BG, c].rearrange("b h w -> b (h w)"))\
                                    .then_inc(image_in, 16)

            @block.gpsimd
            def _(pool):
                with pool.If(is_far(pool)):
                    pool.iota(strip_i[:, :], pattern=[[0, 1]], base=0, channel_multiplier=1)
                    pool.iota(base_i[:, 0, :, :], pattern=[[0, NP], [1, PT], [0, PT]], base=0, channel_multiplier=0)
                    pool.iota(base_i[:, 1, :, :], pattern=[[PT, NP], [0, PT], [1, PT]], base=0,
                              channel_multiplier=0).then_inc(grid, 1)

            @block.vector
            def _(dve):
                with dve.If(is_far(dve)):
                    dve.wait_ge(grid, 1)
                    dve.tensor_scalar(strip_i[:, :], strip_i[:, :], -PT, None, ALU.bitwise_and).then_inc(setup, 1)
                    dve.wait_ge(setup, 1)
                    dve.tensor_copy(strip_y[:, :], strip_i[:, :])
                    dve.tensor_copy(base[:, :, :, :], base_i[:, :, :, :]).then_inc(setup, 1)
                    dve.wait_ge(setup, 2)
                    dve.tensor_scalar(base[:, 0, :, :], base[:, 0, :, :], strip_y[:, 0:1], None, ALU.add)\
                        .then_inc(setup, 1)
                    dve.wait_ge(setup, 3)
                    with dve.Fori(0, G) as g:
                        dve.wait_ge(off_in, (g + 1) * 16)
                        dve.tensor_tensor(pos[:, :, :, :], base[:, :, :, :],
                                          off[:, :, :, :].rearrange("p w a k -> p a w k"), ALU.add).then_inc(off_read, 1)
                        for c in range(C):
                            dve.wait_ge(image_in, g * (16 * NP * C) + 16 * NP * (c + 1))
                            dve.memset(smp[c][:, :], 0.0)
                            dve.memset(tap[:, 0:1], 0.0)
                            dve.drain()
                            with dve.Fori(0, FAR_ROWS) as y:
                                dve.tensor_scalar(tap_w[:, :], pos[:, 0, :, :].rearrange("p w k -> p (w k)"), tap[:, 0:1],
                                                  None, ALU.subtract)
                                dve.drain()
                                dve.scalar_tensor_tensor(out=dist[:, :], in0=tap_w[:, :], scalar=-1.0,
                                                         in1=tap_w[:, :], op0=ALU.mult, op1=ALU.max)
                                dve.drain()
                                dve.tensor_scalar(dist[:, :], dist[:, :], -1.0, 1.0, ALU.mult, ALU.add)
                                dve.memset(tap[:, 1:2], 0.0)
                                dve.drain()
                                dve.tensor_scalar(row_w[:, :], dist[:, :], 0.0, None, ALU.max)
                                dve.drain()
                                with dve.Fori(0, FAR_COLS) as x:
                                    dve.tensor_scalar(tap_w[:, :], pos[:, 1, :, :].rearrange("p w k -> p (w k)"),
                                                      tap[:, 1:2], None, ALU.subtract)
                                    dve.drain()
                                    dve.scalar_tensor_tensor(out=dist[:, :], in0=tap_w[:, :], scalar=-1.0,
                                                             in1=tap_w[:, :], op0=ALU.mult, op1=ALU.max)
                                    dve.drain()
                                    dve.tensor_scalar(dist[:, :], dist[:, :], -1.0, 1.0, ALU.mult, ALU.add)
                                    dve.tensor_scalar(tap[:, 1:2], tap[:, 1:2], 1.0, None, ALU.add)
                                    dve.drain()
                                    dve.scalar_tensor_tensor(out=tap_w[:, :], in0=dist[:, :], scalar=0.0,
                                                             in1=row_w[:, :], op0=ALU.max, op1=ALU.mult)
                                    dve.drain()
                                    dve.scalar_tensor_tensor(out=smp[c][:, :], in0=tap_w[:, :],
                                                             scalar=image[:, bass.ds(y * IMG + x, 1)],
                                                             in1=smp[c][:, :], op0=ALU.mult, op1=ALU.add)
                                    dve.drain()
                                dve.tensor_scalar(tap[:, 0:1], tap[:, 0:1], 1.0, None, ALU.add)
                                dve.drain()
                            dve.sem_inc(image_read, 1)
                        dve.sem_inc(group_ready, 1)
                        for pw in range(NP):
                            dve.wait_ge(y_done, g * NP + (pw + 1))
                            place = YT[:, :, bass.ds(g * (BG * N), BG * N)]\
                                .rearrange("c h (b q w) -> c h q b w", b=BG, q=NP)[:, :, :, :, pw]
                            dve.tensor_scalar(place, psY[0:HO, 0:2 * STR].rearrange("c (h q b) -> c h q b", h=2, q=NP),
                                              1.0, None, ALU.mult).then_inc(y_ready, 1)

            @block.scalar
            def _(act):
                with act.If(is_far(act)):
                    with act.Fori(0, U) as u:
                        act.wait_ge(turned, u + 1)
                        for a, b, at in ((0, 4, 0), (4, 6, 512)):
                            last = act.activation(smpT[:, a:b, :], psT[:, at:at + (b - a) * STR]
                                                  .rearrange("p (b t) -> p b t", t=STR), ACT.Copy)
                        last.then_inc(smpT_ready, 1)

            @block.tensor
            def _(pe):
                with pe.If(is_far(pe)):
                    pe.sem_inc(y_ready, 1)
                    with pe.Fori(0, G) as g:
                        pe.wait_ge(group_ready, g + 1)
                        for pw in range(NP):
                            pe.wait_ge(y_ready, g * NP + (pw + 1))
                            for blk in range(BLK):
                                c, h = divmod(blk, 2)
                                at = blk * STR if blk < 4 else 512 + (blk - 4) * STR
                                last = pe.transpose(psT[:, at:at + STR],
                                                    smp[c][:, pw * K + h * 128:pw * K + (h + 1) * 128],
                                                    ident[0:STR, 0:STR])
                            last.then_inc(turned, 1)
                            pe.wait_ge(smpT_ready, g * NP + (pw + 1))
                            for h in range(2):
                                for blk in range(BLK):
                                    last = pe.matmul(psY[0:HO, h * STR:(h + 1) * STR], dwT[:, blk, h * HO:(h + 1) * HO],
                                                     smpT[:, blk, :], start=(blk == 0), stop=(blk == BLK - 1))
                            last.then_inc(y_done, 1)


def batch_norm(nc, d, YT, HT):
    with ExitStack() as ctx:
        def sb(name, shape, dt=F32):
            return ctx.enter_context(nc.sbuf_tensor(name, shape, dt))

        def sem(name):
            return ctx.enter_context(nc.semaphore(name))

        gb = sb("bn_gb", [HO, 2, 2])
        st = sb("bn_st", [HO, 2, NP, 6])
        mv = sb("bn_mv", [HO, 2, 2])
        aff = sb("bn_aff", [HO, 2, 2])
        tmp = sb("bn_tmp", [HO, 2])
        dev = sb("bn_dev", [HO, 2])
        gb_in = sem("bn_gb_in")
        step = sem("bn_step")
        rooted = sem("bn_rooted")
        h_ready = sem("h_ready")

        with nc.Block() as block:
            @block.sync
            def _(sp):
                for n, w in enumerate(("bn_gamma", "bn_beta")):
                    sp.dma_start(gb[:, n, :], d[w].rearrange("(h c) -> c h", h=2),
                                 allow_slow_non_contiguous=True).then_inc(gb_in, 16)

            @block.vector
            def _(dve):
                for h in range(2):
                    for q in range(NP):
                        last = dve.bn_stats(st[:, h, q, :], YT[:, h, q * (T // NP):(q + 1) * (T // NP)])
                last.then_inc(step, 1)
                dve.wait_ge(step, 1)
                for h in range(2):
                    last = dve.bn_aggr(mv[:, h, :], st[:, h, :, :].rearrange("c q s -> c (q s)"))
                last.then_inc(step, 1)
                dve.wait_ge(step, 2)
                dve.tensor_scalar(tmp[:, :], mv[:, :, 1], EPS, None, ALU.add).then_inc(step, 1)
                dve.wait_ge(rooted, 1)
                dve.reciprocal(tmp[:, :], dev[:, :]).then_inc(step, 1)
                dve.wait_ge(step, 4)
                dve.wait_ge(gb_in, 32)
                dve.tensor_tensor(aff[:, 0, :], tmp[:, :], gb[:, 0, :], ALU.mult).then_inc(step, 1)
                dve.wait_ge(step, 5)
                dve.tensor_tensor(tmp[:, :], mv[:, :, 0], aff[:, 0, :], ALU.mult).then_inc(step, 1)
                dve.wait_ge(step, 6)
                dve.tensor_tensor(aff[:, 1, :], gb[:, 1, :], tmp[:, :], ALU.subtract).then_inc(step, 1)

            @block.scalar
            def _(act):
                act.wait_ge(step, 3)
                act.activation(dev[:, :], tmp[:, :], ACT.Sqrt).then_inc(rooted, 1)
                act.wait_ge(step, 7)
                for h in range(2):
                    act.activation(HT[:, h, 0:T], YT[:, h, 0:T], ACT.Gelu, bias=aff[:, 1, h:h + 1],
                                   scale=aff[:, 0, h:h + 1]).then_inc(h_ready, 1)


def attention(nc, d, HT, OUTS, SSQ, W1, W2, ident, ones):
    with ExitStack() as ctx:
        def sb(name, shape, dt=F32):
            return ctx.enter_context(nc.sbuf_tensor(name, shape, dt))

        def sem(name):
            return ctx.enter_context(nc.semaphore(name))

        def ps(name, banks):
            return ctx.enter_context(nc.psum_tensor(name, [128, banks * 512], F32))

        wqkv = sb("wqkv", [HO, 3, 2, O])
        qk_bias = sb("qk_bias", [HO, 2, 2])
        q_bias = sb("q_bias", [HO, 2])
        bv_row = sb("bv_row", [1, O])
        bv_all = sb("bv_all", [128, O // 2])
        lam_in = sb("lam_in", [1, 4, HD])
        lam_pr = sb("lam_pr", [1, 2, HD])
        lam_sum = sb("lam_sum", [1, 2])
        lam_exp = sb("lam_exp", [1, 2])
        neg_lam = sb("neg_lam", [1, 1])
        head_sign = sb("head_sign", [128, 6, 2])
        head_mask = sb("head_mask", [HO, 6])
        hp = [sb(f"hp{s}", [HO, 2, 128]) for s in range(2)]
        qT = [sb(f"qT{s}", [HO, 2, 128]) for s in range(2)]
        kT = [sb(f"kT{s}", [HO, 2, 2, N]) for s in range(2)]
        kx = [sb(f"kx{s}", [HO, 2, 2, 6, N]) for s in range(2)]
        vals = [sb(f"vals{s}", [128, 2, O // 2]) for s in range(2)]
        top = [sb(f"top{s}", [128, 12]) for s in range(2)]
        den = [sb(f"den{s}", [128, 12]) for s in range(2)]
        coef = [sb(f"coef{s}", [128, 12]) for s in range(2)]
        ex = [sb(f"ex{s}", [128, 12, N]) for s in range(2)]
        pm = [sb(f"pm{s}", [128, 2, 6, 64]) for s in range(2)]
        dT = [sb(f"dT{s}", [128, 3, 128]) for s in range(2)]
        sq = [sb(f"sq{s}", [128, O]) for s in range(2)]
        ssq = [sb(f"ssq{s}", [128, 6]) for s in range(2)]

        stage = [sb(f"stage_{n}", [128, 2 * H]) for n in ("fast", "slow", "h")]
        zero = sb("zero", [128, O])
        gates_row = sb("gates_row", [1, 2, E])
        gates = sb("gates", [128, 2, E])

        psP = ps("psP", 1)
        psV = ps("psV", 1)
        psA = ps("psA", 2)
        psD = ps("psD", 1)
        psX = ps("psX", 2)

        w_in = sem("a_w_in")
        b1_in = sem("b1_in")
        zero_ready = sem("zero_ready")
        slots_zero = sem("slots_zero")
        stage_in = sem("stage_in")
        stage_free = sem("stage_free")
        stage_step = sem("stage_step")
        stage_taken = sem("stage_taken")
        setup = sem("a_setup")
        mask_ready = sem("mask_ready")
        lam_ready = sem("lam_ready")
        lam_expd = sem("lam_expd")
        spread = sem("a_spread")
        hp_ready = sem("hp_ready")
        hp_free = sem("hp_free")
        qk_done = sem("qk_done")
        v_done = sem("v_done")
        q_ready = sem("q_ready")
        k_ready = sem("k_ready")
        kx_ready = sem("kx_ready")
        v_ready = sem("v_ready")
        scored = sem("scored")
        top_ready = sem("top_ready")
        shifted = sem("shifted")
        exped = sem("exped")
        den_ready = sem("den_ready")
        coef_ready = sem("coef_ready")
        pm_ready = sem("pm_ready")
        diffed = sem("diffed")
        dT_ready = sem("dT_ready")
        weighing = sem("weighing")
        av_done = sem("av_done")
        sq_ready = sem("sq_ready")
        ssq_ready = sem("ssq_ready")
        out_ready = sem("out_ready")

        def paired(psum):
            return psum[:, :].rearrange("p (b c) -> p b c", b=2)[:, :, 0:6 * N].rearrange("p b (h k) -> p b h k", k=N)

        def by_head(tile):
            return strided(tile[:, :], 0, [[6, 2], [1, 6], [0, N]])

        def head_order(psum):
            return psum[:, :].rearrange("p (g c) -> p g c", g=2)[:, :, 0:O // 2].rearrange("p g (f v) -> p f g v", f=3)

        with nc.Block() as block:
            @block.sync
            def _(sp):
                for n, w in enumerate(("Wq", "Wk", "Wv")):
                    sp.dma_start(wqkv[:, n, :, :], d[w].rearrange("(k c) o -> c k o", k=2)).then_inc(w_in, 16)
                for n, w in enumerate(("bq", "bk")):
                    sp.dma_start(qk_bias[:, n, :], d[w].rearrange("(h c) -> c h", h=2),
                                 allow_slow_non_contiguous=True).then_inc(w_in, 16)
                sp.dma_start(bv_row[:, :], d["bv"].rearrange("(a n) -> a n", a=1)).then_inc(w_in, 16)
                for n, w in enumerate(("lambda_q1", "lambda_q2", "lambda_k1", "lambda_k2")):
                    sp.dma_start(lam_in[:, n, :], d[w].rearrange("(a n) -> a n", a=1)).then_inc(w_in, 16)
                for n, w in enumerate(("m_gate1", "m_gate2")):
                    sp.dma_start(gates_row[:, n, :], d[w].rearrange("(a n) -> a n", a=1)).then_inc(w_in, 16)
                sp.dma_start(W1[HO:HO + 1, :].rearrange("a (e k h) -> a e k h", e=E, k=2)[:, :, 0, :],
                             d["b1"].rearrange("(a e) h -> a e h", a=1)).then_inc(b1_in, 16)
                sp.wait_ge(zero_ready, 1)
                sp.dma_start(d["xg"].rearrange("(p t) o -> p t o", p=128), strided(zero[:, :], 0, [[0, TILES], [1, O]]))\
                    .then_inc(slots_zero, 16)
                with sp.Fori(0, E) as e:
                    for n in range(2):
                        sp.wait_ge(stage_free, e * 2 + (n + 1))
                        for t, w in enumerate(("w_fast", "w_slow", "h_fast")):
                            src = d[w + "12"[n]].rearrange("e r c -> (e r) c")
                            if n == 0:
                                sp.dma_start(stage[t][0:HO, :].rearrange("c (k h) -> c k h", k=2),
                                             src[bass.ds(e * O, O), :].rearrange("(k c) h -> c k h", k=2))\
                                    .then_inc(stage_in, 16)
                            else:
                                sp.dma_start(stage[t][:, 0:H // 128 * O].rearrange("p (b o) -> p b o", o=O),
                                             src[bass.ds(e * H, H), :].rearrange("(b p) o -> p b o", p=128))\
                                    .then_inc(stage_in, 16)
                sp.wait_ge(b1_in, 16)
                sp.wait_ge(slots_zero, 16)

            @block.gpsimd
            def _(pool):
                pool.memset(head_mask[:, :], 1.0).then_inc(mask_ready, 1)
                pool.wait_ge(mask_ready, 1)
                pool.affine_select(out=head_mask[:, :], in_=head_mask[:, :], compare_op=ALU.is_ge, fill=0.0, base=0,
                                   pattern=[[-HD, 6]], channel_multiplier=1).then_inc(mask_ready, 1)
                pool.wait_ge(mask_ready, 2)
                pool.affine_select(out=head_mask[:, :], in_=head_mask[:, :], compare_op=ALU.is_ge, fill=0.0,
                                   base=HD - 1, pattern=[[HD, 6]], channel_multiplier=-1).then_inc(mask_ready, 1)
                pool.wait_ge(mask_ready, 3)

                def window(m, s):
                    pool.wait_ge(hp_free, m + 1)
                    view = HT[:, :, bass.ds(m * (2 * N), N + 64)]
                    pool.tensor_copy(hp[s][:, :, :].rearrange("c h (i t) -> c h i t", i=2),
                                     bass.AP(tensor=view.tensor, offset=view.offset,
                                             ap=[list(view.ap[0]), [TP, 2], [N, 2], [1, 64]])).then_inc(hp_ready, 1)

                def spread_keys(m, s, first=False):
                    pool.wait_ge(k_ready, m + 1)
                    if not first:
                        pool.wait_ge(scored, m - 1)
                    for h in range(2):
                        last = pool.tensor_tensor(kx[s][:, h, :, :, :],
                                                  strided(kT[s][:, :, :, :], h * 2 * N, [[N, 2], [0, 6], [1, N]]),
                                                  strided(head_mask[:, :], 0, [[0, 2], [1, 6], [0, N]]), ALU.mult)
                    last.then_inc(kx_ready, 1)

                window(0, 0)
                window(1, 1)
                def put_together(e, n, part):
                    rows, width, W = (HO, 2 * H, W1) if n == 0 else (128, H // 128 * O, W2)
                    at, size = part * (width // 2), width // 2
                    fast, slow, h = (t[0:rows, at:at + size] for t in stage)
                    dst = W[0:rows, bass.ds(e * width + at, size)]
                    gate = gates[0:rows, n, bass.ds(e, 1)]
                    steps = e * 12 + (6 * n + 3 * part)
                    pool.wait_ge(stage_in, e * (16 * 6) + 48 * (n + 1))
                    pool.sem_inc(stage_taken, 1)
                    pool.tensor_tensor(slow, slow, bass.AP(tensor=gate.tensor, offset=gate.offset,
                                                           ap=[list(gate.ap[0]), [0, size]]), ALU.mult)\
                        .then_inc(stage_step, 1)
                    pool.wait_ge(stage_step, steps + 1)
                    pool.tensor_tensor(slow, slow, fast, ALU.add).then_inc(stage_step, 1)
                    pool.wait_ge(stage_step, steps + 2)
                    pool.sem_inc(stage_taken, 1)
                    pool.tensor_tensor(dst, slow, h, ALU.add).then_inc(stage_step, 1)
                    if part == 1:
                        pool.wait_ge(stage_step, steps + 3)
                        pool.sem_inc(stage_free, 1)

                pool.wait_ge(setup, 5)
                pool.sem_inc(stage_free, 1)
                spread_keys(0, 0, first=True)
                window(2, 0)
                spread_keys(1, 1, first=True)
                window(3, 1)
                with pool.Fori(0, E - 1) as e:
                    for q in range(4):
                        spread_keys(e * 4 + (q + 2), q % 2)
                        window(e * 4 + (q + 4), q % 2)
                        put_together(e, q // 2, q % 2)
                for m in range(PAIRS - 2, PAIRS):
                    spread_keys(m, m % 2)
                for q in range(4):
                    put_together(E - 1, q // 2, q % 2)

            @block.vector
            def _(dve):
                dve.memset(zero[:, :], 0.0).then_inc(zero_ready, 1)
                for s in range(2):
                    last = dve.memset(pm[s][:, :, :, N:64], 0.0)
                dve.memset(head_sign[:, :, 0], 1.0).then_inc(setup, 1)
                dve.wait_ge(w_in, 16 * 12)
                dve.tensor_scalar(q_bias[:, :], qk_bias[:, 0, :], SCALE, None, ALU.mult).then_inc(setup, 1)
                dve.tensor_tensor(lam_pr[:, :, :], lam_in[:, 0:2, :], lam_in[:, 2:4, :], ALU.mult).then_inc(lam_ready, 1)
                dve.wait_ge(lam_ready, 1)
                dve.tensor_reduce(lam_sum[:, :], lam_pr[:, :, :], AX.X, ALU.add).then_inc(lam_ready, 1)
                dve.wait_ge(lam_expd, 1)
                dve.scalar_tensor_tensor(out=neg_lam[:, :], in0=lam_exp[:, 1:2], scalar=LAMBDA_INIT,
                                         in1=lam_exp[:, 0:1], op0=ALU.subtract, op1=ALU.subtract).then_inc(lam_ready, 1)
                dve.wait_ge(spread, 1)
                dve.tensor_copy(head_sign[:, :, 1], psD[:, 0:6]).then_inc(setup, 1)
                dve.tensor_copy(bv_all[:, :], psX[:, 0:O // 2]).then_inc(setup, 1)
                dve.tensor_copy(gates[:, :, :].rearrange("p a e -> p (a e)"), psD[:, 8:8 + 2 * E]).then_inc(setup, 1)
                dve.wait_ge(setup, 5)

                def values(m, s, first=False):
                    dve.wait_ge(v_done, m + 1)
                    if not first:
                        dve.wait_ge(av_done, m - 1)
                    dve.tensor_tensor(vals[s][:, :, :], psV[:, 0:O].rearrange("p (i v) -> p i v", i=2),
                                      strided(bv_all[:, :], 0, [[0, 2], [1, O // 2]]), ALU.add).then_inc(v_ready, 1)

                def softmax(m, s, first=False):
                    dve.wait_ge(scored, m + 1)
                    dve.tensor_reduce(top[s][:, :], paired(psA), AX.X, ALU.max).then_inc(top_ready, 1)
                    dve.wait_ge(top_ready, m + 1)
                    shape = "p (b h) k -> p b h k"
                    dve.tensor_tensor(ex[s][:, :, :].rearrange(shape, b=2), paired(psA), by_head(top[s]),
                                      ALU.subtract).then_inc(shifted, 1)
                    dve.wait_ge(exped, m + 1)
                    dve.tensor_reduce(den[s][:, :], ex[s][:, :, :], AX.X, ALU.add).then_inc(den_ready, 1)
                    dve.wait_ge(den_ready, m * 2 + 1)
                    dve.reciprocal(den[s][:, :], den[s][:, :]).then_inc(den_ready, 1)
                    dve.wait_ge(den_ready, m * 2 + 2)
                    dve.tensor_tensor(coef[s][:, :], den[s][:, :], head_sign[:, :, :].rearrange("p e m -> p (e m)"),
                                      ALU.mult).then_inc(coef_ready, 1)
                    dve.wait_ge(coef_ready, m + 1)
                    if not first:
                        dve.wait_ge(diffed, m - 1)
                    for b in range(2):
                        last = dve.tensor_tensor(pm[s][:, :, 3 * b:3 * b + 3, 0:N].rearrange("p m e k -> p e m k"),
                                                 ex[s][:, 6 * b:6 * b + 6, :].rearrange("p (e m) k -> p e m k", m=2),
                                                 strided(coef[s][:, :], 6 * b, [[2, 3], [1, 2], [0, N]]), ALU.mult)
                    last.then_inc(pm_ready, 1)

                def outputs(m, s):
                    dve.wait_ge(sq_ready, m + 1)
                    dve.tensor_scalar(OUTS[:, bass.ds(m * O, O)].rearrange("p (f g v) -> p f g v", f=3, g=2), head_order(psX),
                                      1.0, None, ALU.mult).then_inc(out_ready, 1)
                    dve.tensor_reduce(ssq[s][:, :], sq[s][:, :].rearrange("p (e v) -> p e v", e=6), AX.X,
                                      ALU.add).then_inc(ssq_ready, 1)
                    dve.wait_ge(ssq_ready, m + 1)
                    dve.tensor_scalar(SSQ[:, bass.ds(m * 6, 6)], ssq[s][:, :], 1.0, None, ALU.mult)

                values(0, 0, first=True)
                values(1, 1, first=True)
                softmax(0, 0, first=True)
                values(2, 0)
                outputs(0, 0)
                softmax(1, 1, first=True)
                values(3, 1)
                outputs(1, 1)
                with dve.Fori(0, PAIRS // 2 - 2) as t:
                    for e in range(2):
                        m = t * 2 + (e + 2)
                        softmax(m, e)
                        values(m + 2, e)
                        outputs(m, e)
                for m in range(PAIRS - 2, PAIRS):
                    softmax(m, m % 2)
                    outputs(m, m % 2)

            @block.scalar
            def _(act):
                act.wait_ge(lam_ready, 2)
                act.activation(lam_exp[:, :], lam_sum[:, :], ACT.Exp).then_inc(lam_expd, 1)
                act.wait_ge(setup, 5)

                def queries_keys(m, s, first=False):
                    act.wait_ge(qk_done, m + 1)
                    if not first:
                        act.wait_ge(scored, m - 1)
                    for h in range(2):
                        last = act.activation(qT[s][:, h, :], psP[0:HO, h * 128:(h + 1) * 128], ACT.Identity,
                                              bias=q_bias[:, h:h + 1], scale=SCALE)
                    last.then_inc(q_ready, 1)
                    if not first:
                        act.wait_ge(kx_ready, m - 1)
                    for h in range(2):
                        last = act.activation(kT[s][:, h, :, :],
                                              psP[0:HO, 256 + h * 128:384 + h * 128].rearrange("c (i t) -> c i t", i=2)
                                              [:, :, 0:N], ACT.Identity, bias=qk_bias[:, 1, h:h + 1])
                    last.then_inc(k_ready, 1)

                def exps(m, s):
                    act.wait_ge(shifted, m + 1)
                    act.activation(ex[s][:, :, :], ex[s][:, :, :], ACT.Exp).then_inc(exped, 1)

                def differences(m, s, first=False):
                    act.wait_ge(diffed, m + 1)
                    if not first:
                        act.wait_ge(av_done, m - 1)
                    act.activation(dT[s][:, :, :].rearrange("p f q -> p (f q)"), psD[:, 0:3 * 128],
                                   ACT.Copy).then_inc(dT_ready, 1)

                def squares(m, s, first=False):
                    act.wait_ge(av_done, m + 1)
                    if not first:
                        act.wait_ge(ssq_ready, m - 1)
                    act.activation(sq[s][:, :].rearrange("p (f g v) -> p f g v", f=3, g=2), head_order(psX), ACT.Square).then_inc(sq_ready, 1)

                def steps(m, s, first=False, last=False):
                    exps(m, s)
                    differences(m, s, first)
                    if not last:
                        queries_keys(m + 2, s)
                    squares(m, s, first)

                queries_keys(0, 0, first=True)
                queries_keys(1, 1, first=True)
                steps(0, 0, first=True)
                steps(1, 1, first=True)
                with act.Fori(0, PAIRS // 2 - 2) as t:
                    for e in range(2):
                        steps(t * 2 + (e + 2), e)
                for m in range(PAIRS - 2, PAIRS):
                    steps(m, m % 2, last=True)

            @block.tensor
            def _(pe):
                pe.sem_inc(hp_free, 2)
                pe.wait_ge(lam_ready, 3)
                pe.matmul(psD[:, 0:6], ones[0:1, 0:128], neg_lam[:, 0:1].to_broadcast([1, 6]), start=True, stop=True)
                pe.matmul(psD[:, 8:8 + 2 * E], ones[0:1, 0:128], gates_row[:, :, :].rearrange("p a e -> p (a e)"),
                          start=True, stop=True)
                bv_view = bv_row[:, :].rearrange("p (f g v) -> p g f v", g=2, v=2 * HD)
                for g in range(2):
                    last = pe.matmul(psX[64 * g:64 * g + 64, 0:O // 2], ones[0:1, 0:64], bv_view[:, g, :, :],
                                     start=True, stop=True)
                last.then_inc(spread, 1)
                pe.wait_ge(setup, 5)

                def project(m, s, first=False):
                    pe.wait_ge(hp_ready, m + 1)
                    if not first:
                        pe.wait_ge(k_ready, m)
                    for n in range(2):
                        for h in range(2):
                            at = n * 256 + h * 128
                            for k in range(2):
                                last = pe.matmul(psP[0:HO, at:at + 128], wqkv[:, n, k, h * HO:(h + 1) * HO],
                                                 hp[s][:, k, :], start=(k == 0), stop=(k == 1))
                    last.then_inc(qk_done, 1)
                    if not first:
                        pe.wait_ge(v_ready, m)
                    for i in range(2):
                        for g in range(2):
                            for k in range(2):
                                rhs = wqkv[:, 2, k, :].rearrange("c (f g v) -> c g f v", g=2, v=2 * HD)[:, g, :, :]
                                last = pe.matmul(psV[64 * g:64 * g + 64, i * HO:(i + 1) * HO],
                                                 hp[s][:, k, 64 * i:64 * i + 64], rhs, start=(k == 0), stop=(k == 1))
                    last.then_inc(v_done, 1)
                    pe.wait_ge(v_done, m + 1)
                    pe.sem_inc(hp_free, 1)

                def scores(m, s, first=False):
                    pe.wait_ge(q_ready, m + 1)
                    pe.wait_ge(kx_ready, m + 1)
                    if not first:
                        pe.wait_ge(shifted, m)
                    for i in range(2):
                        for h in range(2):
                            last = pe.matmul(psA[64 * i:64 * i + 64, h * 512:h * 512 + 6 * N],
                                             qT[s][:, h, 64 * i:64 * i + 64],
                                             kx[s][:, h, i, :, :].rearrange("c h k -> c (h k)"),
                                             start=True, stop=True)
                    last.then_inc(scored, 1)

                def turn_maps(m, s, first=False):
                    pe.wait_ge(pm_ready, m + 1)
                    if not first:
                        pe.wait_ge(dT_ready, m)
                    for f in range(3):
                        for n in range(2):
                            last = pe.matmul(psD[:, f * 128:(f + 1) * 128],
                                             pm[s][:, n, 2 * f:2 * f + 2, :].rearrange("p e k -> p (e k)"),
                                             ident[:, :], is_transpose=True, start=(n == 0), stop=(n == 1))
                    last.then_inc(diffed, 1)

                def weigh_values(m, s, first=False):
                    pe.wait_ge(dT_ready, m + 1)
                    pe.wait_ge(v_ready, m + 1)
                    if not first:
                        pe.wait_ge(out_ready, m)
                        pe.wait_ge(sq_ready, m)
                    pe.sem_inc(weighing, 1)
                    for i in range(2):
                        for f in range(3):
                            for g in range(2):
                                last = pe.matmul(psX[64 * i:64 * i + 64, g * 512 + f * 2 * HD:g * 512 + (f + 1) * 2 * HD],
                                                 dT[s][64 * g:64 * g + N, f, 64 * i:64 * i + 64],
                                                 vals[s][64 * g:64 * g + N, i, f * 2 * HD:(f + 1) * 2 * HD],
                                                 start=True, stop=True)
                    last.then_inc(av_done, 1)

                project(0, 0, first=True)
                scores(0, 0, first=True)
                project(1, 1)
                turn_maps(0, 0, first=True)
                scores(1, 1)
                project(2, 0)
                weigh_values(0, 0, first=True)
                with pe.Fori(0, PAIRS // 2 - 2) as t:
                    for e in range(2):
                        m, s = t * 2 + (e + 1), (e + 1) % 2
                        turn_maps(m, s)
                        scores(m + 1, 1 - s)
                        project(m + 2, s)
                        weigh_values(m, s)
                for m in range(PAIRS - 3, PAIRS):
                    turn_maps(m, m % 2)
                    if m + 1 < PAIRS:
                        scores(m + 1, (m + 1) % 2)
                    if m + 2 < PAIRS:
                        project(m + 2, m % 2)
                    weigh_values(m, m % 2)


def mix(nc, d, HT, H2, SSQ, RL, ident, ones):
    with ExitStack() as ctx:
        def sb(name, shape, dt=F32):
            return ctx.enter_context(nc.sbuf_tensor(name, shape, dt))

        def sem(name):
            return ctx.enter_context(nc.semaphore(name))

        def ps(name, banks):
            return ctx.enter_context(nc.psum_tensor(name, [128, banks * 512], F32))

        wo = sb("wo", [HO, 2, O])
        nw = sb("nw", [HO, 1])
        bo_row = sb("bo_row", [1, O])
        eps = sb("eps", [128, 1])
        hw = [sb(f"hw{s}", [HO, 2, 128]) for s in range(2)]
        on = [sb(f"on{s}", [128, O]) for s in range(2)]
        oT = [sb(f"oT{s}", [HO, 2, 128]) for s in range(2)]
        hn = [sb(f"hn{s}", [128, O]) for s in range(2)]
        hnT = [sb(f"hnT{s}", [HO, 2, 128]) for s in range(2)]
        rms = sb("rms", [128, PAIRS * 6])
        st = sb("ln_st", [128, PAIRS, 6])
        mv = sb("ln_mv", [128, PAIRS, 2])
        dev = sb("ln_dev", [128, PAIRS])
        rstd = sb("ln_rstd", [128, PAIRS])
        rw = sb("rw", [E, O])
        pw = sb("pw", [DR, O])
        emb = sb("emb", [E, DR])
        emb2 = sb("emb2", [E, DR])
        embn = sb("embn", [E, DR])
        embT = sb("embT", [DR, E])
        gain = sb("gain", [E, 4])
        align = sb("align", [E, O])
        RW = sb("RW", [HO, 2, RC])
        bias8 = sb("bias8", [1, 3, E])
        rl_row = sb("rl_row", [1, RC])

        psO = ps("m_psO", 1)
        psM = ps("m_psM", 1)
        psR = ps("m_psR", 1)
        psH = ps("m_psH", 1)

        w_in = sem("m_w_in")
        eps_ready = sem("eps_ready")
        step = sem("m_step")
        rooted = sem("m_rooted")
        turned = sem("m_turned")
        wo_ready = sem("wo_ready")
        hw_ready = sem("hw_ready")
        on_ready = sem("on_ready")
        o_turned = sem("o_turned")
        oT_ready = sem("oT_ready")
        mixed = sem("mixed")
        x_ready = sem("x_ready")
        stat = sem("m_stat")
        hn_ready = sem("hn_ready")
        hn_turned = sem("hn_turned")
        hnT_ready = sem("hnT_ready")
        routed = sem("routed")
        rl_ready = sem("rl_ready")

        mv_flat = mv[:, :, :].rearrange("p m a -> p (m a)")

        with nc.Block() as block:
            @block.sync
            def _(sp):
                sp.dma_start(wo[:, :, :], d["Wo"].rearrange("(k c) o -> c k o", k=2)).then_inc(w_in, 16)
                for n in range(3):
                    sp.dma_start(nw[32 * n:32 * n + 32, :], d["norm_weight"].rearrange("(n a) -> n a", a=1)).then_inc(w_in, 16)
                sp.dma_start(bo_row[:, :], d["bo"].rearrange("(a n) -> a n", a=1)).then_inc(w_in, 16)
                sp.dma_start(rw[:, :], d["router_w"]).then_inc(w_in, 16)
                sp.dma_start(pw[:, :], d["probe_w"]).then_inc(w_in, 16)
                sp.dma_start(emb[:, :], d["router_emb"]).then_inc(w_in, 16)
                sp.dma_start(bias8[:, 0, :], d["energy"].rearrange("(a n) -> a n", a=1)).then_inc(w_in, 16)
                sp.dma_start(bias8[:, 1, :], d["fatigue"].rearrange("(a n) -> a n", a=1)).then_inc(w_in, 16)

            @block.gpsimd
            def _(pool):
                def window(m, s, first=False):
                    if not first:
                        pool.wait_ge(mixed, m - 1)
                    view = HT[:, :, bass.ds(m * (2 * N), N + 64)]
                    pool.tensor_copy(hw[s][:, :, :].rearrange("c h (i t) -> c h i t", i=2),
                                     bass.AP(tensor=view.tensor, offset=view.offset,
                                             ap=[list(view.ap[0]), [TP, 2], [N, 2], [1, 64]])).then_inc(hw_ready, 1)

                window(0, 0, first=True)
                window(1, 1, first=True)
                with pool.Fori(0, PAIRS // 2 - 1) as t:
                    for e in range(2):
                        window(t * 2 + (e + 2), e)

            @block.vector
            def _(dve):
                dve.memset(eps[:, :], EPS).then_inc(eps_ready, 1)
                dve.memset(rl_row[:, :], 0.0).then_inc(step, 1)
                dve.wait_ge(w_in, 16 * 10)
                dve.tensor_tensor(emb2[:, :], emb[:, :], emb[:, :], ALU.mult).then_inc(step, 1)
                dve.wait_ge(step, 2)
                dve.tensor_reduce(gain[:, 0:1], emb2[:, :], AX.X, ALU.add).then_inc(step, 1)
                dve.tensor_scalar(wo[:, :, :], wo[:, :, :], nw[:, 0:1], 1.0 - LAMBDA_INIT, ALU.mult,
                                  ALU.mult).then_inc(wo_ready, 1)
                dve.tensor_scalar(bias8[:, 2, :], bias8[:, 1, :], 0.1, None, ALU.mult).then_inc(step, 1)
                dve.wait_ge(step, 4)
                dve.scalar_tensor_tensor(out=rl_row[:, 0:E], in0=bias8[:, 0, :], scalar=0.1, in1=bias8[:, 2, :],
                                         op0=ALU.mult, op1=ALU.subtract).then_inc(step, 1)
                dve.wait_ge(rooted, 2)
                dve.tensor_scalar(gain[:, 2:3], gain[:, 1:2], 1e-12, None, ALU.max).then_inc(step, 1)
                dve.wait_ge(step, 6)
                dve.reciprocal(gain[:, 2:3], gain[:, 2:3]).then_inc(step, 1)
                dve.tensor_scalar(gain[:, 3:4], gain[:, 1:2], 0.02 / O, 0.02 / O, ALU.mult, ALU.add).then_inc(step, 1)
                dve.wait_ge(step, 8)
                dve.tensor_scalar(embn[:, :], emb[:, :], gain[:, 2:3], None, ALU.mult).then_inc(step, 1)
                dve.tensor_scalar(rw[:, :], rw[:, :], gain[:, 3:4], None, ALU.add).then_inc(step, 1)
                dve.wait_ge(turned, 1)
                dve.tensor_copy(embT[:, :], psR[0:DR, 0:E]).then_inc(step, 1)
                dve.wait_ge(turned, 2)
                dve.tensor_copy(align[:, :], psH[0:E, 0:O]).then_inc(step, 1)
                dve.wait_ge(turned, 3)
                dve.tensor_copy(RW[:, :, :].rearrange("c k n -> c (k n)"), psR[0:HO, 0:2 * RC]).then_inc(step, 1)
                dve.reciprocal(rms[:, :], rms[:, :]).then_inc(step, 1)
                dve.wait_ge(step, 14)

                def normed(m, s, first=False):
                    if not first:
                        dve.wait_ge(o_turned, m - 1)
                    factor = rms[:, bass.ds(m * 6, 6)]
                    dve.tensor_tensor(on[s][:, :].rearrange("p (e v) -> p e v", e=6),
                                      H2[:, bass.ds(m * O, O)].rearrange("p (e v) -> p e v", e=6),
                                      bass.AP(tensor=factor.tensor, offset=factor.offset,
                                              ap=[list(factor.ap[0]), [1, 6], [0, 2 * HD]]), ALU.mult)\
                        .then_inc(on_ready, 1)

                def keep(m, s):
                    dve.wait_ge(mixed, m + 1)
                    dve.tensor_scalar(H2[:, bass.ds(m * O, O)], psM[:, 0:O], 1.0, None, ALU.mult).then_inc(x_ready, 1)

                normed(0, 0, first=True)
                normed(1, 1, first=True)
                keep(0, 0)
                with dve.Fori(0, PAIRS // 2 - 1) as t:
                    for e in range(2):
                        normed(t * 2 + (e + 2), e)
                        keep(t * 2 + (e + 1), 1 - e)
                keep(PAIRS - 1, 1)

                dve.wait_ge(x_ready, PAIRS)
                for m in range(PAIRS):
                    last = dve.bn_stats(st[:, m, :], H2[:, m * O:(m + 1) * O])
                last.then_inc(stat, 1)
                dve.wait_ge(stat, 1)
                for m in range(PAIRS):
                    last = dve.bn_aggr(mv[:, m, :], st[:, m, :])
                last.then_inc(stat, 1)
                dve.wait_ge(rooted, 3)
                dve.reciprocal(rstd[:, :], dev[:, :]).then_inc(stat, 1)
                dve.wait_ge(stat, 3)

                def layer_norm(m, s, first=False):
                    if not first:
                        dve.wait_ge(hn_turned, m - 1)
                    dve.tensor_scalar(hn[s][:, :], H2[:, bass.ds(m * O, O)], mv_flat[:, bass.ds(m * 2, 1)],
                                      rstd[:, bass.ds(m, 1)], ALU.subtract, ALU.mult).then_inc(hn_ready, 1)
                    dve.wait_ge(hn_ready, m + 1)
                    dve.tensor_scalar(H2[:, bass.ds(m * O, O)], hn[s][:, :], 1.0, None, ALU.mult)

                def keep_router(m, s):
                    dve.wait_ge(routed, m + 1)
                    dve.tensor_scalar(RL[:, bass.ds(m * RC, RC)], psR[:, 0:RC], 1.0, None, ALU.mult).then_inc(rl_ready, 1)

                layer_norm(0, 0, first=True)
                layer_norm(1, 1, first=True)
                keep_router(0, 0)
                with dve.Fori(0, PAIRS // 2 - 1) as t:
                    for e in range(2):
                        layer_norm(t * 2 + (e + 2), e)
                        keep_router(t * 2 + (e + 1), 1 - e)
                keep_router(PAIRS - 1, 1)

            @block.scalar
            def _(act):
                act.wait_ge(eps_ready, 1)
                act.activation(rms[:, :], SSQ[:, :], ACT.Sqrt, bias=eps[:, 0:1], scale=1.0 / (2 * HD)).then_inc(rooted, 1)
                act.wait_ge(step, 3)
                act.activation(gain[:, 1:2], gain[:, 0:1], ACT.Sqrt).then_inc(rooted, 1)

                def copy_oT(m, s, first=False):
                    act.wait_ge(o_turned, m + 1)
                    if not first:
                        act.wait_ge(mixed, m - 1)
                    act.activation(oT[s][:, :, :].rearrange("c k t -> c (k t)"), psO[0:HO, 0:256],
                                   ACT.Copy).then_inc(oT_ready, 1)

                copy_oT(0, 0, first=True)
                copy_oT(1, 1, first=True)
                with act.Fori(0, PAIRS // 2 - 1) as t:
                    for e in range(2):
                        copy_oT(t * 2 + (e + 2), e)
                act.wait_ge(stat, 2)
                act.activation(dev[:, :], mv[:, :, 1], ACT.Sqrt, bias=eps[:, 0:1]).then_inc(rooted, 1)

                def copy_hnT(m, s, first=False):
                    act.wait_ge(hn_turned, m + 1)
                    if not first:
                        act.wait_ge(routed, m - 1)
                    act.activation(hnT[s][:, :, :].rearrange("c k t -> c (k t)"), psO[0:HO, 0:256],
                                   ACT.Copy).then_inc(hnT_ready, 1)

                copy_hnT(0, 0, first=True)
                copy_hnT(1, 1, first=True)
                with act.Fori(0, PAIRS // 2 - 1) as t:
                    for e in range(2):
                        copy_hnT(t * 2 + (e + 2), e)

            @block.tensor
            def _(pe):
                pe.wait_ge(step, 10)
                pe.transpose(psR[0:DR, 0:E], embn[:, :], ident[0:E, 0:E]).then_inc(turned, 1)
                pe.wait_ge(step, 11)
                pe.matmul(psH[0:E, 0:O], embT[:, :], pw[:, :], start=True, stop=True).then_inc(turned, 1)
                pe.wait_ge(step, 12)
                for k in range(2):
                    for at, rows, w in ((0, E, rw), (E, E, align), (2 * E, DR, pw)):
                        last = pe.transpose(psR[0:HO, k * RC + at:k * RC + at + rows], w[:, k * HO:(k + 1) * HO],
                                            ident[0:rows, 0:rows])
                last.then_inc(turned, 1)
                pe.wait_ge(wo_ready, 1)

                def turn(src, s, ready, done, copied, m, first=False):
                    pe.wait_ge(ready, m + 1)
                    if not first:
                        pe.wait_ge(copied, m)
                    for k in range(2):
                        last = pe.transpose(psO[0:HO, k * 128:(k + 1) * 128], src[s][:, k * HO:(k + 1) * HO], ident[:, :])
                    last.then_inc(done, 1)

                def project(m, s, first=False):
                    pe.wait_ge(oT_ready, m + 1)
                    pe.wait_ge(hw_ready, m + 1)
                    if not first:
                        pe.wait_ge(x_ready, m)
                    for h in range(2):
                        half = slice(h * HO, (h + 1) * HO)
                        pe.matmul(psM[:, half], ones[0:1, 0:128], bo_row[:, half], start=True, stop=False)
                        for k in range(2):
                            pe.matmul(psM[:, half], oT[s][:, k, :], wo[:, k, half], start=False, stop=False)
                        last = pe.matmul(psM[:, half], hw[s][:, h, :], ident[0:HO, 0:HO], start=False, stop=True)
                    last.then_inc(mixed, 1)

                turn(on, 0, on_ready, o_turned, oT_ready, 0, first=True)
                turn(on, 1, on_ready, o_turned, oT_ready, 1)
                project(0, 0, first=True)
                with pe.Fori(0, PAIRS // 2 - 1) as t:
                    for e in range(2):
                        turn(on, e, on_ready, o_turned, oT_ready, t * 2 + (e + 2))
                        project(t * 2 + (e + 1), 1 - e)
                project(PAIRS - 1, 1)

                def route(m, s, first=False):
                    pe.wait_ge(hnT_ready, m + 1)
                    if first:
                        pe.wait_ge(step, 13)
                    else:
                        pe.wait_ge(rl_ready, m)
                    pe.matmul(psR[:, 0:RC], ones[0:1, 0:128], rl_row[:, :], start=True, stop=False)
                    for k in range(2):
                        last = pe.matmul(psR[:, 0:RC], hnT[s][:, k, :], RW[:, k, :], start=False, stop=(k == 1))
                    last.then_inc(routed, 1)

                turn(hn, 0, hn_ready, hn_turned, hnT_ready, 0, first=True)
                turn(hn, 1, hn_ready, hn_turned, hnT_ready, 1)
                route(0, 0, first=True)
                with pe.Fori(0, PAIRS // 2 - 1) as t:
                    for e in range(2):
                        turn(hn, e, hn_ready, hn_turned, hnT_ready, t * 2 + (e + 2))
                        route(t * 2 + (e + 1), 1 - e)
                route(PAIRS - 1, 1)


def experts(nc, d, out, H2, W1, W2, RL, ident, ones):
    with ExitStack() as ctx:
        def sb(name, shape, dt=F32):
            return ctx.enter_context(nc.sbuf_tensor(name, shape, dt))

        def sem(name):
            return ctx.enter_context(nc.semaphore(name))

        def ps(name, banks):
            return ctx.enter_context(nc.psum_tensor(name, [128, banks * 512], F32))

        rl = RL[:, :].rearrange("p (m r) -> p m r", r=RC)
        valid = sb("valid", [128, 1])
        nowhere = sb("nowhere", [128, 1])
        below = sb("below", [128, 128])
        rank_i = sb("rank_i", [128, E], I32)
        rank_e = sb("rank_e", [128, E])
        tile_i = sb("tile_i", [1, TILES], I32)
        tile_f = sb("tile_f", [1, TILES])
        probe2 = sb("probe2", [128, PAIRS, DR])
        norm = sb("norm", [128, 2, PAIRS])
        logit = sb("logit", [128, PAIRS, E])
        cand = sb("cand", [128, PAIRS, E])
        best = sb("best", [128, 4, PAIRS])
        one_hot = [sb(f"one_hot{n}", [128, PAIRS, E]) for n in range(2)]
        gate = sb("gate", [128, 3, PAIRS])
        picked = sb("picked", [128, PAIRS, E])
        total = sb("total", [128, PAIRS, E])
        run = [sb(f"run{n}", [128, PAIRS, E]) for n in range(2)]
        count_i = sb("count_i", [128, E], I32)
        ends = [sb(f"ends{n}", [128, E]) for n in range(3)]
        slot = sb("slot", [128, 2, PAIRS])
        scat = sb("scat", [128, 2, PAIRS], U32)
        gath = sb("gath", [128, 2, PAIRS], U32)
        past = sb("past", [1, TILES, E])
        owner_f = sb("owner_f", [1, TILES])
        owner = sb("owner", [1, TILES], I32)
        b2_row = sb("b2_row", [1, E * O])
        xg = [sb(f"xg{s}", [RT, O]) for s in range(2)]
        xgT = [sb(f"xgT{s}", [HO + 1, 2, RT]) for s in range(2)]
        hid = [sb(f"hid{s}", [RT, H]) for s in range(2)]
        hidT = [sb(f"hidT{s}", [128, H // 128, RT]) for s in range(2)]
        yg = [sb(f"yg{s}", [RT, O]) for s in range(2)]
        back = [sb(f"back{s}", [128, O]) for s in range(YRING)]
        eps = sb("f_eps", [128, 1])
        st = sb("f_st", [128, PAIRS, 6])
        mv = sb("f_mv", [128, PAIRS, 2])
        dev = sb("f_dev", [128, PAIRS])
        rstd = sb("f_rstd", [128, PAIRS])

        psT = ps("f_psT", 1)
        psH = ps("f_psH", 2)
        psHT = ps("f_psHT", 2)
        psY = ps("f_psY", 1)
        psC = ps("f_psC", 2)

        const = sem("f_const")
        below_ready = sem("below_ready")
        b2_in = sem("b2_in")
        step = sem("f_step")
        rooted = sem("f_rooted")
        counted = sem("counted")
        slots_ready = sem("slots_ready")
        owner_ready = sem("owner_ready")
        scattered = sem("scattered")
        xg_in = [sem(f"xg_in{s}") for s in range(2)]
        xg_turned = sem("xg_turned")
        xgT_ready = sem("xgT_ready")
        hidden = sem("hidden")
        hid_ready = sem("hid_ready")
        hid_turned = sem("hid_turned")
        hidT_ready = sem("hidT_ready")
        y_done = sem("f_y_done")
        yg_ready = sem("yg_ready")
        y_stored = [sem(f"y_stored{s}") for s in range(2)]
        all_stored = sem("all_stored")
        back_in = [sem(f"back_in{s}") for s in range(YRING)]
        added = sem("added")
        final = sem("final")
        stored = sem("f_stored")

        with nc.Block() as block:
            @block.gpsimd
            def _(pool):
                pool.memset(below[:, :], 1.0).then_inc(below_ready, 1)
                pool.wait_ge(below_ready, 1)
                pool.affine_select(out=below[:, :], in_=below[:, :], compare_op=ALU.is_ge, fill=0.0, base=-1,
                                   pattern=[[1, 128]], channel_multiplier=-1).then_inc(below_ready, 1)
                pool.iota(rank_i[:, :], pattern=[[-1, E]], base=E, channel_multiplier=0).then_inc(const, 1)
                pool.iota(tile_i[:, :], pattern=[[1, TILES]], base=0, channel_multiplier=0).then_inc(const, 1)
                pool.wait_ge(slots_ready, 1)
                for m in range(PAIRS):
                    for n in range(2):
                        pool.indirect_dma_start(out=d["xg"], out_offset=bass.IndirectOffsetOnAxis(
                            ap=scat[:, n, m:m + 1], axis=0), in_=H2[:, m * O:(m + 1) * O], in_offset=None,
                            bounds_check=SLOTS - 1, oob_is_err=False).then_inc(scattered, 16)
                pool.wait_ge(all_stored, 1)
                for m in range(PAIRS):
                    for n in range(2):
                        q = 2 * m + n
                        if q >= YRING:
                            pool.wait_ge(added, q - YRING + 1)
                        pool.indirect_dma_start(out=back[q % YRING][:, :], out_offset=None, in_=d["yg"],
                                                in_offset=bass.IndirectOffsetOnAxis(ap=gath[:, n, m:m + 1], axis=0),
                                                bounds_check=SLOTS - 1, oob_is_err=False).then_inc(back_in[q % YRING], 16)

            @block.vector
            def _(dve):
                links = [0]

                def link(ins):
                    links[0] += 1
                    ins.then_inc(step, 1)
                    dve.wait_ge(step, links[0])

                def over_experts(view):
                    return strided(view, 0, [[1, PAIRS], [0, E]])

                def over_pairs(view):
                    return strided(view, 0, [[0, PAIRS], [1, E]])

                dve.memset(valid[:, :], 0.0)
                dve.memset(eps[:, :], EPS)
                for s in range(2):
                    dve.memset(xgT[s][HO:HO + 1, 0, :], 1.0)
                link(dve.memset(nowhere[:, :], float(4 * SLOTS)))
                for i in range(2):
                    dve.memset(valid[64 * i:64 * i + N, :], 1.0)
                    last = dve.memset(nowhere[64 * i:64 * i + N, :], 0.0)
                link(last)
                dve.wait_ge(const, 2)
                dve.tensor_copy(rank_e[:, :], rank_i[:, :])
                dve.tensor_copy(tile_f[:, :], tile_i[:, :])
                link(dve.tensor_tensor(probe2[:, :, :], rl[:, :, 2 * E:RC], rl[:, :, 2 * E:RC], ALU.mult))
                link(dve.tensor_reduce(norm[:, 0, :], probe2[:, :, :], AX.X, ALU.add))
                dve.wait_ge(rooted, 1)
                link(dve.tensor_scalar(norm[:, 1, :], norm[:, 1, :], 1e-12, None, ALU.max))
                link(dve.reciprocal(norm[:, 1, :], norm[:, 1, :]))
                link(dve.tensor_tensor(cand[:, :, :], rl[:, :, E:2 * E], over_experts(norm[:, 1, :]), ALU.mult))
                link(dve.scalar_tensor_tensor(out=logit[:, :, :], in0=cand[:, :, :], scalar=0.02, in1=rl[:, :, 0:E],
                                              op0=ALU.mult, op1=ALU.add))
                for n in range(2):
                    link(dve.tensor_reduce(best[:, n, :], logit[:, :, :], AX.X, ALU.max))
                    link(dve.tensor_tensor(cand[:, :, :], logit[:, :, :], over_experts(best[:, n, :]), ALU.is_equal))
                    link(dve.tensor_tensor(cand[:, :, :], cand[:, :, :], over_pairs(rank_e[:, :]), ALU.mult))
                    link(dve.tensor_reduce(best[:, 2 + n, :], cand[:, :, :], AX.X, ALU.max))
                    link(dve.tensor_tensor(one_hot[n][:, :, :], over_pairs(rank_e[:, :]), over_experts(best[:, 2 + n, :]),
                                           ALU.is_equal))
                    if n == 0:
                        link(dve.scalar_tensor_tensor(out=logit[:, :, :], in0=one_hot[0][:, :, :], scalar=-3e38,
                                                      in1=logit[:, :, :], op0=ALU.mult, op1=ALU.add))
                link(dve.tensor_tensor(picked[:, :, :], one_hot[0][:, :, :], one_hot[1][:, :, :], ALU.add))
                link(dve.tensor_scalar(picked[:, :, :], picked[:, :, :], valid[:, 0:1], None, ALU.mult))
                assert links[0] == PICKED
                link(dve.tensor_tensor(gate[:, 2, :], best[:, 1, :], best[:, 0, :], ALU.subtract))
                dve.wait_ge(counted, 1)
                link(dve.tensor_copy(total[:, :, :], psC[:, 512:512 + PAIRS * E].rearrange("p (m e) -> p m e", e=E)))
                src = total
                for n in range(5):
                    dst, reach = run[n % 2], 1 << n
                    dve.tensor_copy(dst[:, 0:reach, :], src[:, 0:reach, :])
                    link(dve.tensor_tensor(dst[:, reach:PAIRS, :], src[:, reach:PAIRS, :], src[:, 0:PAIRS - reach, :],
                                           ALU.add))
                    src = dst
                link(dve.tensor_scalar(count_i[:, :], src[:, PAIRS - 1, :], float(RT - 1), None, ALU.add))
                link(dve.tensor_scalar(count_i[:, :], count_i[:, :], RT.bit_length() - 1, None, ALU.arith_shift_right))
                link(dve.tensor_copy(ends[0][:, :], count_i[:, :]))
                link(dve.tensor_tensor(run[1 - 0][:, :, :], src[:, :, :], total[:, :, :], ALU.subtract))
                eat = ends[0]
                for n in range(3):
                    dst, reach = ends[1 + n % 2], 1 << n
                    dve.tensor_copy(dst[:, 0:reach], eat[:, 0:reach])
                    link(dve.tensor_tensor(dst[:, reach:E], eat[:, reach:E], eat[:, 0:E - reach], ALU.add))
                    eat = dst
                link(dve.tensor_tensor(ends[0][:, :], eat[:, :], ends[0][:, :], ALU.subtract))
                link(dve.tensor_scalar(ends[0][:, :], ends[0][:, :], float(RT), None, ALU.mult))
                link(dve.tensor_tensor(run[1][:, :, :], run[1][:, :, :], over_pairs(ends[0][:, :]), ALU.add))
                link(dve.tensor_tensor(run[1][:, :, :], run[1][:, :, :],
                                       psC[:, 0:PAIRS * E].rearrange("p (m e) -> p m e", e=E), ALU.add))
                for n in range(2):
                    link(dve.tensor_tensor(cand[:, :, :], run[1][:, :, :], one_hot[n][:, :, :], ALU.mult))
                    link(dve.tensor_reduce(slot[:, n, :], cand[:, :, :], AX.X, ALU.add))
                for n in range(2):
                    dve.tensor_scalar(scat[:, n, :], slot[:, n, :], valid[:, 0:1], nowhere[:, 0:1], ALU.mult, ALU.add)
                    last = dve.tensor_scalar(gath[:, n, :], slot[:, n, :], valid[:, 0:1], None, ALU.mult)
                last.then_inc(slots_ready, 1)
                link(dve.tensor_tensor(past[:, :, :], strided(tile_f[:, :], 0, [[1, TILES], [0, E]]),
                                       strided(eat[0:1, :], 0, [[0, TILES], [1, E]]), ALU.is_ge))
                link(dve.tensor_reduce(owner_f[:, :], past[:, :, :], AX.X, ALU.add))
                dve.tensor_scalar(owner[:, :], owner_f[:, :], float(E - 1), None, ALU.min).then_inc(owner_ready, 1)
                dve.wait_ge(rooted, 2)
                link(dve.tensor_scalar(gate[:, 0, :], gate[:, 2, :], 1.0, None, ALU.add))
                link(dve.reciprocal(gate[:, 0, :], gate[:, 0, :]))
                link(dve.tensor_tensor(gate[:, 1, :], gate[:, 2, :], gate[:, 0, :], ALU.mult))

                def rectify(j, s, first=False):
                    dve.wait_ge(hidden, j + 1)
                    if not first:
                        dve.wait_ge(hid_turned, j - 1)
                    dve.tensor_scalar(hid[s][:, :], psH[:, 0:H], 0.0, None, ALU.max).then_inc(hid_ready, 1)

                def keep(j, s, first=False):
                    dve.wait_ge(y_done, j + 1)
                    if not first:
                        dve.wait_ge(y_stored[s], stored_so_far(j, s))
                    dve.tensor_scalar(yg[s][:, :], psY[:, 0:O], 1.0, None, ALU.mult).then_inc(yg_ready, 1)

                def stored_so_far(j, s):
                    return j * 8 - 8 * s

                rectify(0, 0, first=True)
                rectify(1, 1, first=True)
                keep(0, 0, first=True)
                rectify(2, 0)
                keep(1, 1, first=True)
                with dve.Fori(0, (TILES - 4) // 2) as t:
                    for e in range(2):
                        rectify(t * 2 + (e + 3), 1 - e)
                        keep(t * 2 + (e + 2), e)
                for j in range(TILES - 2, TILES):
                    if j + 1 < TILES:
                        rectify(j + 1, (j + 1) % 2)
                    keep(j, j % 2)

                for m in range(PAIRS):
                    row = H2[:, m * O:(m + 1) * O]
                    for n in range(2):
                        q = 2 * m + n
                        dve.wait_ge(back_in[q % YRING], 16 * (q // YRING + 1))
                        if n == 1:
                            dve.wait_ge(added, q)
                        dve.scalar_tensor_tensor(out=row, in0=back[q % YRING][:, :], scalar=gate[:, n, m:m + 1],
                                                 in1=row, op0=ALU.mult, op1=ALU.add).then_inc(added, 1)
                    dve.wait_ge(added, 2 * m + 2)
                    last = dve.bn_stats(st[:, m, :], row)
                link(last)
                for m in range(PAIRS):
                    last = dve.bn_aggr(mv[:, m, :], st[:, m, :])
                link(last)
                assert links[0] == AGGREGATED
                dve.wait_ge(rooted, 3)
                link(dve.reciprocal(rstd[:, :], dev[:, :]))
                for m in range(PAIRS):
                    row = H2[:, m * O:(m + 1) * O]
                    dve.tensor_scalar(row, row, mv[:, m, 0:1], rstd[:, m:m + 1], ALU.subtract, ALU.mult).then_inc(final, 1)

            @block.scalar
            def _(act):
                act.wait_ge(step, 4)
                act.activation(norm[:, 1, :], norm[:, 0, :], ACT.Sqrt).then_inc(rooted, 1)
                act.wait_ge(step, PICKED + 1)
                act.activation(gate[:, 2, :], gate[:, 2, :], ACT.Exp).then_inc(rooted, 1)

                def copy_xgT(j, s, first=False):
                    act.wait_ge(xg_turned, j + 1)
                    if not first:
                        act.wait_ge(hidden, j - 1)
                    act.activation(xgT[s][0:HO, :, :].rearrange("c k t -> c (k t)"), psT[0:HO, 0:2 * RT],
                                   ACT.Copy).then_inc(xgT_ready, 1)

                def square(j, s, first=False):
                    act.wait_ge(hid_turned, j + 1)
                    if not first:
                        act.wait_ge(y_done, j - 1)
                    act.activation(hidT[s][:, :, :].rearrange("c b t -> c (b t)"), psHT[:, 0:H],
                                   ACT.Square).then_inc(hidT_ready, 1)

                copy_xgT(0, 0, first=True)
                copy_xgT(1, 1, first=True)
                square(0, 0, first=True)
                copy_xgT(2, 0)
                square(1, 1, first=True)
                with act.Fori(0, (TILES - 4) // 2) as t:
                    for e in range(2):
                        copy_xgT(t * 2 + (e + 3), 1 - e)
                        square(t * 2 + (e + 2), e)
                for j in range(TILES - 2, TILES):
                    if j + 1 < TILES:
                        copy_xgT(j + 1, (j + 1) % 2)
                    square(j, j % 2)
                act.wait_ge(step, AGGREGATED)
                act.activation(dev[:, :], mv[:, :, 1], ACT.Sqrt, bias=eps[:, 0:1]).then_inc(rooted, 1)

            @block.tensor
            def _(pe):
                flat = picked[:, :, :].rearrange("p m e -> p (m e)")
                pe.wait_ge(below_ready, 2)
                pe.wait_ge(step, PICKED)
                pe.matmul(psC[:, 0:PAIRS * E], below[:, :], flat, start=True, stop=True)
                pe.matmul(psC[:, 512:512 + PAIRS * E], ones[:, :], flat, start=True, stop=True).then_inc(counted, 1)
                pe.wait_ge(owner_ready, 1)
                pe.wait_ge(b2_in, 16)

                def expert_of(j):
                    return pe.value_load(owner[0:1, bass.ds(j, 1)], min_val=0, max_val=E - 1)

                def turn(j, s, first=False):
                    pe.wait_ge(xg_in[s], j * 8 + (16 - 8 * s))
                    if not first:
                        pe.wait_ge(xgT_ready, j)
                    for k in range(2):
                        last = pe.transpose(psT[0:HO, k * RT:(k + 1) * RT], xg[s][:, k * HO:(k + 1) * HO], ident[:, :])
                    last.then_inc(xg_turned, 1)

                def widen(j, s, first=False):
                    e = expert_of(j)
                    pe.wait_ge(xgT_ready, j + 1)
                    if not first:
                        pe.wait_ge(hid_ready, j)
                    for at, size in ((0, 512), (512, H - 512)):
                        for k in range(2):
                            rows = HO + 1 - k
                            last = pe.matmul(psH[:, at:at + size], xgT[s][0:rows, k, :],
                                             W1[0:rows, bass.ds(e * (2 * H) + (k * H + at), size)],
                                             start=(k == 0), stop=(k == 1))
                    last.then_inc(hidden, 1)

                def turn_hidden(j, s, first=False):
                    pe.wait_ge(hid_ready, j + 1)
                    if not first:
                        pe.wait_ge(hidT_ready, j)
                    for b in range(H // 128):
                        last = pe.transpose(psHT[:, b * RT:(b + 1) * RT], hid[s][:, b * 128:(b + 1) * 128], ident[:, :])
                    last.then_inc(hid_turned, 1)

                def narrow(j, s, first=False):
                    e = expert_of(j)
                    pe.wait_ge(hidT_ready, j + 1)
                    if not first:
                        pe.wait_ge(yg_ready, j)
                    pe.matmul(psY[:, 0:O], ones[0:1, 0:RT], b2_row[:, bass.ds(e * O, O)], start=True, stop=False)
                    for b in range(H // 128):
                        last = pe.matmul(psY[:, 0:O], hidT[s][:, b, :],
                                         W2[:, bass.ds(e * (H // 128 * O) + b * O, O)],
                                         start=False, stop=(b == H // 128 - 1))
                    last.then_inc(y_done, 1)

                turn(0, 0, first=True)
                turn(1, 1)
                widen(0, 0, first=True)
                turn_hidden(0, 0, first=True)
                widen(1, 1)
                narrow(0, 0, first=True)
                turn(2, 0)
                with pe.Fori(0, (TILES - 4) // 2) as t:
                    for e in range(2):
                        j, s = t * 2 + (e + 1), 1 - e
                        turn_hidden(j, s)
                        widen(j + 1, 1 - s)
                        narrow(j, s)
                        turn(j + 2, s)
                for j in range(TILES - 3, TILES):
                    turn_hidden(j, j % 2)
                    if j + 1 < TILES:
                        widen(j + 1, (j + 1) % 2)
                    narrow(j, j % 2)
                    if j + 2 < TILES:
                        turn(j + 2, j % 2)

            @block.sync
            def _(sp):
                sp.dma_start(b2_row[:, :], d["b2"].rearrange("(a e) o -> a (e o)", a=1)).then_inc(b2_in, 16)
                sp.wait_ge(scattered, 16 * 2 * PAIRS)

                def load(j, s, first=False):
                    if not first:
                        sp.wait_ge(xg_turned, j - 1)
                    sp.dma_start(xg[s][:, :], d["xg"][bass.ds(j * RT, RT), :]).then_inc(xg_in[s], 16)

                def store(j, s):
                    sp.wait_ge(yg_ready, j + 1)
                    sp.dma_start(d["yg"][bass.ds(j * RT, RT), :], yg[s][:, :]).then_inc(y_stored[s], 16)

                load(0, 0, first=True)
                load(1, 1, first=True)
                with sp.Fori(0, TILES // 2 - 1) as t:
                    for e in range(2):
                        load(t * 2 + (e + 2), e)
                        store(t * 2 + e, e)
                for j in range(TILES - 2, TILES):
                    store(j, j % 2)
                for s in range(2):
                    sp.wait_ge(y_stored[s], 16 * (TILES // 2))
                sp.sem_inc(all_stored, 1)
                rows = out.rearrange("(m i) n o -> i n m o", i=2)
                for m in range(0, PAIRS, 4):
                    sp.wait_ge(final, m + 4)
                    for i in range(2):
                        sp.dma_start(rows[i, :, m:m + 4, :],
                                     H2[64 * i:64 * i + N, m * O:(m + 4) * O].rearrange("p (m o) -> p m o", o=O))\
                            .then_inc(stored, 16)
                sp.wait_ge(stored, 16 * (PAIRS // 2))


def vit_kernel(nc, d, out):
    d["off_all"] = nc.dram_tensor("off_all", [G, STR, NP, 2 * K], F32, kind="Internal").ap()
    d["xg"] = nc.dram_tensor("xg_all", [SLOTS, O], F32, kind="Internal").ap()
    d["yg"] = nc.dram_tensor("yg_all", [SLOTS, O], F32, kind="Internal").ap()
    with ExitStack() as ctx:
        def sb(name, shape):
            return ctx.enter_context(nc.sbuf_tensor(name, shape, F32))

        ident = sb("ident", [128, 128])
        ones = sb("ones", [128, 128])
        HT = sb("HT", [HO, 2, TP])
        with nc.sbuf_tensor("dwT", [128, BLK, O], F32) as dwT, nc.sbuf_tensor("far", [1, 1], I32) as far:
            tokenizer(nc, d, HT, dwT, far, ident, ones)
            far_taps(nc, d, HT, dwT, far, ident, ones)
            batch_norm(nc, d, HT, HT)
        H2 = sb("H2", [128, PAIRS * O])
        SSQ = sb("SSQ", [128, PAIRS * 6])
        RL = sb("RL", [128, PAIRS * RC])
        W1 = sb("W1", [128, E * 2 * H])
        W2 = sb("W2", [128, E * H // 128 * O])
        attention(nc, d, HT, H2, SSQ, W1, W2, ident, ones)
        mix(nc, d, HT, H2, SSQ, RL, ident, ones)
        experts(nc, d, out, H2, W1, W2, RL, ident, ones)


_INS = ['x', 'L0_tok_offset_w', 'L0_tok_offset_b', 'L0_tok_dconv_w', 'L0_tok_bn_gamma', 'L0_tok_bn_beta', 'L0_attn_Wq', 'L0_attn_bq', 'L0_attn_Wk', 'L0_attn_bk', 'L0_attn_Wv', 'L0_attn_bv', 'L0_attn_Wo', 'L0_attn_bo', 'L0_attn_lambda_q1', 'L0_attn_lambda_k1', 'L0_attn_lambda_q2', 'L0_attn_lambda_k2', 'L0_attn_norm_weight', 'L0_ffn_router_w', 'L0_ffn_probe_w', 'L0_ffn_router_emb', 'L0_ffn_fatigue', 'L0_ffn_energy', 'L0_ffn_w_fast1', 'L0_ffn_w_slow1', 'L0_ffn_h_fast1', 'L0_ffn_m_gate1', 'L0_ffn_b1', 'L0_ffn_w_fast2', 'L0_ffn_w_slow2', 'L0_ffn_h_fast2', 'L0_ffn_m_gate2', 'L0_ffn_b2']
_OUT = (64, 49, 192)


def kernel(**inputs):
    import numpy as _np
    import concourse.bacc as _bacc
    from concourse import mybir as _mybir
    from concourse.bass_utils import run_bass_kernel_spmd as _run

    nc = _bacc.Bacc("TRN2", target_bir_lowering=False, num_devices=1)
    arrays, views = {}, {}
    for name in _INS:
        a = _np.ascontiguousarray(inputs[name])
        arrays[f"in_{name}"] = a
        short = name.replace("L0_tok_", "").replace("L0_attn_", "").replace("L0_ffn_", "")
        views[short] = nc.dram_tensor(f"in_{name}", a.shape, _mybir.dt.from_np(a.dtype), kind="ExternalInput").ap()
    out = nc.dram_tensor("out_0", _OUT, _mybir.dt.float32, kind="ExternalOutput").ap()
    vit_kernel(nc, views, out)
    r = _run(nc, [arrays], core_ids=[0])
    return r.results[0]["out_0"]
```

```python
from contextlib import ExitStack

import concourse.bass as bass
from concourse import mybir

F32 = mybir.dt.float32
I32 = mybir.dt.int32
U32 = mybir.dt.uint32
ALU = mybir.AluOpType
ACT = mybir.ActivationFunctionType
AX = mybir.AxisListType

B, C, IMG = 64, 3, 112
PT = 16
NP = IMG // PT
K = PT * PT
O = 192
HO = O // 2
BG = 16
STR = NP * BG
G = B // BG
U = G * NP
N = NP * NP
T = B * N
EPS = 1e-5
TP = T + 16
PAIRS = B // 2
FIRST_STEP, LAST_STEP = 4, PAIRS - 2
HD = 16
SCALE = HD ** -0.5
LAMBDA_INIT = 0.8
E, H, DR = 8, 768, 24
RC = 2 * E + DR
FIRST, LAST = 6, PAIRS - 2
RT = 128
TILES = -(-(2 * T) // RT) + E - 1
SLOTS = TILES * RT
YRING = 8
PICKED = 21
AGGREGATED = 50

R = 2
TAPS = 2 * R + 1
XR, XC = PT + 2 * R, IMG + 2 * R
FAR_ROWS = FAR_COLS = IMG
BLK = 2 * C
NPROD = TAPS * C
PRING = 8
BIAS_AFTER = 3
BUNCH = (3, 8)
XDMA = NP * C


def strided(view, offset, dims):
    return bass.AP(tensor=view.tensor, offset=view.offset + offset, ap=[list(view.ap[0])] + [list(d) for d in dims])


def tokenizer(nc, d, YT, dwT, far, ident, ones):
    with ExitStack() as ctx:
        def sb(name, shape, dt=F32):
            return ctx.enter_context(nc.sbuf_tensor(name, shape, dt))

        def sem(name):
            return ctx.enter_context(nc.semaphore(name))

        def ps(name, banks):
            return ctx.enter_context(nc.psum_tensor(name, [128, banks * 512], F32))

        xs = [sb(f"xs{s}", [STR, C, XR, XC]) for s in range(2)]
        prods = [sb(f"prod{s}", [STR, TAPS, K]) for s in range(PRING)]
        wts = [sb(f"wts{i}", [STR, TAPS, K]) for i in range(TAPS)]
        hats = [sb(f"hats{s}", [STR, 2, TAPS, K]) for s in range(2)]
        patch = [sb(f"patch{s}", [STR, C, K]) for s in range(2)]
        xT = [sb(f"xT{s}", [128, BLK, STR]) for s in range(2)]
        smpT = [sb(f"smpT{s}", [128, BLK, STR]) for s in range(2)]
        off = [sb(f"off{s}", [STR, 2, K]) for s in range(2)]
        owT = sb("owT", [128, BLK, 2, K])
        obias = sb("obias", [STR, 2 * K])
        tapb = sb("tapb", [STR, TAPS])
        reach = sb("reach", [STR, 1])
        beyond = sb("beyond", [STR, 2, 2, K], mybir.dt.bfloat16)
        excess = sb("excess", [STR, U])
        worst = sb("worst", [STR, 1])
        ow_raw = [prods[t][:, :, :] for t in range(4)]

        psT = ps("psT", 2)
        psO = ps("psO", 1)
        psS = ps("psS", 2)
        psX = [ps(f"psX{c}", 1) for c in range(C)]
        psW = psX[0]

        w_in = sem("w_in")
        w_turned = sem("w_turned")
        w_copied = sem("w_copied")
        consts = sem("consts")
        halo_zero = sem("halo_zero")
        xs_in = [sem(f"xs_in{s}") for s in range(2)]
        patch_ready = sem("patch_ready")
        patch_free = sem("patch_free")
        turned = sem("turned")
        xT_ready = sem("xT_ready")
        offs_done = sem("offs_done")
        off_copied = sem("off_copied")
        off_ready = sem("off_ready")
        px_ready = sem("px_ready")
        off_stored = [sem(f"off_stored{s}") for s in range(2)]
        dist_ready = sem("dist_ready")
        hats_ready = sem("hats_ready")
        wts_ready = sem("wts_ready")
        prod_made = sem("prod_made")
        prod_free = sem("prod_free")
        smp_ready = sem("smp_ready")
        y_done = sem("y_done")
        y_ready = sem("y_ready")
        checked = sem("checked")
        worst_ready = sem("worst_ready")
        worst_summed = sem("worst_summed")
        far_ready = sem("far_ready")

        psY = psT[:, 512 + 2 * STR:512 + 4 * STR]

        def block_cols(psum, blk, rows=128, cols=STR):
            at = blk * STR if blk < 4 else 512 + (blk - 4) * STR
            return psum[0:rows, at:at + cols]

        def two_banks(psum):
            return ((psum[:, 0:4 * STR].rearrange("p (b t) -> p b t", b=4), 0, 4),
                    (psum[:, 512:512 + 2 * STR].rearrange("p (b t) -> p b t", b=2), 4, 6))

        def frees_before(n):
            return n + 1 if n >= PRING else n + 1 + 2 * PRING - NPROD if n + PRING < NPROD else 1

        def product(n):
            i, c = divmod(n, C)
            pixels = strided(psX[c][0:STR, :], i * (PT + 2 * R), [[1, TAPS], [PT + 2 * R, PT], [1, PT]])
            shape = "p j (r w) -> p j r w"
            return nc.vector.tensor_tensor(prods[n % PRING][:, :, :].rearrange(shape, r=PT), pixels,
                                           wts[i][:, :, :].rearrange(shape, r=PT), ALU.mult)

        with nc.Block() as block:
            @block.sync
            def _(sp):
                for t in range(4):
                    raw = bass.AP(tensor=prods[t][:, :, :].tensor, offset=0, ap=[[TAPS * K, STR], [1, C * K]])
                    sp.dma_start(raw, d["offset_w"].rearrange("o c h w -> o (c h w)")[t * STR:(t + 1) * STR, :]).then_inc(w_in, 16)
                raw = bass.AP(tensor=prods[4][:, :, :].tensor, offset=0, ap=[[TAPS * K, 64], [1, C * K]])
                sp.dma_start(raw, d["offset_w"].rearrange("o c h w -> o (c h w)")[4 * STR:512, :]).then_inc(w_in, 16)
                for t in range(2):
                    raw = bass.AP(tensor=wts[t][:, :, :].tensor, offset=0, ap=[[TAPS * K, HO], [1, C * K]])
                    sp.dma_start(raw, d["dconv_w"].rearrange("o c h w -> o (c h w)")[t * HO:(t + 1) * HO, :]).then_inc(w_in, 16)
                sp.dma_start(obias[:, :], d["offset_b"].rearrange("(a n) -> a n", a=1).to_broadcast([STR, 2 * K])).then_inc(w_in, 16)

                def load_strips(g):
                    s = g % 2
                    images = d["x"][g * BG:(g + 1) * BG]
                    if g < 2:
                        sp.wait_ge(halo_zero, g + 1)
                    else:
                        done = (g - 1) * NP
                        sp.wait_ge(px_ready, C * done)
                        sp.wait_ge(patch_ready, done)
                    for q in range(NP):
                        r0, r1 = max(q * PT - R, 0), min((q + 1) * PT + R, IMG)
                        top = r0 - (q * PT - R)
                        for c in range(C):
                            sp.dma_start(xs[s][q * BG:(q + 1) * BG, c, top:top + r1 - r0, R:R + IMG],
                                         images[:, c, r0:r1, :]).then_inc(xs_in[s], 16)

                load_strips(0)
                load_strips(1)
                for u in range(U):
                    sp.wait_ge(off_ready, u + 1)
                    sp.dma_start(d["off_all"][u // NP, :, u % NP, :], off[u % 2][:, :, :].rearrange("p a k -> p (a k)"))\
                        .then_inc(off_stored[u % 2], 16)
                    if u % NP == 2 and NP < u < (G - 1) * NP:
                        load_strips(u // NP + 1)
                for s in range(2):
                    sp.wait_ge(off_stored[s], 16 * (U // 2))

            @block.gpsimd
            def _(pool):
                pool.memset(ident[:, :], 0.0).then_inc(consts, 1)
                pool.memset(ones[:, :], 1.0).then_inc(consts, 1)
                pool.memset(tapb[:, 0:1], float(R))
                pool.memset(reach[:, :], -2.0 * R)
                for j in range(1, TAPS):
                    last = pool.memset(tapb[:, j:j + 1], float(R - j))
                last.then_inc(consts, 1)
                pool.wait_ge(consts, 3)
                pool.affine_select(out=ident[:, :], in_=ident[:, :], compare_op=ALU.not_equal, fill=1.0, base=0,
                                   pattern=[[-1, 128]], channel_multiplier=1).then_inc(consts, 1)
                pool.wait_ge(w_in, 16 * 8)
                pool.wait_ge(w_copied, BLK + 3)

                def bias(u, s):
                    pool.wait_ge(off_copied, u + 1)
                    offs = off[s][:, :, :]
                    pool.tensor_tensor(offs, offs, obias[:, :].rearrange("p (k t) -> p t k", t=2), ALU.add)\
                        .then_inc(off_ready, 1)

                def weights(u, s, last=False):
                    pool.wait_ge(hats_ready, u + 1)
                    for i in range(TAPS):
                        pool.wait_ge(prod_made, u * NPROD + C * (i + 1))
                        pool.tensor_tensor(wts[i][:, :, :], strided(hats[s][:, :, :, :], i * K, [[0, TAPS], [1, K]]),
                                           hats[s][:, 1, :, :], ALU.mult).then_inc(wts_ready, 1)
                        if i == BIAS_AFTER and not last:
                            bias(u + 1, 1 - s)

                bias(0, 0)
                with pool.Fori(0, U // 2 - 1) as t:
                    for s in range(2):
                        weights(t * 2 + s, s)
                weights(U - 2, 0)
                weights(U - 1, 1, last=True)

            @block.vector
            def _(dve):
                for s in range(2):
                    dve.memset(xs[s][:, :, :, 0:R], 0.0)
                    dve.memset(xs[s][:, :, :, XC - R:XC], 0.0)
                    dve.memset(xs[s][0:BG, :, 0:R, R:R + IMG], 0.0)
                    dve.memset(xs[s][STR - BG:STR, :, XR - R:XR, R:R + IMG], 0.0).then_inc(halo_zero, 1)
                dve.memset(YT[:, :, T:TP], 0.0)
                dve.wait_ge(w_copied, BLK + 3)
                dve.sem_inc(prod_made, NPROD)

                with dve.Fori(0, U) as u:
                    for n in range(NPROD):
                        if n % C == 0:
                            dve.wait_ge(wts_ready, u * TAPS + (n // C + 1))
                        if n < C:
                            dve.wait_ge(px_ready, u * C + (n + 1))
                        dve.wait_ge(prod_free, u * NPROD + frees_before(n))
                        product(n).then_inc(prod_made, 1)
                dve.wait_ge(checked, U)
                dve.tensor_reduce(worst[:, :], excess[:, :], AX.X, ALU.max).then_inc(worst_ready, 1)
                dve.wait_ge(worst_summed, 1)
                dve.tensor_scalar(far[:, :], psT[0:1, 0:1], 0.0, None, ALU.is_gt).then_inc(far_ready, 1)
                dve.wait_ge(far_ready, 1)

            @block.scalar
            def _(act):
                for blk in range(BLK):
                    act.wait_ge(w_turned, blk + 1)
                    act.activation(owT[:, blk, :, :].rearrange("p t k -> p k t"),
                                   (psO if blk % 2 == 0 else psW)[:, 0:512].rearrange("p (k t) -> p k t", t=2),
                                   ACT.Copy).then_inc(w_copied, 1)
                for t in range(3):
                    act.wait_ge(w_turned, BLK + t + 1)
                    act.activation(dwT[:, 2 * t:2 * t + 2, :],
                                   (psO if t % 2 == 0 else psW)[:, 0:2 * O].rearrange("p (b o) -> p b o", b=2),
                                   ACT.Copy).then_inc(w_copied, 1)

                def copy_patch(u):
                    g, pw = divmod(u, NP)
                    act.wait_ge(xs_in[g % 2], 16 * XDMA * (g // 2 + 1))
                    act.wait_ge(patch_free, u + 1)
                    act.activation(patch[u % 2][:, :, :].rearrange("p c (r w) -> p c r w", r=PT),
                                   xs[g % 2][:, :, R:R + PT, R + pw * PT:R + (pw + 1) * PT],
                                   ACT.Copy).then_inc(patch_ready, 1)

                def copy_pixels(u, c):
                    g, pw = divmod(u, NP)
                    if u % NP == 0:
                        act.wait_ge(xs_in[g % 2], 16 * XDMA * (g // 2 + 1))
                    act.wait_ge(prod_made, NPROD * (u + 1) - (C - 1 - c))
                    act.activation(strided(psX[c][0:STR, :], 0, [[PT + 2 * R, PT + 2 * R], [1, PT + 2 * R]]),
                                   xs[g % 2][:, c, :, pw * PT:pw * PT + PT + 2 * R], ACT.Copy).then_inc(px_ready, 1)

                def copy_xT(u):
                    act.wait_ge(turned, u + 1)
                    if u >= 2:
                        act.wait_ge(offs_done, u - 1)
                    for view, a, b in two_banks(psT):
                        last = act.activation(xT[u % 2][:, a:b, :], view, ACT.Copy)
                    last.then_inc(xT_ready, 1)

                def copy_off(u):
                    act.wait_ge(offs_done, u + 1)
                    if u >= 2:
                        act.wait_ge(off_stored[u % 2], 16 * (u // 2))
                    act.activation(off[u % 2][:, :, :].rearrange("p a k -> p (a k)"), psO[0:STR, :],
                                   ACT.Copy).then_inc(off_copied, 1)

                def make_hats(u):
                    s = u % 2
                    act.wait_ge(off_ready, u + 1)
                    if u >= 2:
                        act.wait_ge(wts_ready, TAPS * (u - 1))
                    for j in range(TAPS):
                        last = act.activation(hats[s][:, :, j, :], off[s][:, :, :], ACT.Abs, bias=tapb[:, j:j + 1])
                    last.then_inc(dist_ready, 1)
                    act.wait_ge(dist_ready, u + 1)
                    if u >= 1:
                        act.wait_ge(checked, u)
                    act.activation(beyond[:, :, :, :],
                                   strided(hats[s][:, :, :, :], 0, [[TAPS * K, 2], [(TAPS - 1) * K, 2], [1, K]]),
                                   ACT.Relu, bias=reach[:, 0:1], accum_out=excess[:, u:u + 1]).then_inc(checked, 1)
                    act.wait_ge(checked, u + 1)
                    act.activation(hats[s][:, :, :, :], hats[s][:, :, :, :], ACT.Relu, bias=ones[0:STR, 0:1],
                                   scale=-1.0).then_inc(hats_ready, 1)

                def copy_sampled(u):
                    act.wait_ge(prod_free, PRING + NPROD * (u + 1))
                    if u >= 2:
                        act.wait_ge(y_done, u - 1)
                    for view, a, b in two_banks(psS):
                        last = act.activation(smpT[u % 2][:, a:b, :], view, ACT.Copy)
                    last.then_inc(smp_ready, 1)

                def copy_y(u):
                    g, pw = divmod(u, NP)
                    act.wait_ge(y_done, u + 1)
                    place = YT[:, :, g * BG * N:(g + 1) * BG * N]\
                        .rearrange("c h (b q w) -> c h q b w", b=BG, q=NP)[:, :, :, :, pw]
                    act.activation(place, psY[0:HO, :].rearrange("c (h q b) -> c h q b", h=2, q=NP),
                                   ACT.Copy).then_inc(y_ready, 1)

                act.wait_ge(consts, 4)
                act.sem_inc(y_ready, 1)
                copy_patch(0)
                copy_patch(1)
                for c in range(C):
                    copy_pixels(0, c)
                for u in range(2):
                    copy_xT(u)
                    copy_off(u)
                    make_hats(u)
                copy_patch(2)
                copy_xT(2)
                copy_patch(3)
                for u in range(U):
                    if u >= 1:
                        copy_y(u - 1)
                    if u + 2 < U:
                        copy_off(u + 2)
                    if u + 1 < U:
                        for c in range(C):
                            copy_pixels(u + 1, c)
                    copy_sampled(u)
                    if u + 3 < U:
                        copy_xT(u + 3)
                    if u + 2 < U:
                        make_hats(u + 2)
                    if u + 4 < U:
                        copy_patch(u + 4)
                copy_y(U - 1)

            @block.tensor
            def _(pe):
                pe.wait_ge(consts, 4)
                pe.wait_ge(w_in, 16 * 8)
                for blk in range(BLK):
                    if blk >= 2:
                        pe.wait_ge(w_copied, blk - 1)
                    for t in range(5):
                        rows = STR if t < 4 else 64
                        raw = bass.AP(tensor=prods[t][:, :, :].tensor, offset=blk * 128, ap=[[TAPS * K, rows], [1, 128]])
                        last = pe.transpose((psO if blk % 2 == 0 else psW)[:, t * STR:t * STR + rows], raw,
                                            ident[0:rows, 0:rows])
                    last.then_inc(w_turned, 1)
                for t in range(3):
                    pe.wait_ge(w_copied, BLK - 1 + t)
                    for b in range(2):
                        for h in range(2):
                            raw = bass.AP(tensor=wts[h][:, :, :].tensor, offset=(2 * t + b) * 128,
                                          ap=[[TAPS * K, HO], [1, 128]])
                            last = pe.transpose((psO if t % 2 == 0 else psW)[:, b * O + h * HO:b * O + (h + 1) * HO],
                                                raw, ident[0:HO, 0:HO])
                    last.then_inc(w_turned, 1)
                pe.wait_ge(w_copied, BLK + 3)
                pe.sem_inc(patch_free, 2)
                pe.sem_inc(prod_free, PRING)

                def turn_patch(u, s, first=False, outputs=None):
                    pe.wait_ge(patch_ready, u + 1)
                    if not first:
                        pe.wait_ge(xT_ready, u)
                    if outputs is not None:
                        pe.wait_ge(y_ready, outputs + 2)
                    for blk in range(BLK):
                        c, h = divmod(blk, 2)
                        last = pe.transpose(block_cols(psT, blk), patch[s][:, c, h * 128:(h + 1) * 128],
                                            ident[0:STR, 0:STR])
                    last.then_inc(turned, 1)
                    pe.wait_ge(turned, u + 1)
                    pe.sem_inc(patch_free, 1)

                def offsets(u, s, first=False):
                    pe.wait_ge(xT_ready, u + 1)
                    if not first:
                        pe.wait_ge(off_copied, u)
                    for blk in range(BLK):
                        last = pe.matmul(psO[0:STR, :], xT[s][:, blk, :],
                                         owT[:, blk, :, :].rearrange("p a k -> p (a k)"),
                                         start=(blk == 0), stop=(blk == BLK - 1))
                    last.then_inc(offs_done, 1)

                def sum_taps(u, products, bunch):
                    pe.wait_ge(prod_made, u * NPROD + (NPROD + bunch + 1))
                    if products[0] == 0 and not (isinstance(u, int) and u == 0):
                        pe.wait_ge(smp_ready, u)
                    for n in products:
                        pe.wait_ge(prod_made, u * NPROD + (NPROD + n + 1))
                        i, c = divmod(n, C)
                        for j in range(TAPS):
                            for h in range(2):
                                blk = 2 * c + h
                                last = pe.matmul(block_cols(psS, blk), prods[n % PRING][:, j, h * 128:(h + 1) * 128],
                                                 ident[0:STR, 0:STR], is_transpose=True,
                                                 start=(i == 0 and j == 0 and blk in (0, 4)),
                                                 stop=(i == TAPS - 1 and j == TAPS - 1), skip_group_check=True)
                        last.then_inc(prod_free, 1)

                def project(u, s, xT_before):
                    pe.wait_ge(smp_ready, u + 1)
                    pe.wait_ge(y_ready, u + 1)
                    pe.wait_ge(xT_ready, xT_before)
                    for h in range(2):
                        for blk in range(BLK):
                            last = pe.matmul(psY[0:HO, h * STR:(h + 1) * STR], dwT[:, blk, h * HO:(h + 1) * HO],
                                             smpT[s][:, blk, :], start=(blk == 0), stop=(blk == BLK - 1))
                    last.then_inc(y_done, 1)

                half = NPROD // 2 + 1
                turn_patch(0, 0, first=True)
                offsets(0, 0, first=True)
                turn_patch(1, 1)
                offsets(1, 1)
                turn_patch(2, 0)
                sum_taps(0, range(half), BUNCH[0])
                offsets(2, 0)
                sum_taps(0, range(half, NPROD), BUNCH[1])
                turn_patch(3, 1)
                with pe.Fori(0, (U - 4) // 2) as m:
                    for e in range(1, 3):
                        u, s = m * 2 + e, e % 2
                        sum_taps(u, range(half), BUNCH[0])
                        offsets(u + 2, s)
                        project(u - 1, 1 - s, u + 3)
                        sum_taps(u, range(half, NPROD), BUNCH[1])
                        turn_patch(u + 3, 1 - s, outputs=u - 1)
                for u in range(U - 3, U):
                    sum_taps(u, range(half), BUNCH[0])
                    if u + 2 < U:
                        offsets(u + 2, u % 2)
                    project(u - 1, (u - 1) % 2, min(u + 3, U))
                    sum_taps(u, range(half, NPROD), BUNCH[1])
                    if u + 3 < U:
                        turn_patch(u + 3, (u + 3) % 2, outputs=u - 1)
                project(U - 1, (U - 1) % 2, U)
                pe.wait_ge(worst_ready, 1)
                pe.matmul(psT[0:1, 0:1], worst[:, 0:1], ones[0:STR, 0:1], start=True, stop=True).then_inc(worst_summed, 1)


def far_taps(nc, d, YT, dwT, far, ident, ones):
    with ExitStack() as ctx:
        def sb(name, shape, dt=F32):
            return ctx.enter_context(nc.sbuf_tensor(name, shape, dt))

        def sem(name):
            return ctx.enter_context(nc.semaphore(name))

        image = sb("image", [STR, IMG * IMG])
        off = sb("far_off", [STR, NP, 2, K])
        pos = sb("pos", [STR, 2, NP, K])
        base_i = sb("base_i", [STR, 2, NP, K], I32)
        strip_i = sb("strip_i", [STR, 1], I32)
        strip_y = sb("strip_y", [STR, 1])
        base = sb("base", [STR, 2, NP, K])
        tap = sb("tap", [STR, 2])
        dist = sb("far_dist", [STR, NP * K])
        row_w = sb("row_w", [STR, NP * K])
        tap_w = sb("tap_w", [STR, NP * K])
        smp = [sb(f"smp{c}", [STR, NP * K]) for c in range(C)]
        smpT = sb("far_smpT", [128, BLK, STR])
        psT = ctx.enter_context(nc.psum_tensor("far_psT", [128, 1024], F32))
        psY = ctx.enter_context(nc.psum_tensor("far_psY", [128, 512], F32))

        grid = sem("far_grid")
        off_in = sem("far_off_in")
        image_in = sem("image_in")
        off_read = sem("far_off_read")
        image_read = sem("image_read")
        setup = sem("far_setup")
        group_ready = sem("group_ready")
        turned = sem("far_turned")
        smpT_ready = sem("far_smpT_ready")
        y_done = sem("far_y_done")
        y_ready = sem("far_y_ready")

        def is_far(eng):
            return eng.value_load(far[0:1, 0:1], min_val=0, max_val=1) > 0

        with nc.Block() as block:
            @block.sync
            def _(sp):
                with sp.If(is_far(sp)):
                    for g in range(G):
                        if g >= 1:
                            sp.wait_ge(off_read, g)
                        sp.dma_start(off[:, :, :, :].rearrange("p w a k -> p (w a k)"),
                                     d["off_all"][g].rearrange("p w k -> p (w k)")).then_inc(off_in, 16)
                        for c in range(C):
                            if g + c >= 1:
                                sp.wait_ge(image_read, g * C + c)
                            for q in range(NP):
                                sp.dma_start(image[q * BG:(q + 1) * BG, :],
                                             d["x"][g * BG:(g + 1) * BG, c].rearrange("b h w -> b (h w)"))\
                                    .then_inc(image_in, 16)

            @block.gpsimd
            def _(pool):
                with pool.If(is_far(pool)):
                    pool.iota(strip_i[:, :], pattern=[[0, 1]], base=0, channel_multiplier=1)
                    pool.iota(base_i[:, 0, :, :], pattern=[[0, NP], [1, PT], [0, PT]], base=0, channel_multiplier=0)
                    pool.iota(base_i[:, 1, :, :], pattern=[[PT, NP], [0, PT], [1, PT]], base=0,
                              channel_multiplier=0).then_inc(grid, 1)

            @block.vector
            def _(dve):
                with dve.If(is_far(dve)):
                    dve.wait_ge(grid, 1)
                    dve.tensor_scalar(strip_i[:, :], strip_i[:, :], -PT, None, ALU.bitwise_and).then_inc(setup, 1)
                    dve.wait_ge(setup, 1)
                    dve.tensor_copy(strip_y[:, :], strip_i[:, :])
                    dve.tensor_copy(base[:, :, :, :], base_i[:, :, :, :]).then_inc(setup, 1)
                    dve.wait_ge(setup, 2)
                    dve.tensor_scalar(base[:, 0, :, :], base[:, 0, :, :], strip_y[:, 0:1], None, ALU.add)\
                        .then_inc(setup, 1)
                    dve.wait_ge(setup, 3)
                    with dve.Fori(0, G) as g:
                        dve.wait_ge(off_in, (g + 1) * 16)
                        dve.tensor_tensor(pos[:, :, :, :], base[:, :, :, :],
                                          off[:, :, :, :].rearrange("p w a k -> p a w k"), ALU.add).then_inc(off_read, 1)
                        for c in range(C):
                            dve.wait_ge(image_in, g * (16 * NP * C) + 16 * NP * (c + 1))
                            dve.memset(smp[c][:, :], 0.0)
                            dve.memset(tap[:, 0:1], 0.0)
                            dve.drain()
                            with dve.Fori(0, FAR_ROWS) as y:
                                dve.tensor_scalar(tap_w[:, :], pos[:, 0, :, :].rearrange("p w k -> p (w k)"), tap[:, 0:1],
                                                  None, ALU.subtract)
                                dve.drain()
                                dve.scalar_tensor_tensor(out=dist[:, :], in0=tap_w[:, :], scalar=-1.0,
                                                         in1=tap_w[:, :], op0=ALU.mult, op1=ALU.max)
                                dve.drain()
                                dve.tensor_scalar(dist[:, :], dist[:, :], -1.0, 1.0, ALU.mult, ALU.add)
                                dve.memset(tap[:, 1:2], 0.0)
                                dve.drain()
                                dve.tensor_scalar(row_w[:, :], dist[:, :], 0.0, None, ALU.max)
                                dve.drain()
                                with dve.Fori(0, FAR_COLS) as x:
                                    dve.tensor_scalar(tap_w[:, :], pos[:, 1, :, :].rearrange("p w k -> p (w k)"),
                                                      tap[:, 1:2], None, ALU.subtract)
                                    dve.drain()
                                    dve.scalar_tensor_tensor(out=dist[:, :], in0=tap_w[:, :], scalar=-1.0,
                                                             in1=tap_w[:, :], op0=ALU.mult, op1=ALU.max)
                                    dve.drain()
                                    dve.tensor_scalar(dist[:, :], dist[:, :], -1.0, 1.0, ALU.mult, ALU.add)
                                    dve.tensor_scalar(tap[:, 1:2], tap[:, 1:2], 1.0, None, ALU.add)
                                    dve.drain()
                                    dve.scalar_tensor_tensor(out=tap_w[:, :], in0=dist[:, :], scalar=0.0,
                                                             in1=row_w[:, :], op0=ALU.max, op1=ALU.mult)
                                    dve.drain()
                                    dve.scalar_tensor_tensor(out=smp[c][:, :], in0=tap_w[:, :],
                                                             scalar=image[:, bass.ds(y * IMG + x, 1)],
                                                             in1=smp[c][:, :], op0=ALU.mult, op1=ALU.add)
                                    dve.drain()
                                dve.tensor_scalar(tap[:, 0:1], tap[:, 0:1], 1.0, None, ALU.add)
                                dve.drain()
                            dve.sem_inc(image_read, 1)
                        dve.sem_inc(group_ready, 1)
                        for pw in range(NP):
                            dve.wait_ge(y_done, g * NP + (pw + 1))
                            place = YT[:, :, bass.ds(g * (BG * N), BG * N)]\
                                .rearrange("c h (b q w) -> c h q b w", b=BG, q=NP)[:, :, :, :, pw]
                            dve.tensor_scalar(place, psY[0:HO, 0:2 * STR].rearrange("c (h q b) -> c h q b", h=2, q=NP),
                                              1.0, None, ALU.mult).then_inc(y_ready, 1)

            @block.scalar
            def _(act):
                with act.If(is_far(act)):
                    with act.Fori(0, U) as u:
                        act.wait_ge(turned, u + 1)
                        for a, b, at in ((0, 4, 0), (4, 6, 512)):
                            last = act.activation(smpT[:, a:b, :], psT[:, at:at + (b - a) * STR]
                                                  .rearrange("p (b t) -> p b t", t=STR), ACT.Copy)
                        last.then_inc(smpT_ready, 1)

            @block.tensor
            def _(pe):
                with pe.If(is_far(pe)):
                    pe.sem_inc(y_ready, 1)
                    with pe.Fori(0, G) as g:
                        pe.wait_ge(group_ready, g + 1)
                        for pw in range(NP):
                            pe.wait_ge(y_ready, g * NP + (pw + 1))
                            for blk in range(BLK):
                                c, h = divmod(blk, 2)
                                at = blk * STR if blk < 4 else 512 + (blk - 4) * STR
                                last = pe.transpose(psT[:, at:at + STR],
                                                    smp[c][:, pw * K + h * 128:pw * K + (h + 1) * 128],
                                                    ident[0:STR, 0:STR])
                            last.then_inc(turned, 1)
                            pe.wait_ge(smpT_ready, g * NP + (pw + 1))
                            for h in range(2):
                                for blk in range(BLK):
                                    last = pe.matmul(psY[0:HO, h * STR:(h + 1) * STR], dwT[:, blk, h * HO:(h + 1) * HO],
                                                     smpT[:, blk, :], start=(blk == 0), stop=(blk == BLK - 1))
                            last.then_inc(y_done, 1)


def batch_norm(nc, d, YT, HT):
    with ExitStack() as ctx:
        def sb(name, shape, dt=F32):
            return ctx.enter_context(nc.sbuf_tensor(name, shape, dt))

        def sem(name):
            return ctx.enter_context(nc.semaphore(name))

        gb = sb("bn_gb", [HO, 2, 2])
        st = sb("bn_st", [HO, 2, NP, 6])
        mv = sb("bn_mv", [HO, 2, 2])
        aff = sb("bn_aff", [HO, 2, 2])
        tmp = sb("bn_tmp", [HO, 2])
        dev = sb("bn_dev", [HO, 2])
        gb_in = sem("bn_gb_in")
        step = sem("bn_step")
        rooted = sem("bn_rooted")
        h_ready = sem("h_ready")

        with nc.Block() as block:
            @block.sync
            def _(sp):
                for n, w in enumerate(("bn_gamma", "bn_beta")):
                    sp.dma_start(gb[:, n, :], d[w].rearrange("(h c) -> c h", h=2),
                                 allow_slow_non_contiguous=True).then_inc(gb_in, 16)

            @block.vector
            def _(dve):
                for h in range(2):
                    for q in range(NP):
                        last = dve.bn_stats(st[:, h, q, :], YT[:, h, q * (T // NP):(q + 1) * (T // NP)])
                last.then_inc(step, 1)
                dve.wait_ge(step, 1)
                for h in range(2):
                    last = dve.bn_aggr(mv[:, h, :], st[:, h, :, :].rearrange("c q s -> c (q s)"))
                last.then_inc(step, 1)
                dve.wait_ge(step, 2)
                dve.tensor_scalar(tmp[:, :], mv[:, :, 1], EPS, None, ALU.add).then_inc(step, 1)
                dve.wait_ge(rooted, 1)
                dve.reciprocal(tmp[:, :], dev[:, :]).then_inc(step, 1)
                dve.wait_ge(step, 4)
                dve.wait_ge(gb_in, 32)
                dve.tensor_tensor(aff[:, 0, :], tmp[:, :], gb[:, 0, :], ALU.mult).then_inc(step, 1)
                dve.wait_ge(step, 5)
                dve.tensor_tensor(tmp[:, :], mv[:, :, 0], aff[:, 0, :], ALU.mult).then_inc(step, 1)
                dve.wait_ge(step, 6)
                dve.tensor_tensor(aff[:, 1, :], gb[:, 1, :], tmp[:, :], ALU.subtract).then_inc(step, 1)

            @block.scalar
            def _(act):
                act.wait_ge(step, 3)
                act.activation(dev[:, :], tmp[:, :], ACT.Sqrt).then_inc(rooted, 1)
                act.wait_ge(step, 7)
                for h in range(2):
                    act.activation(HT[:, h, 0:T], YT[:, h, 0:T], ACT.Gelu, bias=aff[:, 1, h:h + 1],
                                   scale=aff[:, 0, h:h + 1]).then_inc(h_ready, 1)


def attention(nc, d, HT, OUTS, SSQ, W1, W2, ident, ones):
    with ExitStack() as ctx:
        def sb(name, shape, dt=F32):
            return ctx.enter_context(nc.sbuf_tensor(name, shape, dt))

        def sem(name):
            return ctx.enter_context(nc.semaphore(name))

        def ps(name, banks):
            return ctx.enter_context(nc.psum_tensor(name, [128, banks * 512], F32))

        wqkv = sb("wqkv", [HO, 3, 2, O])
        qk_bias = sb("qk_bias", [HO, 2, 2])
        q_bias = sb("q_bias", [HO, 2])
        bv_row = sb("bv_row", [1, O])
        bv_all = sb("bv_all", [128, O // 2])
        lam_in = sb("lam_in", [1, 4, HD])
        lam_pr = sb("lam_pr", [1, 2, HD])
        lam_sum = sb("lam_sum", [1, 2])
        lam_exp = sb("lam_exp", [1, 2])
        neg_lam = sb("neg_lam", [1, 1])
        head_sign = sb("head_sign", [128, 6, 2])
        head_mask = sb("head_mask", [HO, 6])
        kx_bias = sb("kx_bias", [HO, 2, 6])
        hp = [sb(f"hp{s}", [HO, 2, 128]) for s in range(2)]
        qT = [sb(f"qT{s}", [HO, 2, 128]) for s in range(2)]
        kx = [sb(f"kx{s}", [HO, 2, 2, 6, N]) for s in range(2)]
        vals = [sb(f"vals{s}", [128, 2, O // 2]) for s in range(2)]
        top = [sb(f"top{s}", [128, 12]) for s in range(2)]
        den = [sb(f"den{s}", [128, 12]) for s in range(2)]
        coef = [sb(f"coef{s}", [128, 12]) for s in range(2)]
        ex = [sb(f"ex{s}", [128, 12, N]) for s in range(2)]
        pm = [sb(f"pm{s}", [128, 2, 6, 64]) for s in range(2)]
        dT = [sb(f"dT{s}", [128, 3, 128]) for s in range(2)]
        sq = [sb(f"sq{s}", [128, O]) for s in range(2)]
        ssq = [sb(f"ssq{s}", [128, 6]) for s in range(2)]

        stage = [sb(f"stage_{n}", [128, 2 * H]) for n in ("fast", "slow", "h")]
        zero = sb("zero", [128, O])
        gates_row = sb("gates_row", [1, 2, E])
        gates = sb("gates", [128, 2, E])

        psP = ps("psP", 1)
        psV = ps("psV", 1)
        psA = ps("psA", 2)
        psD = ps("psD", 1)
        psX = ps("psX", 2)

        w_in = sem("a_w_in")
        b1_in = sem("b1_in")
        zero_ready = sem("zero_ready")
        slots_zero = sem("slots_zero")
        stage_in = sem("stage_in")
        stage_free = sem("stage_free")
        stage_step = sem("stage_step")
        stage_taken = sem("stage_taken")
        setup = sem("a_setup")
        mask_ready = sem("mask_ready")
        lam_ready = sem("lam_ready")
        lam_expd = sem("lam_expd")
        spread = sem("a_spread")
        hp_ready = sem("hp_ready")
        qk_done = sem("qk_done")
        v_done = sem("v_done")
        q_ready = sem("q_ready")
        v_ready = sem("v_ready")
        scored = sem("scored")
        top_ready = sem("top_ready")
        shifted = sem("shifted")
        exped = sem("exped")
        den_ready = sem("den_ready")
        coef_ready = sem("coef_ready")
        pm_ready = sem("pm_ready")
        diffed = sem("diffed")
        dT_ready = sem("dT_ready")
        weighing = sem("weighing")
        av_done = sem("av_done")
        sq_ready = sem("sq_ready")
        ssq_ready = sem("ssq_ready")
        out_ready = sem("out_ready")

        def paired(psum):
            return psum[:, :].rearrange("p (b c) -> p b c", b=2)[:, :, 0:6 * N].rearrange("p b (h k) -> p b h k", k=N)

        def by_head(tile):
            return strided(tile[:, :], 0, [[6, 2], [1, 6], [0, N]])

        def head_order(psum):
            return psum[:, :].rearrange("p (g c) -> p g c", g=2)[:, :, 0:O // 2].rearrange("p g (f v) -> p f g v", f=3)

        def exists(m):
            return not isinstance(m, int) or 0 <= m < PAIRS

        def reused(m):
            return not isinstance(m, int) or m >= 2

        def another(m):
            return not isinstance(m, int) or m >= 1

        with nc.Block() as block:
            @block.sync
            def _(sp):
                for n, w in enumerate(("Wq", "Wk", "Wv")):
                    sp.dma_start(wqkv[:, n, :, :], d[w].rearrange("(k c) o -> c k o", k=2)).then_inc(w_in, 16)
                for n, w in enumerate(("bq", "bk")):
                    sp.dma_start(qk_bias[:, n, :], d[w].rearrange("(h c) -> c h", h=2),
                                 allow_slow_non_contiguous=True).then_inc(w_in, 16)
                sp.dma_start(bv_row[:, :], d["bv"].rearrange("(a n) -> a n", a=1)).then_inc(w_in, 16)
                for n, w in enumerate(("lambda_q1", "lambda_q2", "lambda_k1", "lambda_k2")):
                    sp.dma_start(lam_in[:, n, :], d[w].rearrange("(a n) -> a n", a=1)).then_inc(w_in, 16)
                for n, w in enumerate(("m_gate1", "m_gate2")):
                    sp.dma_start(gates_row[:, n, :], d[w].rearrange("(a n) -> a n", a=1)).then_inc(w_in, 16)
                sp.dma_start(W1[HO:HO + 1, :].rearrange("a (e k h) -> a e k h", e=E, k=2)[:, :, 0, :],
                             d["b1"].rearrange("(a e) h -> a e h", a=1)).then_inc(b1_in, 16)
                sp.wait_ge(zero_ready, 1)
                sp.dma_start(d["xg"].rearrange("(p t) o -> p t o", p=128), strided(zero[:, :], 0, [[0, TILES], [1, O]]))\
                    .then_inc(slots_zero, 16)
                with sp.Fori(0, E) as e:
                    for n in range(2):
                        sp.wait_ge(stage_free, e * 2 + (n + 1))
                        for t, w in enumerate(("w_fast", "w_slow", "h_fast")):
                            src = d[w + "12"[n]].rearrange("e r c -> (e r) c")
                            if n == 0:
                                sp.dma_start(stage[t][0:HO, :].rearrange("c (k h) -> c k h", k=2),
                                             src[bass.ds(e * O, O), :].rearrange("(k c) h -> c k h", k=2))\
                                    .then_inc(stage_in, 16)
                            else:
                                sp.dma_start(stage[t][:, 0:H // 128 * O].rearrange("p (b o) -> p b o", o=O),
                                             src[bass.ds(e * H, H), :].rearrange("(b p) o -> p b o", p=128))\
                                    .then_inc(stage_in, 16)
                sp.wait_ge(b1_in, 16)
                sp.wait_ge(slots_zero, 16)

            @block.gpsimd
            def _(pool):
                pool.memset(head_mask[:, :], 1.0).then_inc(mask_ready, 1)
                pool.wait_ge(mask_ready, 1)
                pool.affine_select(out=head_mask[:, :], in_=head_mask[:, :], compare_op=ALU.is_ge, fill=0.0, base=0,
                                   pattern=[[-HD, 6]], channel_multiplier=1).then_inc(mask_ready, 1)
                pool.wait_ge(mask_ready, 2)
                pool.affine_select(out=head_mask[:, :], in_=head_mask[:, :], compare_op=ALU.is_ge, fill=0.0,
                                   base=HD - 1, pattern=[[HD, 6]], channel_multiplier=-1).then_inc(mask_ready, 1)
                pool.wait_ge(mask_ready, 3)

                def window(m, s):
                    if reused(m):
                        pool.wait_ge(v_done, m - 1)
                    view = HT[:, :, bass.ds(m * (2 * N), N + 64)]
                    pool.tensor_copy(hp[s][:, :, :].rearrange("c h (i t) -> c h i t", i=2),
                                     bass.AP(tensor=view.tensor, offset=view.offset,
                                             ap=[list(view.ap[0]), [TP, 2], [N, 2], [1, 64]])).then_inc(hp_ready, 1)

                window(0, 0)
                window(1, 1)

                def put_together(e, n, part):
                    rows, width, W = (HO, 2 * H, W1) if n == 0 else (128, H // 128 * O, W2)
                    at, size = part * (width // 2), width // 2
                    fast, slow, h = (t[0:rows, at:at + size] for t in stage)
                    dst = W[0:rows, bass.ds(e * width + at, size)]
                    gate = gates[0:rows, n, bass.ds(e, 1)]
                    steps = e * 12 + (6 * n + 3 * part)
                    pool.wait_ge(stage_in, e * (16 * 6) + 48 * (n + 1))
                    pool.sem_inc(stage_taken, 1)
                    pool.tensor_tensor(slow, slow, bass.AP(tensor=gate.tensor, offset=gate.offset,
                                                           ap=[list(gate.ap[0]), [0, size]]), ALU.mult)\
                        .then_inc(stage_step, 1)
                    pool.wait_ge(stage_step, steps + 1)
                    pool.tensor_tensor(slow, slow, fast, ALU.add).then_inc(stage_step, 1)
                    pool.wait_ge(stage_step, steps + 2)
                    pool.sem_inc(stage_taken, 1)
                    pool.tensor_tensor(dst, slow, h, ALU.add).then_inc(stage_step, 1)
                    if part == 1:
                        pool.wait_ge(stage_step, steps + 3)
                        pool.sem_inc(stage_free, 1)

                pool.wait_ge(setup, 6)
                pool.sem_inc(stage_free, 1)
                with pool.Fori(0, E - 1) as e:
                    for q in range(4):
                        window(e * 4 + (q + 2), q % 2)
                        put_together(e, q // 2, q % 2)
                for m in range(PAIRS - 2, PAIRS):
                    window(m, m % 2)
                for q in range(4):
                    put_together(E - 1, q // 2, q % 2)

            @block.vector
            def _(dve):
                dve.memset(zero[:, :], 0.0).then_inc(zero_ready, 1)
                for s in range(2):
                    last = dve.memset(pm[s][:, :, :, N:64], 0.0)
                dve.memset(head_sign[:, :, 0], 1.0).then_inc(setup, 1)
                dve.wait_ge(w_in, 16 * 12)
                dve.tensor_scalar(q_bias[:, :], qk_bias[:, 0, :], SCALE, None, ALU.mult).then_inc(setup, 1)
                dve.tensor_tensor(lam_pr[:, :, :], lam_in[:, 0:2, :], lam_in[:, 2:4, :], ALU.mult).then_inc(lam_ready, 1)
                dve.wait_ge(lam_ready, 1)
                dve.tensor_reduce(lam_sum[:, :], lam_pr[:, :, :], AX.X, ALU.add).then_inc(lam_ready, 1)
                dve.wait_ge(lam_expd, 1)
                dve.scalar_tensor_tensor(out=neg_lam[:, :], in0=lam_exp[:, 1:2], scalar=LAMBDA_INIT,
                                         in1=lam_exp[:, 0:1], op0=ALU.subtract, op1=ALU.subtract).then_inc(lam_ready, 1)
                dve.wait_ge(spread, 1)
                dve.tensor_copy(head_sign[:, :, 1], psD[:, 0:6]).then_inc(setup, 1)
                dve.tensor_copy(bv_all[:, :], psX[:, 0:O // 2]).then_inc(setup, 1)
                dve.tensor_copy(gates[:, :, :].rearrange("p a e -> p (a e)"), psD[:, 8:8 + 2 * E]).then_inc(setup, 1)
                dve.wait_ge(mask_ready, 3)
                dve.tensor_tensor(kx_bias[:, :, :], strided(head_mask[:, :], 0, [[0, 2], [1, 6]]),
                                  strided(qk_bias[:, :, :], 2, [[1, 2], [0, 6]]), ALU.mult).then_inc(setup, 1)
                dve.wait_ge(setup, 6)

                def values(m, s):
                    if not exists(m):
                        return
                    dve.wait_ge(v_done, m + 1)
                    if reused(m):
                        dve.wait_ge(av_done, m - 1)
                    dve.tensor_tensor(vals[s][:, :, :], psV[:, 0:O].rearrange("p (i v) -> p i v", i=2),
                                      strided(bv_all[:, :], 0, [[0, 2], [1, O // 2]]), ALU.add).then_inc(v_ready, 1)

                def shift(m, s):
                    if not exists(m):
                        return
                    dve.wait_ge(scored, m + 1)
                    if reused(m):
                        dve.wait_ge(pm_ready, m - 1)
                    dve.tensor_reduce(top[s][:, :], paired(psA), AX.X, ALU.max).then_inc(top_ready, 1)
                    dve.wait_ge(top_ready, m + 1)
                    dve.tensor_tensor(ex[s][:, :, :].rearrange("p (b h) k -> p b h k", b=2), paired(psA), by_head(top[s]),
                                      ALU.subtract).then_inc(shifted, 1)

                def maps(m, s):
                    if not exists(m):
                        return
                    dve.wait_ge(exped, m + 1)
                    dve.tensor_reduce(den[s][:, :], ex[s][:, :, :], AX.X, ALU.add).then_inc(den_ready, 1)
                    dve.wait_ge(den_ready, m * 2 + 1)
                    dve.reciprocal(den[s][:, :], den[s][:, :]).then_inc(den_ready, 1)
                    dve.wait_ge(den_ready, m * 2 + 2)
                    dve.tensor_tensor(coef[s][:, :], den[s][:, :], head_sign[:, :, :].rearrange("p e m -> p (e m)"),
                                      ALU.mult).then_inc(coef_ready, 1)
                    dve.wait_ge(coef_ready, m + 1)
                    if reused(m):
                        dve.wait_ge(diffed, m - 1)
                    for b in range(2):
                        last = dve.tensor_tensor(pm[s][:, :, 3 * b:3 * b + 3, 0:N].rearrange("p m e k -> p e m k"),
                                                 ex[s][:, 6 * b:6 * b + 6, :].rearrange("p (e m) k -> p e m k", m=2),
                                                 strided(coef[s][:, :], 6 * b, [[2, 3], [1, 2], [0, N]]), ALU.mult)
                    last.then_inc(pm_ready, 1)

                def outputs(m, s):
                    if not exists(m):
                        return
                    dve.wait_ge(sq_ready, m + 1)
                    dve.tensor_scalar(OUTS[:, bass.ds(m * O, O)].rearrange("p (f g v) -> p f g v", f=3, g=2), head_order(psX),
                                      1.0, None, ALU.mult).then_inc(out_ready, 1)
                    dve.tensor_reduce(ssq[s][:, :], sq[s][:, :].rearrange("p (e v) -> p e v", e=6), AX.X,
                                      ALU.add).then_inc(ssq_ready, 1)
                    dve.wait_ge(ssq_ready, m + 1)
                    dve.tensor_scalar(SSQ[:, bass.ds(m * 6, 6)], ssq[s][:, :], 1.0, None, ALU.mult)

                def step_of(i, s):
                    shift(i + 1, 1 - s)
                    maps(i, s)
                    outputs(i - 1, 1 - s)
                    values(i + 1, 1 - s)

                for i in range(-2, FIRST_STEP):
                    step_of(i, i % 2)
                with dve.Fori(0, (LAST_STEP - FIRST_STEP) // 2) as t:
                    for e in range(2):
                        step_of(t * 2 + (FIRST_STEP + e), e)
                for i in range(LAST_STEP, PAIRS + 1):
                    step_of(i, i % 2)

            @block.scalar
            def _(act):
                act.wait_ge(lam_ready, 2)
                act.activation(lam_exp[:, :], lam_sum[:, :], ACT.Exp).then_inc(lam_expd, 1)
                act.wait_ge(setup, 6)

                def queries_keys(m, s):
                    if not exists(m):
                        return
                    act.wait_ge(qk_done, m + 1)
                    if reused(m):
                        act.wait_ge(scored, m - 1)
                    for h in range(2):
                        keys = psP[0:HO, 256 + h * 128:384 + h * 128].rearrange("c (i t) -> c i t", i=2)[:, :, 0:N]
                        for e in range(6):
                            last = act.activation(kx[s][:, h, :, e, :], keys, ACT.Identity,
                                                  bias=kx_bias[:, h, e:e + 1], scale=head_mask[:, e:e + 1])
                    for h in range(2):
                        last = act.activation(qT[s][:, h, :], psP[0:HO, h * 128:(h + 1) * 128], ACT.Identity,
                                              bias=q_bias[:, h:h + 1], scale=SCALE)
                    last.then_inc(q_ready, 1)

                def exps(m, s):
                    if not exists(m):
                        return
                    act.wait_ge(shifted, m + 1)
                    act.activation(ex[s][:, :, :], ex[s][:, :, :], ACT.Exp).then_inc(exped, 1)

                def differences(m, s):
                    if not exists(m):
                        return
                    act.wait_ge(diffed, m + 1)
                    if reused(m):
                        act.wait_ge(av_done, m - 1)
                    act.activation(dT[s][:, :, :].rearrange("p f q -> p (f q)"), psD[:, 0:3 * 128],
                                   ACT.Copy).then_inc(dT_ready, 1)

                def squares(m, s):
                    if not exists(m):
                        return
                    act.wait_ge(av_done, m + 1)
                    if reused(m):
                        act.wait_ge(ssq_ready, m - 1)
                    act.activation(sq[s][:, :].rearrange("p (f g v) -> p f g v", f=3, g=2), head_order(psX),
                                   ACT.Square).then_inc(sq_ready, 1)

                def step_of(i, s):
                    queries_keys(i + 2, s)
                    exps(i + 1, 1 - s)
                    squares(i - 1, 1 - s)
                    differences(i, s)

                for i in range(-2, FIRST_STEP):
                    step_of(i, i % 2)
                with act.Fori(0, (LAST_STEP - FIRST_STEP) // 2) as t:
                    for e in range(2):
                        step_of(t * 2 + (FIRST_STEP + e), e)
                for i in range(LAST_STEP, PAIRS + 1):
                    step_of(i, i % 2)

            @block.tensor
            def _(pe):
                pe.wait_ge(lam_ready, 3)
                pe.matmul(psD[:, 0:6], ones[0:1, 0:128], neg_lam[:, 0:1].to_broadcast([1, 6]), start=True, stop=True)
                pe.matmul(psD[:, 8:8 + 2 * E], ones[0:1, 0:128], gates_row[:, :, :].rearrange("p a e -> p (a e)"),
                          start=True, stop=True)
                bv_view = bv_row[:, :].rearrange("p (f g v) -> p g f v", g=2, v=2 * HD)
                for g in range(2):
                    last = pe.matmul(psX[64 * g:64 * g + 64, 0:O // 2], ones[0:1, 0:64], bv_view[:, g, :, :],
                                     start=True, stop=True)
                last.then_inc(spread, 1)
                pe.wait_ge(setup, 6)

                def project(m, s):
                    if not exists(m):
                        return
                    pe.wait_ge(hp_ready, m + 1)
                    if another(m):
                        pe.wait_ge(q_ready, m)
                    for n in range(2):
                        for h in range(2):
                            at = n * 256 + h * 128
                            for k in range(2):
                                last = pe.matmul(psP[0:HO, at:at + 128], wqkv[:, n, k, h * HO:(h + 1) * HO],
                                                 hp[s][:, k, :], start=(k == 0), stop=(k == 1))
                    last.then_inc(qk_done, 1)

                def project_values(m, s):
                    if not exists(m):
                        return
                    if another(m):
                        pe.wait_ge(v_ready, m)
                        pe.sem_inc(weighing, 1)
                    for i in range(2):
                        for g in range(2):
                            for k in range(2):
                                rhs = wqkv[:, 2, k, :].rearrange("c (f g v) -> c g f v", g=2, v=2 * HD)[:, g, :, :]
                                last = pe.matmul(psV[64 * g:64 * g + 64, i * HO:(i + 1) * HO],
                                                 hp[s][:, k, 64 * i:64 * i + 64], rhs, start=(k == 0), stop=(k == 1))
                    last.then_inc(v_done, 1)

                def scores(m, s):
                    if not exists(m):
                        return
                    pe.wait_ge(q_ready, m + 1)
                    if another(m):
                        pe.wait_ge(shifted, m)
                    for i in range(2):
                        for h in range(2):
                            last = pe.matmul(psA[64 * i:64 * i + 64, h * 512:h * 512 + 6 * N],
                                             qT[s][:, h, 64 * i:64 * i + 64],
                                             kx[s][:, h, i, :, :].rearrange("c h k -> c (h k)"),
                                             start=True, stop=True)
                    last.then_inc(scored, 1)

                def turn_maps(m, s):
                    if not exists(m):
                        return
                    pe.wait_ge(pm_ready, m + 1)
                    if another(m):
                        pe.wait_ge(dT_ready, m)
                    for f in range(3):
                        for n in range(2):
                            last = pe.matmul(psD[:, f * 128:(f + 1) * 128],
                                             pm[s][:, n, 2 * f:2 * f + 2, :].rearrange("p e k -> p (e k)"),
                                             ident[:, :], is_transpose=True, start=(n == 0), stop=(n == 1))
                    last.then_inc(diffed, 1)

                def weigh_values(m, s):
                    if not exists(m):
                        return
                    pe.wait_ge(dT_ready, m + 1)
                    pe.wait_ge(v_ready, m + 1)
                    if another(m):
                        pe.wait_ge(out_ready, m)
                        pe.wait_ge(sq_ready, m)
                    pe.sem_inc(weighing, 1)
                    for i in range(2):
                        for f in range(3):
                            for g in range(2):
                                last = pe.matmul(psX[64 * i:64 * i + 64, g * 512 + f * 2 * HD:g * 512 + (f + 1) * 2 * HD],
                                                 dT[s][64 * g:64 * g + N, f, 64 * i:64 * i + 64],
                                                 vals[s][64 * g:64 * g + N, i, f * 2 * HD:(f + 1) * 2 * HD],
                                                 start=True, stop=True)
                    last.then_inc(av_done, 1)

                def step_of(i, s):
                    scores(i + 1, 1 - s)
                    project(i + 2, s)
                    project_values(i + 1, 1 - s)
                    weigh_values(i - 1, 1 - s)
                    turn_maps(i, s)

                for i in range(-2, FIRST_STEP):
                    step_of(i, i % 2)
                with pe.Fori(0, (LAST_STEP - FIRST_STEP) // 2) as t:
                    for e in range(2):
                        step_of(t * 2 + (FIRST_STEP + e), e)
                for i in range(LAST_STEP, PAIRS + 1):
                    step_of(i, i % 2)


def mix(nc, d, HT, H2, SSQ, RL, ident, ones):
    with ExitStack() as ctx:
        def sb(name, shape, dt=F32):
            return ctx.enter_context(nc.sbuf_tensor(name, shape, dt))

        def sem(name):
            return ctx.enter_context(nc.semaphore(name))

        def ps(name, banks):
            return ctx.enter_context(nc.psum_tensor(name, [128, banks * 512], F32))

        wo = sb("wo", [HO, 2, O])
        nw = sb("nw", [HO, 1])
        bo_row = sb("bo_row", [1, O])
        eps = sb("eps", [128, 1])
        hw = [sb(f"hw{s}", [HO, 2, 128]) for s in range(2)]
        on = [sb(f"on{s}", [128, O]) for s in range(2)]
        oT = [sb(f"oT{s}", [HO, 2, 128]) for s in range(2)]
        hn = [sb(f"hn{s}", [128, O]) for s in range(2)]
        hnT = [sb(f"hnT{s}", [HO, 2, 128]) for s in range(2)]
        rms = sb("rms", [128, PAIRS * 6])
        st = [sb(f"ln_st{s}", [128, 6]) for s in range(2)]
        mv = [sb(f"ln_mv{s}", [128, 2]) for s in range(2)]
        dev = [sb(f"ln_dev{s}", [128, 1]) for s in range(2)]
        rstd = [sb(f"ln_rstd{s}", [128, 1]) for s in range(2)]
        rw = sb("rw", [E, O])
        pw = sb("pw", [DR, O])
        emb = sb("emb", [E, DR])
        emb2 = sb("emb2", [E, DR])
        embn = sb("embn", [E, DR])
        embT = sb("embT", [DR, E])
        gain = sb("gain", [E, 4])
        align = sb("align", [E, O])
        RW = sb("RW", [HO, 2, RC])
        bias8 = sb("bias8", [1, 3, E])
        rl_row = sb("rl_row", [1, RC])

        psO = [ps(f"m_psO{s}", 1) for s in range(2)]
        psM = [ps(f"m_psM{s}", 1) for s in range(2)]
        psN = [ps(f"m_psN{s}", 1) for s in range(2)]
        psR = [ps(f"m_psR{s}", 1) for s in range(2)]

        w_in = sem("m_w_in")
        eps_ready = sem("eps_ready")
        step = sem("m_step")
        rooted = sem("m_rooted")
        turned = sem("m_turned")
        wo_ready = sem("wo_ready")
        hw_ready = sem("hw_ready")
        on_ready = sem("on_ready")
        o_turned = sem("o_turned")
        oT_ready = sem("oT_ready")
        mixed = sem("mixed")
        stats_ready = sem("stats_ready")
        stats_waited = sem("stats_waited")
        mv_ready = sem("mv_ready")
        dev_ready = sem("dev_ready")
        rstd_ready = sem("rstd_ready")
        hn_ready = sem("hn_ready")
        hn_turned = sem("hn_turned")
        hnT_ready = sem("hnT_ready")
        routed = sem("routed")
        rl_ready = sem("rl_ready")

        def exists(m):
            return not isinstance(m, int) or 0 <= m < PAIRS

        def reused(m):
            return not isinstance(m, int) or m >= 2

        with nc.Block() as block:
            @block.sync
            def _(sp):
                sp.dma_start(wo[:, :, :], d["Wo"].rearrange("(k c) o -> c k o", k=2)).then_inc(w_in, 16)
                for n in range(3):
                    sp.dma_start(nw[32 * n:32 * n + 32, :], d["norm_weight"].rearrange("(n a) -> n a", a=1)).then_inc(w_in, 16)
                sp.dma_start(bo_row[:, :], d["bo"].rearrange("(a n) -> a n", a=1)).then_inc(w_in, 16)
                sp.dma_start(rw[:, :], d["router_w"]).then_inc(w_in, 16)
                sp.dma_start(pw[:, :], d["probe_w"]).then_inc(w_in, 16)
                sp.dma_start(emb[:, :], d["router_emb"]).then_inc(w_in, 16)
                sp.dma_start(bias8[:, 0, :], d["energy"].rearrange("(a n) -> a n", a=1)).then_inc(w_in, 16)
                sp.dma_start(bias8[:, 1, :], d["fatigue"].rearrange("(a n) -> a n", a=1)).then_inc(w_in, 16)

            @block.gpsimd
            def _(pool):
                def window(m, s, first=False):
                    if not first:
                        pool.wait_ge(mixed, m - 1)
                    view = HT[:, :, bass.ds(m * (2 * N), N + 64)]
                    pool.tensor_copy(hw[s][:, :, :].rearrange("c h (i t) -> c h i t", i=2),
                                     bass.AP(tensor=view.tensor, offset=view.offset,
                                             ap=[list(view.ap[0]), [TP, 2], [N, 2], [1, 64]])).then_inc(hw_ready, 1)

                window(0, 0, first=True)
                window(1, 1, first=True)
                with pool.Fori(0, PAIRS // 2 - 1) as t:
                    for e in range(2):
                        window(t * 2 + (e + 2), e)

            @block.vector
            def _(dve):
                dve.memset(eps[:, :], EPS).then_inc(eps_ready, 1)
                dve.memset(rl_row[:, :], 0.0).then_inc(step, 1)
                dve.wait_ge(w_in, 16 * 10)
                dve.tensor_tensor(emb2[:, :], emb[:, :], emb[:, :], ALU.mult).then_inc(step, 1)
                dve.wait_ge(step, 2)
                dve.tensor_reduce(gain[:, 0:1], emb2[:, :], AX.X, ALU.add).then_inc(step, 1)
                dve.tensor_scalar(wo[:, :, :], wo[:, :, :], nw[:, 0:1], 1.0 - LAMBDA_INIT, ALU.mult,
                                  ALU.mult).then_inc(wo_ready, 1)
                dve.tensor_scalar(bias8[:, 2, :], bias8[:, 1, :], 0.1, None, ALU.mult).then_inc(step, 1)
                dve.wait_ge(step, 4)
                dve.scalar_tensor_tensor(out=rl_row[:, 0:E], in0=bias8[:, 0, :], scalar=0.1, in1=bias8[:, 2, :],
                                         op0=ALU.mult, op1=ALU.subtract).then_inc(step, 1)
                dve.wait_ge(rooted, 2)
                dve.tensor_scalar(gain[:, 2:3], gain[:, 1:2], 1e-12, None, ALU.max).then_inc(step, 1)
                dve.wait_ge(step, 6)
                dve.reciprocal(gain[:, 2:3], gain[:, 2:3]).then_inc(step, 1)
                dve.tensor_scalar(gain[:, 3:4], gain[:, 1:2], 0.02 / O, 0.02 / O, ALU.mult, ALU.add).then_inc(step, 1)
                dve.wait_ge(step, 8)
                dve.tensor_scalar(embn[:, :], emb[:, :], gain[:, 2:3], None, ALU.mult).then_inc(step, 1)
                dve.tensor_scalar(rw[:, :], rw[:, :], gain[:, 3:4], None, ALU.add).then_inc(step, 1)
                dve.wait_ge(turned, 1)
                dve.tensor_copy(embT[:, :], psR[0][0:DR, 0:E]).then_inc(step, 1)
                dve.wait_ge(turned, 2)
                dve.tensor_copy(align[:, :], psR[1][0:E, 0:O]).then_inc(step, 1)
                dve.wait_ge(turned, 3)
                dve.tensor_copy(RW[:, :, :].rearrange("c k n -> c (k n)"), psR[0][0:HO, 0:2 * RC]).then_inc(step, 1)
                dve.reciprocal(rms[:, :], rms[:, :]).then_inc(step, 1)
                dve.wait_ge(step, 14)

                def normed(m, s):
                    if not exists(m):
                        return
                    if reused(m):
                        dve.wait_ge(o_turned, m - 1)
                    factor = rms[:, bass.ds(m * 6, 6)]
                    dve.tensor_tensor(on[s][:, :].rearrange("p (e v) -> p e v", e=6),
                                      H2[:, bass.ds(m * O, O)].rearrange("p (e v) -> p e v", e=6),
                                      bass.AP(tensor=factor.tensor, offset=factor.offset,
                                              ap=[list(factor.ap[0]), [1, 6], [0, 2 * HD]]), ALU.mult)\
                        .then_inc(on_ready, 1)

                def statistics(m, s):
                    if not exists(m):
                        return
                    dve.wait_ge(mixed, m + 1)
                    dve.bn_stats(st[s][:, :], psM[s][:, 0:O]).then_inc(stats_ready, 1)
                    dve.wait_ge(stats_ready, m + 1)
                    dve.sem_inc(stats_waited, 1)
                    dve.bn_aggr(mv[s][:, :], st[s][:, :]).then_inc(mv_ready, 1)

                def layer_norm(m, s):
                    if not exists(m):
                        return
                    dve.wait_ge(dev_ready, m + 1)
                    dve.reciprocal(rstd[s][:, :], dev[s][:, :]).then_inc(rstd_ready, 1)
                    dve.wait_ge(rstd_ready, m + 1)
                    if reused(m):
                        dve.wait_ge(hn_turned, m - 1)
                    dve.tensor_scalar(hn[s][:, :], psM[s][:, 0:O], mv[s][:, 0:1], rstd[s][:, 0:1],
                                      ALU.subtract, ALU.mult).then_inc(hn_ready, 1)

                def keep_rows(m, s):
                    if not exists(m):
                        return
                    dve.wait_ge(hn_ready, m + 1)
                    dve.tensor_scalar(H2[:, bass.ds(m * O, O)], hn[s][:, :], 1.0, None, ALU.mult)

                def keep_router(m, s):
                    if not exists(m):
                        return
                    dve.wait_ge(routed, m + 1)
                    dve.tensor_scalar(RL[:, bass.ds(m * RC, RC)], psR[s][:, 0:RC], 1.0, None, ALU.mult).then_inc(rl_ready, 1)

                def step_of(i, s):
                    layer_norm(i - 2, s)
                    normed(i + 1, 1 - s)
                    keep_rows(i - 2, s)
                    statistics(i - 1, 1 - s)
                    keep_router(i - 4, s)

                for i in range(-1, FIRST):
                    step_of(i, i % 2)
                with dve.Fori(0, (LAST - FIRST) // 2) as t:
                    for e in range(2):
                        step_of(t * 2 + (FIRST + e), e)
                for i in range(LAST, PAIRS + 4):
                    step_of(i, i % 2)

            @block.scalar
            def _(act):
                act.wait_ge(eps_ready, 1)
                act.activation(rms[:, :], SSQ[:, :], ACT.Sqrt, bias=eps[:, 0:1], scale=1.0 / (2 * HD)).then_inc(rooted, 1)
                act.wait_ge(step, 3)
                act.activation(gain[:, 1:2], gain[:, 0:1], ACT.Sqrt).then_inc(rooted, 1)

                def copy_oT(m, s):
                    if not exists(m):
                        return
                    act.wait_ge(o_turned, m + 1)
                    if reused(m):
                        act.wait_ge(mixed, m - 1)
                    act.activation(oT[s][:, :, :].rearrange("c k t -> c (k t)"), psO[s][0:HO, 0:256],
                                   ACT.Copy).then_inc(oT_ready, 1)

                def deviations(m, s):
                    if not exists(m):
                        return
                    act.wait_ge(mv_ready, m + 1)
                    if reused(m):
                        act.wait_ge(rstd_ready, m - 1)
                    act.activation(dev[s][:, :], mv[s][:, 1:2], ACT.Sqrt, bias=eps[:, 0:1]).then_inc(dev_ready, 1)

                def copy_hnT(m, s):
                    if not exists(m):
                        return
                    act.wait_ge(hn_turned, m + 1)
                    if reused(m):
                        act.wait_ge(routed, m - 1)
                    act.activation(hnT[s][:, :, :].rearrange("c k t -> c (k t)"), psN[s][0:HO, 0:256],
                                   ACT.Copy).then_inc(hnT_ready, 1)

                def step_of(i, s):
                    copy_oT(i, s)
                    copy_hnT(i - 3, 1 - s)
                    deviations(i - 1, 1 - s)

                for i in range(-1, FIRST):
                    step_of(i, i % 2)
                with act.Fori(0, (LAST - FIRST) // 2) as t:
                    for e in range(2):
                        step_of(t * 2 + (FIRST + e), e)
                for i in range(LAST, PAIRS + 4):
                    step_of(i, i % 2)

            @block.tensor
            def _(pe):
                pe.wait_ge(step, 10)
                pe.transpose(psR[0][0:DR, 0:E], embn[:, :], ident[0:E, 0:E]).then_inc(turned, 1)
                pe.wait_ge(step, 11)
                pe.matmul(psR[1][0:E, 0:O], embT[:, :], pw[:, :], start=True, stop=True).then_inc(turned, 1)
                pe.wait_ge(step, 12)
                for k in range(2):
                    for at, rows, w in ((0, E, rw), (E, E, align), (2 * E, DR, pw)):
                        last = pe.transpose(psR[0][0:HO, k * RC + at:k * RC + at + rows], w[:, k * HO:(k + 1) * HO],
                                            ident[0:rows, 0:rows])
                last.then_inc(turned, 1)
                pe.wait_ge(wo_ready, 1)

                def turn(m, src, psum, ready, copied, done):
                    if not exists(m):
                        return
                    pe.wait_ge(ready, m + 1)
                    if reused(m):
                        pe.wait_ge(copied, m - 1)
                    for k in range(2):
                        last = pe.transpose(psum[0:HO, k * 128:(k + 1) * 128], src[:, k * HO:(k + 1) * HO], ident[:, :])
                    last.then_inc(done, 1)

                def project(m, s):
                    if not exists(m):
                        return
                    pe.wait_ge(oT_ready, m + 1)
                    pe.wait_ge(hw_ready, m + 1)
                    if reused(m):
                        pe.wait_ge(hn_ready, m - 1)
                    for h in range(2):
                        half = slice(h * HO, (h + 1) * HO)
                        pe.matmul(psM[s][:, half], ones[0:1, 0:128], bo_row[:, half], start=True, stop=False)
                        for k in range(2):
                            pe.matmul(psM[s][:, half], oT[s][:, k, :], wo[:, k, half], start=False, stop=False)
                        last = pe.matmul(psM[s][:, half], hw[s][:, h, :], ident[0:HO, 0:HO], start=False, stop=True)
                    last.then_inc(mixed, 1)

                def route(m, s):
                    if not exists(m):
                        return
                    pe.wait_ge(hnT_ready, m + 1)
                    if reused(m):
                        pe.wait_ge(rl_ready, m - 1)
                    pe.matmul(psR[s][:, 0:RC], ones[0:1, 0:128], rl_row[:, :], start=True, stop=False)
                    for k in range(2):
                        last = pe.matmul(psR[s][:, 0:RC], hnT[s][:, k, :], RW[:, k, :], start=False, stop=(k == 1))
                    last.then_inc(routed, 1)

                def step_of(i, s):
                    turn(i, on[s], psO[s], on_ready, oT_ready, o_turned)
                    project(i - 1, 1 - s)
                    turn(i - 3, hn[1 - s], psN[1 - s], hn_ready, hnT_ready, hn_turned)
                    route(i - 4, s)

                pe.wait_ge(step, 13)
                for i in range(-1, FIRST):
                    step_of(i, i % 2)
                with pe.Fori(0, (LAST - FIRST) // 2) as t:
                    for e in range(2):
                        step_of(t * 2 + (FIRST + e), e)
                for i in range(LAST, PAIRS + 4):
                    step_of(i, i % 2)


def experts(nc, d, out, H2, W1, W2, RL, ident, ones):
    with ExitStack() as ctx:
        def sb(name, shape, dt=F32):
            return ctx.enter_context(nc.sbuf_tensor(name, shape, dt))

        def sem(name):
            return ctx.enter_context(nc.semaphore(name))

        def ps(name, banks):
            return ctx.enter_context(nc.psum_tensor(name, [128, banks * 512], F32))

        rl = RL[:, :].rearrange("p (m r) -> p m r", r=RC)
        valid = sb("valid", [128, 1])
        nowhere = sb("nowhere", [128, 1])
        below = sb("below", [128, 128])
        rank_i = sb("rank_i", [128, E], I32)
        rank_e = sb("rank_e", [128, E])
        tile_i = sb("tile_i", [1, TILES], I32)
        tile_f = sb("tile_f", [1, TILES])
        probe2 = sb("probe2", [128, PAIRS, DR])
        norm = sb("norm", [128, 2, PAIRS])
        logit = sb("logit", [128, PAIRS, E])
        cand = sb("cand", [128, PAIRS, E])
        best = sb("best", [128, 4, PAIRS])
        one_hot = [sb(f"one_hot{n}", [128, PAIRS, E]) for n in range(2)]
        gate = sb("gate", [128, 3, PAIRS])
        picked = sb("picked", [128, PAIRS, E])
        total = sb("total", [128, PAIRS, E])
        run = [sb(f"run{n}", [128, PAIRS, E]) for n in range(2)]
        count_i = sb("count_i", [128, E], I32)
        ends = [sb(f"ends{n}", [128, E]) for n in range(3)]
        slot = sb("slot", [128, 2, PAIRS])
        scat = sb("scat", [128, 2, PAIRS], U32)
        gath = sb("gath", [128, 2, PAIRS], U32)
        past = sb("past", [1, TILES, E])
        owner_f = sb("owner_f", [1, TILES])
        owner = sb("owner", [1, TILES], I32)
        b2_row = sb("b2_row", [1, E * O])
        xg = [sb(f"xg{s}", [RT, O]) for s in range(2)]
        xgT = [sb(f"xgT{s}", [HO + 1, 2, RT]) for s in range(2)]
        hid = [sb(f"hid{s}", [RT, H]) for s in range(2)]
        hidT = [sb(f"hidT{s}", [128, H // 128, RT]) for s in range(2)]
        yg = [sb(f"yg{s}", [RT, O]) for s in range(2)]
        back = [sb(f"back{s}", [128, O]) for s in range(YRING)]
        eps = sb("f_eps", [128, 1])
        st = sb("f_st", [128, PAIRS, 6])
        mv = sb("f_mv", [128, PAIRS, 2])
        dev = sb("f_dev", [128, PAIRS])
        rstd = sb("f_rstd", [128, PAIRS])

        psT = ps("f_psT", 1)
        psH = ps("f_psH", 2)
        psHT = ps("f_psHT", 2)
        psY = ps("f_psY", 1)
        psC = ps("f_psC", 2)

        const = sem("f_const")
        below_ready = sem("below_ready")
        b2_in = sem("b2_in")
        step = sem("f_step")
        rooted = sem("f_rooted")
        counted = sem("counted")
        slots_ready = sem("slots_ready")
        owner_ready = sem("owner_ready")
        scattered = sem("scattered")
        xg_in = [sem(f"xg_in{s}") for s in range(2)]
        xg_turned = sem("xg_turned")
        xgT_ready = sem("xgT_ready")
        hidden = sem("hidden")
        hid_ready = sem("hid_ready")
        hid_turned = sem("hid_turned")
        hidT_ready = sem("hidT_ready")
        y_done = sem("f_y_done")
        yg_ready = sem("yg_ready")
        y_stored = [sem(f"y_stored{s}") for s in range(2)]
        all_stored = sem("all_stored")
        back_in = [sem(f"back_in{s}") for s in range(YRING)]
        added = sem("added")
        final = sem("final")
        stored = sem("f_stored")

        with nc.Block() as block:
            @block.gpsimd
            def _(pool):
                pool.memset(below[:, :], 1.0).then_inc(below_ready, 1)
                pool.wait_ge(below_ready, 1)
                pool.affine_select(out=below[:, :], in_=below[:, :], compare_op=ALU.is_ge, fill=0.0, base=-1,
                                   pattern=[[1, 128]], channel_multiplier=-1).then_inc(below_ready, 1)
                pool.iota(rank_i[:, :], pattern=[[-1, E]], base=E, channel_multiplier=0).then_inc(const, 1)
                pool.iota(tile_i[:, :], pattern=[[1, TILES]], base=0, channel_multiplier=0).then_inc(const, 1)
                pool.wait_ge(slots_ready, 1)
                for m in range(PAIRS):
                    for n in range(2):
                        pool.indirect_dma_start(out=d["xg"], out_offset=bass.IndirectOffsetOnAxis(
                            ap=scat[:, n, m:m + 1], axis=0), in_=H2[:, m * O:(m + 1) * O], in_offset=None,
                            bounds_check=SLOTS - 1, oob_is_err=False).then_inc(scattered, 16)
                pool.wait_ge(all_stored, 1)
                for m in range(PAIRS):
                    for n in range(2):
                        q = 2 * m + n
                        if q >= YRING:
                            pool.wait_ge(added, q - YRING + 1)
                        pool.indirect_dma_start(out=back[q % YRING][:, :], out_offset=None, in_=d["yg"],
                                                in_offset=bass.IndirectOffsetOnAxis(ap=gath[:, n, m:m + 1], axis=0),
                                                bounds_check=SLOTS - 1, oob_is_err=False).then_inc(back_in[q % YRING], 16)

            @block.vector
            def _(dve):
                links = [0]

                def link(ins):
                    links[0] += 1
                    ins.then_inc(step, 1)
                    dve.wait_ge(step, links[0])

                def over_experts(view):
                    return strided(view, 0, [[1, PAIRS], [0, E]])

                def over_pairs(view):
                    return strided(view, 0, [[0, PAIRS], [1, E]])

                dve.memset(valid[:, :], 0.0)
                dve.memset(eps[:, :], EPS)
                for s in range(2):
                    dve.memset(xgT[s][HO:HO + 1, 0, :], 1.0)
                link(dve.memset(nowhere[:, :], float(4 * SLOTS)))
                for i in range(2):
                    dve.memset(valid[64 * i:64 * i + N, :], 1.0)
                    last = dve.memset(nowhere[64 * i:64 * i + N, :], 0.0)
                link(last)
                dve.wait_ge(const, 2)
                dve.tensor_copy(rank_e[:, :], rank_i[:, :])
                dve.tensor_copy(tile_f[:, :], tile_i[:, :])
                link(dve.tensor_tensor(probe2[:, :, :], rl[:, :, 2 * E:RC], rl[:, :, 2 * E:RC], ALU.mult))
                link(dve.tensor_reduce(norm[:, 0, :], probe2[:, :, :], AX.X, ALU.add))
                dve.wait_ge(rooted, 1)
                link(dve.tensor_scalar(norm[:, 1, :], norm[:, 1, :], 1e-12, None, ALU.max))
                link(dve.reciprocal(norm[:, 1, :], norm[:, 1, :]))
                link(dve.tensor_tensor(cand[:, :, :], rl[:, :, E:2 * E], over_experts(norm[:, 1, :]), ALU.mult))
                link(dve.scalar_tensor_tensor(out=logit[:, :, :], in0=cand[:, :, :], scalar=0.02, in1=rl[:, :, 0:E],
                                              op0=ALU.mult, op1=ALU.add))
                for n in range(2):
                    link(dve.tensor_reduce(best[:, n, :], logit[:, :, :], AX.X, ALU.max))
                    link(dve.tensor_tensor(cand[:, :, :], logit[:, :, :], over_experts(best[:, n, :]), ALU.is_equal))
                    link(dve.tensor_tensor(cand[:, :, :], cand[:, :, :], over_pairs(rank_e[:, :]), ALU.mult))
                    link(dve.tensor_reduce(best[:, 2 + n, :], cand[:, :, :], AX.X, ALU.max))
                    link(dve.tensor_tensor(one_hot[n][:, :, :], over_pairs(rank_e[:, :]), over_experts(best[:, 2 + n, :]),
                                           ALU.is_equal))
                    if n == 0:
                        link(dve.scalar_tensor_tensor(out=logit[:, :, :], in0=one_hot[0][:, :, :], scalar=-3e38,
                                                      in1=logit[:, :, :], op0=ALU.mult, op1=ALU.add))
                link(dve.tensor_tensor(picked[:, :, :], one_hot[0][:, :, :], one_hot[1][:, :, :], ALU.add))
                link(dve.tensor_scalar(picked[:, :, :], picked[:, :, :], valid[:, 0:1], None, ALU.mult))
                assert links[0] == PICKED
                link(dve.tensor_tensor(gate[:, 2, :], best[:, 1, :], best[:, 0, :], ALU.subtract))
                dve.wait_ge(counted, 1)
                link(dve.tensor_copy(total[:, :, :], psC[:, 512:512 + PAIRS * E].rearrange("p (m e) -> p m e", e=E)))
                src = total
                for n in range(5):
                    dst, reach = run[n % 2], 1 << n
                    dve.tensor_copy(dst[:, 0:reach, :], src[:, 0:reach, :])
                    link(dve.tensor_tensor(dst[:, reach:PAIRS, :], src[:, reach:PAIRS, :], src[:, 0:PAIRS - reach, :],
                                           ALU.add))
                    src = dst
                link(dve.tensor_scalar(count_i[:, :], src[:, PAIRS - 1, :], float(RT - 1), None, ALU.add))
                link(dve.tensor_scalar(count_i[:, :], count_i[:, :], RT.bit_length() - 1, None, ALU.arith_shift_right))
                link(dve.tensor_copy(ends[0][:, :], count_i[:, :]))
                link(dve.tensor_tensor(run[1 - 0][:, :, :], src[:, :, :], total[:, :, :], ALU.subtract))
                eat = ends[0]
                for n in range(3):
                    dst, reach = ends[1 + n % 2], 1 << n
                    dve.tensor_copy(dst[:, 0:reach], eat[:, 0:reach])
                    link(dve.tensor_tensor(dst[:, reach:E], eat[:, reach:E], eat[:, 0:E - reach], ALU.add))
                    eat = dst
                link(dve.tensor_tensor(ends[0][:, :], eat[:, :], ends[0][:, :], ALU.subtract))
                link(dve.tensor_scalar(ends[0][:, :], ends[0][:, :], float(RT), None, ALU.mult))
                link(dve.tensor_tensor(run[1][:, :, :], run[1][:, :, :], over_pairs(ends[0][:, :]), ALU.add))
                link(dve.tensor_tensor(run[1][:, :, :], run[1][:, :, :],
                                       psC[:, 0:PAIRS * E].rearrange("p (m e) -> p m e", e=E), ALU.add))
                for n in range(2):
                    link(dve.tensor_tensor(cand[:, :, :], run[1][:, :, :], one_hot[n][:, :, :], ALU.mult))
                    link(dve.tensor_reduce(slot[:, n, :], cand[:, :, :], AX.X, ALU.add))
                for n in range(2):
                    dve.tensor_scalar(scat[:, n, :], slot[:, n, :], valid[:, 0:1], nowhere[:, 0:1], ALU.mult, ALU.add)
                    last = dve.tensor_scalar(gath[:, n, :], slot[:, n, :], valid[:, 0:1], None, ALU.mult)
                last.then_inc(slots_ready, 1)
                link(dve.tensor_tensor(past[:, :, :], strided(tile_f[:, :], 0, [[1, TILES], [0, E]]),
                                       strided(eat[0:1, :], 0, [[0, TILES], [1, E]]), ALU.is_ge))
                link(dve.tensor_reduce(owner_f[:, :], past[:, :, :], AX.X, ALU.add))
                dve.tensor_scalar(owner[:, :], owner_f[:, :], float(E - 1), None, ALU.min).then_inc(owner_ready, 1)
                dve.wait_ge(rooted, 2)
                link(dve.tensor_scalar(gate[:, 0, :], gate[:, 2, :], 1.0, None, ALU.add))
                link(dve.reciprocal(gate[:, 0, :], gate[:, 0, :]))
                link(dve.tensor_tensor(gate[:, 1, :], gate[:, 2, :], gate[:, 0, :], ALU.mult))

                def rectify(j, s, first=False):
                    dve.wait_ge(hidden, j + 1)
                    if not first:
                        dve.wait_ge(hid_turned, j - 1)
                    dve.tensor_scalar(hid[s][:, :], psH[:, 0:H], 0.0, None, ALU.max).then_inc(hid_ready, 1)

                def keep(j, s, first=False):
                    dve.wait_ge(y_done, j + 1)
                    if not first:
                        dve.wait_ge(y_stored[s], stored_so_far(j, s))
                    dve.tensor_scalar(yg[s][:, :], psY[:, 0:O], 1.0, None, ALU.mult).then_inc(yg_ready, 1)

                def stored_so_far(j, s):
                    return j * 8 - 8 * s

                rectify(0, 0, first=True)
                rectify(1, 1, first=True)
                keep(0, 0, first=True)
                rectify(2, 0)
                keep(1, 1, first=True)
                with dve.Fori(0, (TILES - 4) // 2) as t:
                    for e in range(2):
                        rectify(t * 2 + (e + 3), 1 - e)
                        keep(t * 2 + (e + 2), e)
                for j in range(TILES - 2, TILES):
                    if j + 1 < TILES:
                        rectify(j + 1, (j + 1) % 2)
                    keep(j, j % 2)

                for m in range(PAIRS):
                    row = H2[:, m * O:(m + 1) * O]
                    for n in range(2):
                        q = 2 * m + n
                        dve.wait_ge(back_in[q % YRING], 16 * (q // YRING + 1))
                        if n == 1:
                            dve.wait_ge(added, q)
                        dve.scalar_tensor_tensor(out=row, in0=back[q % YRING][:, :], scalar=gate[:, n, m:m + 1],
                                                 in1=row, op0=ALU.mult, op1=ALU.add).then_inc(added, 1)
                    dve.wait_ge(added, 2 * m + 2)
                    last = dve.bn_stats(st[:, m, :], row)
                link(last)
                for m in range(PAIRS):
                    last = dve.bn_aggr(mv[:, m, :], st[:, m, :])
                link(last)
                assert links[0] == AGGREGATED
                dve.wait_ge(rooted, 3)
                link(dve.reciprocal(rstd[:, :], dev[:, :]))
                for m in range(PAIRS):
                    row = H2[:, m * O:(m + 1) * O]
                    dve.tensor_scalar(row, row, mv[:, m, 0:1], rstd[:, m:m + 1], ALU.subtract, ALU.mult).then_inc(final, 1)

            @block.scalar
            def _(act):
                act.wait_ge(step, 4)
                act.activation(norm[:, 1, :], norm[:, 0, :], ACT.Sqrt).then_inc(rooted, 1)
                act.wait_ge(step, PICKED + 1)
                act.activation(gate[:, 2, :], gate[:, 2, :], ACT.Exp).then_inc(rooted, 1)

                def copy_xgT(j, s, first=False):
                    act.wait_ge(xg_turned, j + 1)
                    if not first:
                        act.wait_ge(hidden, j - 1)
                    act.activation(xgT[s][0:HO, :, :].rearrange("c k t -> c (k t)"), psT[0:HO, 0:2 * RT],
                                   ACT.Copy).then_inc(xgT_ready, 1)

                def square(j, s, first=False):
                    act.wait_ge(hid_turned, j + 1)
                    if not first:
                        act.wait_ge(y_done, j - 1)
                    act.activation(hidT[s][:, :, :].rearrange("c b t -> c (b t)"), psHT[:, 0:H],
                                   ACT.Square).then_inc(hidT_ready, 1)

                copy_xgT(0, 0, first=True)
                copy_xgT(1, 1, first=True)
                square(0, 0, first=True)
                copy_xgT(2, 0)
                square(1, 1, first=True)
                with act.Fori(0, (TILES - 4) // 2) as t:
                    for e in range(2):
                        copy_xgT(t * 2 + (e + 3), 1 - e)
                        square(t * 2 + (e + 2), e)
                for j in range(TILES - 2, TILES):
                    if j + 1 < TILES:
                        copy_xgT(j + 1, (j + 1) % 2)
                    square(j, j % 2)
                act.wait_ge(step, AGGREGATED)
                act.activation(dev[:, :], mv[:, :, 1], ACT.Sqrt, bias=eps[:, 0:1]).then_inc(rooted, 1)

            @block.tensor
            def _(pe):
                flat = picked[:, :, :].rearrange("p m e -> p (m e)")
                pe.wait_ge(below_ready, 2)
                pe.wait_ge(step, PICKED)
                pe.matmul(psC[:, 0:PAIRS * E], below[:, :], flat, start=True, stop=True)
                pe.matmul(psC[:, 512:512 + PAIRS * E], ones[:, :], flat, start=True, stop=True).then_inc(counted, 1)
                pe.wait_ge(owner_ready, 1)
                pe.wait_ge(b2_in, 16)

                def expert_of(j):
                    return pe.value_load(owner[0:1, bass.ds(j, 1)], min_val=0, max_val=E - 1)

                def turn(j, s, first=False):
                    pe.wait_ge(xg_in[s], j * 8 + (16 - 8 * s))
                    if not first:
                        pe.wait_ge(xgT_ready, j)
                    for k in range(2):
                        last = pe.transpose(psT[0:HO, k * RT:(k + 1) * RT], xg[s][:, k * HO:(k + 1) * HO], ident[:, :])
                    last.then_inc(xg_turned, 1)

                def widen(j, s, first=False):
                    e = expert_of(j)
                    pe.wait_ge(xgT_ready, j + 1)
                    if not first:
                        pe.wait_ge(hid_ready, j)
                    for at, size in ((0, 512), (512, H - 512)):
                        for k in range(2):
                            rows = HO + 1 - k
                            last = pe.matmul(psH[:, at:at + size], xgT[s][0:rows, k, :],
                                             W1[0:rows, bass.ds(e * (2 * H) + (k * H + at), size)],
                                             start=(k == 0), stop=(k == 1))
                    last.then_inc(hidden, 1)

                def turn_hidden(j, s, first=False):
                    pe.wait_ge(hid_ready, j + 1)
                    if not first:
                        pe.wait_ge(hidT_ready, j)
                    for b in range(H // 128):
                        last = pe.transpose(psHT[:, b * RT:(b + 1) * RT], hid[s][:, b * 128:(b + 1) * 128], ident[:, :])
                    last.then_inc(hid_turned, 1)

                def narrow(j, s, first=False):
                    e = expert_of(j)
                    pe.wait_ge(hidT_ready, j + 1)
                    if not first:
                        pe.wait_ge(yg_ready, j)
                    pe.matmul(psY[:, 0:O], ones[0:1, 0:RT], b2_row[:, bass.ds(e * O, O)], start=True, stop=False)
                    for b in range(H // 128):
                        last = pe.matmul(psY[:, 0:O], hidT[s][:, b, :],
                                         W2[:, bass.ds(e * (H // 128 * O) + b * O, O)],
                                         start=False, stop=(b == H // 128 - 1))
                    last.then_inc(y_done, 1)

                turn(0, 0, first=True)
                turn(1, 1)
                widen(0, 0, first=True)
                turn_hidden(0, 0, first=True)
                widen(1, 1)
                narrow(0, 0, first=True)
                turn(2, 0)
                with pe.Fori(0, (TILES - 4) // 2) as t:
                    for e in range(2):
                        j, s = t * 2 + (e + 1), 1 - e
                        turn_hidden(j, s)
                        widen(j + 1, 1 - s)
                        narrow(j, s)
                        turn(j + 2, s)
                for j in range(TILES - 3, TILES):
                    turn_hidden(j, j % 2)
                    if j + 1 < TILES:
                        widen(j + 1, (j + 1) % 2)
                    narrow(j, j % 2)
                    if j + 2 < TILES:
                        turn(j + 2, j % 2)

            @block.sync
            def _(sp):
                sp.dma_start(b2_row[:, :], d["b2"].rearrange("(a e) o -> a (e o)", a=1)).then_inc(b2_in, 16)
                sp.wait_ge(scattered, 16 * 2 * PAIRS)

                def load(j, s, first=False):
                    if not first:
                        sp.wait_ge(xg_turned, j - 1)
                    sp.dma_start(xg[s][:, :], d["xg"][bass.ds(j * RT, RT), :]).then_inc(xg_in[s], 16)

                def store(j, s):
                    sp.wait_ge(yg_ready, j + 1)
                    sp.dma_start(d["yg"][bass.ds(j * RT, RT), :], yg[s][:, :]).then_inc(y_stored[s], 16)

                load(0, 0, first=True)
                load(1, 1, first=True)
                with sp.Fori(0, TILES // 2 - 1) as t:
                    for e in range(2):
                        load(t * 2 + (e + 2), e)
                        store(t * 2 + e, e)
                for j in range(TILES - 2, TILES):
                    store(j, j % 2)
                for s in range(2):
                    sp.wait_ge(y_stored[s], 16 * (TILES // 2))
                sp.sem_inc(all_stored, 1)
                rows = out.rearrange("(m i) n o -> i n m o", i=2)
                for m in range(0, PAIRS, 4):
                    sp.wait_ge(final, m + 4)
                    for i in range(2):
                        sp.dma_start(rows[i, :, m:m + 4, :],
                                     H2[64 * i:64 * i + N, m * O:(m + 4) * O].rearrange("p (m o) -> p m o", o=O))\
                            .then_inc(stored, 16)
                sp.wait_ge(stored, 16 * (PAIRS // 2))


def vit_kernel(nc, d, out):
    d["off_all"] = nc.dram_tensor("off_all", [G, STR, NP, 2 * K], F32, kind="Internal").ap()
    d["xg"] = nc.dram_tensor("xg_all", [SLOTS, O], F32, kind="Internal").ap()
    d["yg"] = nc.dram_tensor("yg_all", [SLOTS, O], F32, kind="Internal").ap()
    with ExitStack() as ctx:
        def sb(name, shape):
            return ctx.enter_context(nc.sbuf_tensor(name, shape, F32))

        ident = sb("ident", [128, 128])
        ones = sb("ones", [128, 128])
        HT = sb("HT", [HO, 2, TP])
        with nc.sbuf_tensor("dwT", [128, BLK, O], F32) as dwT, nc.sbuf_tensor("far", [1, 1], I32) as far:
            tokenizer(nc, d, HT, dwT, far, ident, ones)
            far_taps(nc, d, HT, dwT, far, ident, ones)
            batch_norm(nc, d, HT, HT)
        H2 = sb("H2", [128, PAIRS * O])
        SSQ = sb("SSQ", [128, PAIRS * 6])
        RL = sb("RL", [128, PAIRS * RC])
        W1 = sb("W1", [128, E * 2 * H])
        W2 = sb("W2", [128, E * H // 128 * O])
        attention(nc, d, HT, H2, SSQ, W1, W2, ident, ones)
        mix(nc, d, HT, H2, SSQ, RL, ident, ones)
        experts(nc, d, out, H2, W1, W2, RL, ident, ones)


_INS = ['x', 'L0_tok_offset_w', 'L0_tok_offset_b', 'L0_tok_dconv_w', 'L0_tok_bn_gamma', 'L0_tok_bn_beta', 'L0_attn_Wq', 'L0_attn_bq', 'L0_attn_Wk', 'L0_attn_bk', 'L0_attn_Wv', 'L0_attn_bv', 'L0_attn_Wo', 'L0_attn_bo', 'L0_attn_lambda_q1', 'L0_attn_lambda_k1', 'L0_attn_lambda_q2', 'L0_attn_lambda_k2', 'L0_attn_norm_weight', 'L0_ffn_router_w', 'L0_ffn_probe_w', 'L0_ffn_router_emb', 'L0_ffn_fatigue', 'L0_ffn_energy', 'L0_ffn_w_fast1', 'L0_ffn_w_slow1', 'L0_ffn_h_fast1', 'L0_ffn_m_gate1', 'L0_ffn_b1', 'L0_ffn_w_fast2', 'L0_ffn_w_slow2', 'L0_ffn_h_fast2', 'L0_ffn_m_gate2', 'L0_ffn_b2']
_OUT = (64, 49, 192)


def kernel(**inputs):
    import numpy as _np
    import concourse.bacc as _bacc
    from concourse import mybir as _mybir
    from concourse.bass_utils import run_bass_kernel_spmd as _run

    nc = _bacc.Bacc("TRN2", target_bir_lowering=False, num_devices=1)
    arrays, views = {}, {}
    for name in _INS:
        a = _np.ascontiguousarray(inputs[name])
        arrays[f"in_{name}"] = a
        short = name.replace("L0_tok_", "").replace("L0_attn_", "").replace("L0_ffn_", "")
        views[short] = nc.dram_tensor(f"in_{name}", a.shape, _mybir.dt.from_np(a.dtype), kind="ExternalInput").ap()
    out = nc.dram_tensor("out_0", _OUT, _mybir.dt.float32, kind="ExternalOutput").ap()
    vit_kernel(nc, views, out)
    r = _run(nc, [arrays], core_ids=[0])
    return r.results[0]["out_0"]
```

```python
from contextlib import ExitStack

import concourse.bass as bass
from concourse import mybir

F32 = mybir.dt.float32
I32 = mybir.dt.int32
U32 = mybir.dt.uint32
ALU = mybir.AluOpType
ACT = mybir.ActivationFunctionType
AX = mybir.AxisListType

B, C, IMG = 64, 3, 112
PT = 16
NP = IMG // PT
K = PT * PT
O = 192
HO = O // 2
BG = 16
STR = NP * BG
G = B // BG
U = G * NP
N = NP * NP
T = B * N
EPS = 1e-5
TP = T + 16
PAIRS = B // 2
FIRST_STEP, LAST_STEP = 4, PAIRS - 2
HD = 16
SCALE = HD ** -0.5
LAMBDA_INIT = 0.8
E, H, DR = 8, 768, 24
RC = 2 * E + DR
FIRST, LAST = 6, PAIRS - 2
RT = 128
TILES = -(-(2 * T) // RT) + E - 1
SLOTS = TILES * RT
HROW = O + 2
YG, YRING = 4, 3
ROWS = PAIRS * 128
FAR_ROW = 4 * ROWS
PICKED = 21
AGGREGATED = 50

R = 2
TAPS = 2 * R + 1
XR, XC = PT + 2 * R, IMG + 2 * R
FAR_ROWS = FAR_COLS = IMG
BLK = 2 * C
NPROD = TAPS * C
PRING = 8
BIAS_AFTER = 3
BUNCH = (2, 8)
XDMA = NP * C


def strided(view, offset, dims):
    return bass.AP(tensor=view.tensor, offset=view.offset + offset, ap=[list(view.ap[0])] + [list(d) for d in dims])


def tokenizer(nc, d, YT, dwT, far, ident, ones):
    with ExitStack() as ctx:
        def sb(name, shape, dt=F32):
            return ctx.enter_context(nc.sbuf_tensor(name, shape, dt))

        def sem(name):
            return ctx.enter_context(nc.semaphore(name))

        def ps(name, banks):
            return ctx.enter_context(nc.psum_tensor(name, [128, banks * 512], F32))

        xs = [sb(f"xs{s}", [STR, C, XR, XC]) for s in range(2)]
        prods = [sb(f"prod{s}", [STR, TAPS, K]) for s in range(PRING)]
        wts = [sb(f"wts{i}", [STR, TAPS, K]) for i in range(TAPS)]
        hats = [sb(f"hats{s}", [STR, 2, TAPS, K]) for s in range(2)]
        patch = [sb(f"patch{s}", [STR, C, K]) for s in range(2)]
        xT = [sb(f"xT{s}", [128, BLK, STR]) for s in range(2)]
        smpT = [sb(f"smpT{s}", [128, BLK, STR]) for s in range(2)]
        off = [sb(f"off{s}", [STR, 2, K]) for s in range(2)]
        owT = sb("owT", [128, BLK, 2, K])
        obias = sb("obias", [STR, 2 * K])
        tapb = sb("tapb", [STR, TAPS])
        reach = sb("reach", [STR, 1])
        beyond = sb("beyond", [STR, 2, 2, K], mybir.dt.bfloat16)
        excess = sb("excess", [STR, U])
        worst = sb("worst", [STR, 1])

        psT = ps("psT", 2)
        psO = ps("psO", 1)
        psS = ps("psS", 2)
        psX = [ps(f"psX{c}", 1) for c in range(C)]
        psW = psX[0]

        w_in = sem("w_in")
        w_turned = sem("w_turned")
        w_copied = sem("w_copied")
        consts = sem("consts")
        halo_zero = sem("halo_zero")
        xs_in = [sem(f"xs_in{s}") for s in range(2)]
        patch_ready = sem("patch_ready")
        patch_free = sem("patch_free")
        turned = sem("turned")
        xT_ready = sem("xT_ready")
        offs_done = sem("offs_done")
        off_copied = sem("off_copied")
        off_ready = sem("off_ready")
        px_ready = sem("px_ready")
        off_stored = [sem(f"off_stored{s}") for s in range(2)]
        dist_ready = sem("dist_ready")
        hats_ready = sem("hats_ready")
        wts_ready = sem("wts_ready")
        prod_made = sem("prod_made")
        prod_free = sem("prod_free")
        smp_ready = sem("smp_ready")
        y_done = sem("y_done")
        y_ready = sem("y_ready")
        checked = sem("checked")
        worst_ready = sem("worst_ready")
        worst_summed = sem("worst_summed")
        far_ready = sem("far_ready")

        psY = psT[:, 512 + 2 * STR:512 + 4 * STR]

        def block_cols(psum, blk, rows=128, cols=STR):
            at = blk * STR if blk < 4 else 512 + (blk - 4) * STR
            return psum[0:rows, at:at + cols]

        def two_banks(psum):
            return ((psum[:, 0:4 * STR].rearrange("p (b t) -> p b t", b=4), 0, 4),
                    (psum[:, 512:512 + 2 * STR].rearrange("p (b t) -> p b t", b=2), 4, 6))

        def frees_before(n):
            return n + 1 if n >= PRING else n + 1 + 2 * PRING - NPROD if n + PRING < NPROD else 1

        def product(n):
            i, c = divmod(n, C)
            pixels = strided(psX[c][0:STR, :], i * (PT + 2 * R), [[1, TAPS], [PT + 2 * R, PT], [1, PT]])
            shape = "p j (r w) -> p j r w"
            return nc.vector.tensor_tensor(prods[n % PRING][:, :, :].rearrange(shape, r=PT), pixels,
                                           wts[i][:, :, :].rearrange(shape, r=PT), ALU.mult)

        with nc.Block() as block:
            @block.sync
            def _(sp):
                for t in range(4):
                    raw = bass.AP(tensor=prods[t][:, :, :].tensor, offset=0, ap=[[TAPS * K, STR], [1, C * K]])
                    sp.dma_start(raw, d["offset_w"].rearrange("o c h w -> o (c h w)")[t * STR:(t + 1) * STR, :]).then_inc(w_in, 16)
                raw = bass.AP(tensor=prods[4][:, :, :].tensor, offset=0, ap=[[TAPS * K, 64], [1, C * K]])
                sp.dma_start(raw, d["offset_w"].rearrange("o c h w -> o (c h w)")[4 * STR:512, :]).then_inc(w_in, 16)
                for t in range(2):
                    raw = bass.AP(tensor=wts[t][:, :, :].tensor, offset=0, ap=[[TAPS * K, HO], [1, C * K]])
                    sp.dma_start(raw, d["dconv_w"].rearrange("o c h w -> o (c h w)")[t * HO:(t + 1) * HO, :]).then_inc(w_in, 16)
                sp.dma_start(obias[:, :], d["offset_b"].rearrange("(a n) -> a n", a=1).to_broadcast([STR, 2 * K])).then_inc(w_in, 16)

                def load_strips(g):
                    s = g % 2
                    images = d["x"][g * BG:(g + 1) * BG]
                    if g < 2:
                        sp.wait_ge(halo_zero, g + 1)
                    else:
                        done = (g - 1) * NP
                        sp.wait_ge(px_ready, C * done)
                        sp.wait_ge(patch_ready, done)
                    for q in range(NP):
                        r0, r1 = max(q * PT - R, 0), min((q + 1) * PT + R, IMG)
                        top = r0 - (q * PT - R)
                        for c in range(C):
                            sp.dma_start(xs[s][q * BG:(q + 1) * BG, c, top:top + r1 - r0, R:R + IMG],
                                         images[:, c, r0:r1, :]).then_inc(xs_in[s], 16)

                load_strips(0)
                load_strips(1)
                for u in range(U):
                    sp.wait_ge(off_ready, u + 1)
                    sp.dma_start(d["off_all"][u // NP, :, u % NP, :], off[u % 2][:, :, :].rearrange("p a k -> p (a k)"))\
                        .then_inc(off_stored[u % 2], 16)
                    if u % NP == 2 and NP < u < (G - 1) * NP:
                        load_strips(u // NP + 1)
                for s in range(2):
                    sp.wait_ge(off_stored[s], 16 * (U // 2))

            @block.gpsimd
            def _(pool):
                pool.memset(ident[:, :], 0.0).then_inc(consts, 1)
                pool.memset(ones[:, :], 1.0).then_inc(consts, 1)
                pool.memset(tapb[:, 0:1], float(R))
                pool.memset(reach[:, :], -2.0 * R)
                for j in range(1, TAPS):
                    last = pool.memset(tapb[:, j:j + 1], float(R - j))
                last.then_inc(consts, 1)
                pool.wait_ge(consts, 3)
                pool.affine_select(out=ident[:, :], in_=ident[:, :], compare_op=ALU.not_equal, fill=1.0, base=0,
                                   pattern=[[-1, 128]], channel_multiplier=1).then_inc(consts, 1)
                pool.wait_ge(w_in, 16 * 8)
                pool.wait_ge(w_copied, BLK + 3)

                def bias(u, s):
                    pool.wait_ge(off_copied, u + 1)
                    offs = off[s][:, :, :]
                    pool.tensor_tensor(offs, offs, obias[:, :].rearrange("p (k t) -> p t k", t=2), ALU.add)\
                        .then_inc(off_ready, 1)

                def weights(u, s, last=False):
                    pool.wait_ge(hats_ready, u + 1)
                    for i in range(TAPS):
                        pool.wait_ge(prod_made, u * NPROD + C * (i + 1))
                        pool.tensor_tensor(wts[i][:, :, :], strided(hats[s][:, :, :, :], i * K, [[0, TAPS], [1, K]]),
                                           hats[s][:, 1, :, :], ALU.mult).then_inc(wts_ready, 1)
                        if i == BIAS_AFTER and not last:
                            bias(u + 1, 1 - s)

                bias(0, 0)
                with pool.Fori(0, U // 2 - 1) as t:
                    for s in range(2):
                        weights(t * 2 + s, s)
                weights(U - 2, 0)
                weights(U - 1, 1, last=True)

            @block.vector
            def _(dve):
                for s in range(2):
                    dve.memset(xs[s][:, :, :, 0:R], 0.0)
                    dve.memset(xs[s][:, :, :, XC - R:XC], 0.0)
                    dve.memset(xs[s][0:BG, :, 0:R, R:R + IMG], 0.0)
                    dve.memset(xs[s][STR - BG:STR, :, XR - R:XR, R:R + IMG], 0.0).then_inc(halo_zero, 1)
                dve.memset(YT[:, :, T:TP], 0.0)
                dve.wait_ge(w_copied, BLK + 3)
                dve.sem_inc(prod_made, NPROD)

                with dve.Fori(0, U) as u:
                    for n in range(NPROD):
                        if n % C == 0:
                            dve.wait_ge(wts_ready, u * TAPS + (n // C + 1))
                        if n < C:
                            dve.wait_ge(px_ready, u * C + (n + 1))
                        dve.wait_ge(prod_free, u * NPROD + frees_before(n))
                        product(n).then_inc(prod_made, 1)
                dve.wait_ge(checked, U)
                dve.tensor_reduce(worst[:, :], excess[:, :], AX.X, ALU.max).then_inc(worst_ready, 1)
                dve.wait_ge(worst_summed, 1)
                dve.tensor_scalar(far[:, :], psT[0:1, 0:1], 0.0, None, ALU.is_gt).then_inc(far_ready, 1)
                dve.wait_ge(far_ready, 1)

            @block.scalar
            def _(act):
                for blk in range(BLK):
                    act.wait_ge(w_turned, blk + 1)
                    act.activation(owT[:, blk, :, :].rearrange("p t k -> p k t"),
                                   (psO if blk % 2 == 0 else psW)[:, 0:512].rearrange("p (k t) -> p k t", t=2),
                                   ACT.Copy).then_inc(w_copied, 1)
                for t in range(3):
                    act.wait_ge(w_turned, BLK + t + 1)
                    act.activation(dwT[:, 2 * t:2 * t + 2, :],
                                   (psO if t % 2 == 0 else psW)[:, 0:2 * O].rearrange("p (b o) -> p b o", b=2),
                                   ACT.Copy).then_inc(w_copied, 1)

                def copy_patch(u):
                    g, pw = divmod(u, NP)
                    act.wait_ge(xs_in[g % 2], 16 * XDMA * (g // 2 + 1))
                    act.wait_ge(patch_free, u + 1)
                    act.activation(patch[u % 2][:, :, :].rearrange("p c (r w) -> p c r w", r=PT),
                                   xs[g % 2][:, :, R:R + PT, R + pw * PT:R + (pw + 1) * PT],
                                   ACT.Copy).then_inc(patch_ready, 1)

                def copy_pixels(u, c):
                    g, pw = divmod(u, NP)
                    if u % NP == 0:
                        act.wait_ge(xs_in[g % 2], 16 * XDMA * (g // 2 + 1))
                    act.wait_ge(prod_made, NPROD * (u + 1) - (C - 1 - c))
                    act.activation(strided(psX[c][0:STR, :], 0, [[PT + 2 * R, PT + 2 * R], [1, PT + 2 * R]]),
                                   xs[g % 2][:, c, :, pw * PT:pw * PT + PT + 2 * R], ACT.Copy).then_inc(px_ready, 1)

                def copy_xT(u):
                    act.wait_ge(turned, u + 1)
                    if u >= 2:
                        act.wait_ge(offs_done, u - 1)
                    for view, a, b in two_banks(psT):
                        last = act.activation(xT[u % 2][:, a:b, :], view, ACT.Copy)
                    last.then_inc(xT_ready, 1)

                def copy_off(u):
                    act.wait_ge(offs_done, u + 1)
                    if u >= 2:
                        act.wait_ge(off_stored[u % 2], 16 * (u // 2))
                    act.activation(off[u % 2][:, :, :].rearrange("p a k -> p (a k)"), psO[0:STR, :],
                                   ACT.Copy).then_inc(off_copied, 1)

                def make_hats(u):
                    s = u % 2
                    act.wait_ge(off_ready, u + 1)
                    if u >= 2:
                        act.wait_ge(wts_ready, TAPS * (u - 1))
                    for j in range(TAPS):
                        last = act.activation(hats[s][:, :, j, :], off[s][:, :, :], ACT.Abs, bias=tapb[:, j:j + 1])
                    last.then_inc(dist_ready, 1)
                    act.wait_ge(dist_ready, u + 1)
                    if u >= 1:
                        act.wait_ge(checked, u)
                    act.activation(beyond[:, :, :, :],
                                   strided(hats[s][:, :, :, :], 0, [[TAPS * K, 2], [(TAPS - 1) * K, 2], [1, K]]),
                                   ACT.Relu, bias=reach[:, 0:1], accum_out=excess[:, u:u + 1]).then_inc(checked, 1)
                    act.wait_ge(checked, u + 1)
                    act.activation(hats[s][:, :, :, :], hats[s][:, :, :, :], ACT.Relu, bias=ones[0:STR, 0:1],
                                   scale=-1.0).then_inc(hats_ready, 1)

                def copy_sampled(u):
                    act.wait_ge(prod_free, PRING + NPROD * (u + 1))
                    if u >= 2:
                        act.wait_ge(y_done, u - 1)
                    for view, a, b in two_banks(psS):
                        last = act.activation(smpT[u % 2][:, a:b, :], view, ACT.Copy)
                    last.then_inc(smp_ready, 1)

                def copy_y(u):
                    g, pw = divmod(u, NP)
                    act.wait_ge(y_done, u + 1)
                    place = YT[:, :, g * BG * N:(g + 1) * BG * N]\
                        .rearrange("c h (b q w) -> c h q b w", b=BG, q=NP)[:, :, :, :, pw]
                    act.activation(place, psY[0:HO, :].rearrange("c (h q b) -> c h q b", h=2, q=NP),
                                   ACT.Copy).then_inc(y_ready, 1)

                act.wait_ge(consts, 4)
                act.sem_inc(y_ready, 1)
                copy_patch(0)
                copy_patch(1)
                for c in range(C):
                    copy_pixels(0, c)
                copy_xT(0)
                copy_xT(1)
                copy_patch(2)
                copy_off(0)
                make_hats(0)
                copy_off(1)
                copy_xT(2)
                copy_patch(3)
                make_hats(1)
                for u in range(U):
                    if u >= 1:
                        copy_y(u - 1)
                    if u + 2 < U:
                        copy_off(u + 2)
                    if u + 1 < U:
                        for c in range(C):
                            copy_pixels(u + 1, c)
                    copy_sampled(u)
                    if u + 3 < U:
                        copy_xT(u + 3)
                    if u + 2 < U:
                        make_hats(u + 2)
                    if u + 4 < U:
                        copy_patch(u + 4)
                copy_y(U - 1)

            @block.tensor
            def _(pe):
                pe.wait_ge(consts, 4)
                pe.wait_ge(w_in, 16 * 8)
                for blk in range(BLK):
                    if blk >= 2:
                        pe.wait_ge(w_copied, blk - 1)
                    for t in range(5):
                        rows = STR if t < 4 else 64
                        raw = bass.AP(tensor=prods[t][:, :, :].tensor, offset=blk * 128, ap=[[TAPS * K, rows], [1, 128]])
                        last = pe.transpose((psO if blk % 2 == 0 else psW)[:, t * STR:t * STR + rows], raw,
                                            ident[0:rows, 0:rows])
                    last.then_inc(w_turned, 1)
                for t in range(3):
                    pe.wait_ge(w_copied, BLK - 1 + t)
                    for b in range(2):
                        for h in range(2):
                            raw = bass.AP(tensor=wts[h][:, :, :].tensor, offset=(2 * t + b) * 128,
                                          ap=[[TAPS * K, HO], [1, 128]])
                            last = pe.transpose((psO if t % 2 == 0 else psW)[:, b * O + h * HO:b * O + (h + 1) * HO],
                                                raw, ident[0:HO, 0:HO])
                    last.then_inc(w_turned, 1)
                pe.wait_ge(w_copied, BLK + 3)
                pe.sem_inc(patch_free, 2)
                pe.sem_inc(prod_free, PRING)

                def turn_patch(u, s, first=False, outputs=None):
                    pe.wait_ge(patch_ready, u + 1)
                    if not first:
                        pe.wait_ge(xT_ready, u)
                    if outputs is not None:
                        pe.wait_ge(y_ready, outputs + 2)
                    for blk in range(BLK):
                        c, h = divmod(blk, 2)
                        last = pe.transpose(block_cols(psT, blk), patch[s][:, c, h * 128:(h + 1) * 128],
                                            ident[0:STR, 0:STR])
                    last.then_inc(turned, 1)
                    pe.wait_ge(turned, u + 1)
                    pe.sem_inc(patch_free, 1)

                def offsets(u, s, first=False):
                    pe.wait_ge(xT_ready, u + 1)
                    if not first:
                        pe.wait_ge(off_copied, u)
                    for blk in range(BLK):
                        last = pe.matmul(psO[0:STR, :], xT[s][:, blk, :],
                                         owT[:, blk, :, :].rearrange("p a k -> p (a k)"),
                                         start=(blk == 0), stop=(blk == BLK - 1))
                    last.then_inc(offs_done, 1)

                def sum_taps(u, products, bunch):
                    pe.wait_ge(prod_made, u * NPROD + (NPROD + bunch + 1))
                    if products[0] == 0 and not (isinstance(u, int) and u == 0):
                        pe.wait_ge(smp_ready, u)
                    for n in products:
                        pe.wait_ge(prod_made, u * NPROD + (NPROD + n + 1))
                        i, c = divmod(n, C)
                        for j in range(TAPS):
                            for h in range(2):
                                blk = 2 * c + h
                                last = pe.matmul(block_cols(psS, blk), prods[n % PRING][:, j, h * 128:(h + 1) * 128],
                                                 ident[0:STR, 0:STR], is_transpose=True,
                                                 start=(i == 0 and j == 0 and blk in (0, 4)),
                                                 stop=(i == TAPS - 1 and j == TAPS - 1), skip_group_check=True)
                        last.then_inc(prod_free, 1)

                def project(u, s, xT_before):
                    pe.wait_ge(smp_ready, u + 1)
                    pe.wait_ge(y_ready, u + 1)
                    pe.wait_ge(xT_ready, xT_before)
                    for h in range(2):
                        for blk in range(BLK):
                            last = pe.matmul(psY[0:HO, h * STR:(h + 1) * STR], dwT[:, blk, h * HO:(h + 1) * HO],
                                             smpT[s][:, blk, :], start=(blk == 0), stop=(blk == BLK - 1))
                    last.then_inc(y_done, 1)

                half = NPROD // 2 + 1
                turn_patch(0, 0, first=True)
                turn_patch(1, 1)
                offsets(0, 0, first=True)
                offsets(1, 1)
                turn_patch(2, 0)
                sum_taps(0, range(half), BUNCH[0])
                offsets(2, 0)
                sum_taps(0, range(half, NPROD), BUNCH[1])
                turn_patch(3, 1)
                with pe.Fori(0, (U - 4) // 2) as m:
                    for e in range(1, 3):
                        u, s = m * 2 + e, e % 2
                        sum_taps(u, range(half), BUNCH[0])
                        offsets(u + 2, s)
                        project(u - 1, 1 - s, u + 3)
                        sum_taps(u, range(half, NPROD), BUNCH[1])
                        turn_patch(u + 3, 1 - s, outputs=u - 1)
                for u in range(U - 3, U):
                    sum_taps(u, range(half), BUNCH[0])
                    if u + 2 < U:
                        offsets(u + 2, u % 2)
                    project(u - 1, (u - 1) % 2, min(u + 3, U))
                    sum_taps(u, range(half, NPROD), BUNCH[1])
                    if u + 3 < U:
                        turn_patch(u + 3, (u + 3) % 2, outputs=u - 1)
                project(U - 1, (U - 1) % 2, U)
                pe.wait_ge(worst_ready, 1)
                pe.matmul(psT[0:1, 0:1], worst[:, 0:1], ones[0:STR, 0:1], start=True, stop=True).then_inc(worst_summed, 1)


def far_taps(nc, d, YT, dwT, far, ident, ones):
    with ExitStack() as ctx:
        def sb(name, shape, dt=F32):
            return ctx.enter_context(nc.sbuf_tensor(name, shape, dt))

        def sem(name):
            return ctx.enter_context(nc.semaphore(name))

        image = sb("image", [STR, IMG * IMG])
        off = sb("far_off", [STR, NP, 2, K])
        pos = sb("pos", [STR, 2, NP, K])
        base_i = sb("base_i", [STR, 2, NP, K], I32)
        strip_i = sb("strip_i", [STR, 1], I32)
        strip_y = sb("strip_y", [STR, 1])
        base = sb("base", [STR, 2, NP, K])
        tap = sb("tap", [STR, 2])
        dist = sb("far_dist", [STR, NP * K])
        row_w = sb("row_w", [STR, NP * K])
        tap_w = sb("tap_w", [STR, NP * K])
        smp = [sb(f"smp{c}", [STR, NP * K]) for c in range(C)]
        smpT = sb("far_smpT", [128, BLK, STR])
        psT = ctx.enter_context(nc.psum_tensor("far_psT", [128, 1024], F32))
        psY = ctx.enter_context(nc.psum_tensor("far_psY", [128, 512], F32))

        grid = sem("far_grid")
        off_in = sem("far_off_in")
        image_in = sem("image_in")
        off_read = sem("far_off_read")
        image_read = sem("image_read")
        setup = sem("far_setup")
        group_ready = sem("group_ready")
        turned = sem("far_turned")
        smpT_ready = sem("far_smpT_ready")
        y_done = sem("far_y_done")
        y_ready = sem("far_y_ready")

        def is_far(eng):
            return eng.value_load(far[0:1, 0:1], min_val=0, max_val=1) > 0

        with nc.Block() as block:
            @block.sync
            def _(sp):
                with sp.If(is_far(sp)):
                    for g in range(G):
                        if g >= 1:
                            sp.wait_ge(off_read, g)
                        sp.dma_start(off[:, :, :, :].rearrange("p w a k -> p (w a k)"),
                                     d["off_all"][g].rearrange("p w k -> p (w k)")).then_inc(off_in, 16)
                        for c in range(C):
                            if g + c >= 1:
                                sp.wait_ge(image_read, g * C + c)
                            for q in range(NP):
                                sp.dma_start(image[q * BG:(q + 1) * BG, :],
                                             d["x"][g * BG:(g + 1) * BG, c].rearrange("b h w -> b (h w)"))\
                                    .then_inc(image_in, 16)

            @block.gpsimd
            def _(pool):
                with pool.If(is_far(pool)):
                    pool.iota(strip_i[:, :], pattern=[[0, 1]], base=0, channel_multiplier=1)
                    pool.iota(base_i[:, 0, :, :], pattern=[[0, NP], [1, PT], [0, PT]], base=0, channel_multiplier=0)
                    pool.iota(base_i[:, 1, :, :], pattern=[[PT, NP], [0, PT], [1, PT]], base=0,
                              channel_multiplier=0).then_inc(grid, 1)

            @block.vector
            def _(dve):
                with dve.If(is_far(dve)):
                    dve.wait_ge(grid, 1)
                    dve.tensor_scalar(strip_i[:, :], strip_i[:, :], -PT, None, ALU.bitwise_and).then_inc(setup, 1)
                    dve.wait_ge(setup, 1)
                    dve.tensor_copy(strip_y[:, :], strip_i[:, :])
                    dve.tensor_copy(base[:, :, :, :], base_i[:, :, :, :]).then_inc(setup, 1)
                    dve.wait_ge(setup, 2)
                    dve.tensor_scalar(base[:, 0, :, :], base[:, 0, :, :], strip_y[:, 0:1], None, ALU.add)\
                        .then_inc(setup, 1)
                    dve.wait_ge(setup, 3)
                    with dve.Fori(0, G) as g:
                        dve.wait_ge(off_in, (g + 1) * 16)
                        dve.tensor_tensor(pos[:, :, :, :], base[:, :, :, :],
                                          off[:, :, :, :].rearrange("p w a k -> p a w k"), ALU.add).then_inc(off_read, 1)
                        for c in range(C):
                            dve.wait_ge(image_in, g * (16 * NP * C) + 16 * NP * (c + 1))
                            dve.memset(smp[c][:, :], 0.0)
                            dve.memset(tap[:, 0:1], 0.0)
                            dve.drain()
                            with dve.Fori(0, FAR_ROWS) as y:
                                dve.tensor_scalar(tap_w[:, :], pos[:, 0, :, :].rearrange("p w k -> p (w k)"), tap[:, 0:1],
                                                  None, ALU.subtract)
                                dve.drain()
                                dve.scalar_tensor_tensor(out=dist[:, :], in0=tap_w[:, :], scalar=-1.0,
                                                         in1=tap_w[:, :], op0=ALU.mult, op1=ALU.max)
                                dve.drain()
                                dve.tensor_scalar(dist[:, :], dist[:, :], -1.0, 1.0, ALU.mult, ALU.add)
                                dve.memset(tap[:, 1:2], 0.0)
                                dve.drain()
                                dve.tensor_scalar(row_w[:, :], dist[:, :], 0.0, None, ALU.max)
                                dve.drain()
                                with dve.Fori(0, FAR_COLS) as x:
                                    dve.tensor_scalar(tap_w[:, :], pos[:, 1, :, :].rearrange("p w k -> p (w k)"),
                                                      tap[:, 1:2], None, ALU.subtract)
                                    dve.drain()
                                    dve.scalar_tensor_tensor(out=dist[:, :], in0=tap_w[:, :], scalar=-1.0,
                                                             in1=tap_w[:, :], op0=ALU.mult, op1=ALU.max)
                                    dve.drain()
                                    dve.tensor_scalar(dist[:, :], dist[:, :], -1.0, 1.0, ALU.mult, ALU.add)
                                    dve.tensor_scalar(tap[:, 1:2], tap[:, 1:2], 1.0, None, ALU.add)
                                    dve.drain()
                                    dve.scalar_tensor_tensor(out=tap_w[:, :], in0=dist[:, :], scalar=0.0,
                                                             in1=row_w[:, :], op0=ALU.max, op1=ALU.mult)
                                    dve.drain()
                                    dve.scalar_tensor_tensor(out=smp[c][:, :], in0=tap_w[:, :],
                                                             scalar=image[:, bass.ds(y * IMG + x, 1)],
                                                             in1=smp[c][:, :], op0=ALU.mult, op1=ALU.add)
                                    dve.drain()
                                dve.tensor_scalar(tap[:, 0:1], tap[:, 0:1], 1.0, None, ALU.add)
                                dve.drain()
                            dve.sem_inc(image_read, 1)
                        dve.sem_inc(group_ready, 1)
                        for pw in range(NP):
                            dve.wait_ge(y_done, g * NP + (pw + 1))
                            place = YT[:, :, bass.ds(g * (BG * N), BG * N)]\
                                .rearrange("c h (b q w) -> c h q b w", b=BG, q=NP)[:, :, :, :, pw]
                            dve.tensor_scalar(place, psY[0:HO, 0:2 * STR].rearrange("c (h q b) -> c h q b", h=2, q=NP),
                                              1.0, None, ALU.mult).then_inc(y_ready, 1)

            @block.scalar
            def _(act):
                with act.If(is_far(act)):
                    with act.Fori(0, U) as u:
                        act.wait_ge(turned, u + 1)
                        for a, b, at in ((0, 4, 0), (4, 6, 512)):
                            last = act.activation(smpT[:, a:b, :], psT[:, at:at + (b - a) * STR]
                                                  .rearrange("p (b t) -> p b t", t=STR), ACT.Copy)
                        last.then_inc(smpT_ready, 1)

            @block.tensor
            def _(pe):
                with pe.If(is_far(pe)):
                    pe.sem_inc(y_ready, 1)
                    with pe.Fori(0, G) as g:
                        pe.wait_ge(group_ready, g + 1)
                        for pw in range(NP):
                            pe.wait_ge(y_ready, g * NP + (pw + 1))
                            for blk in range(BLK):
                                c, h = divmod(blk, 2)
                                at = blk * STR if blk < 4 else 512 + (blk - 4) * STR
                                last = pe.transpose(psT[:, at:at + STR],
                                                    smp[c][:, pw * K + h * 128:pw * K + (h + 1) * 128],
                                                    ident[0:STR, 0:STR])
                            last.then_inc(turned, 1)
                            pe.wait_ge(smpT_ready, g * NP + (pw + 1))
                            for h in range(2):
                                for blk in range(BLK):
                                    last = pe.matmul(psY[0:HO, h * STR:(h + 1) * STR], dwT[:, blk, h * HO:(h + 1) * HO],
                                                     smpT[:, blk, :], start=(blk == 0), stop=(blk == BLK - 1))
                            last.then_inc(y_done, 1)


def batch_norm(nc, d, YT, HT):
    with ExitStack() as ctx:
        def sb(name, shape, dt=F32):
            return ctx.enter_context(nc.sbuf_tensor(name, shape, dt))

        def sem(name):
            return ctx.enter_context(nc.semaphore(name))

        gb = sb("bn_gb", [HO, 2, 2])
        st = sb("bn_st", [HO, 2, NP, 6])
        mv = sb("bn_mv", [HO, 2, 2])
        aff = sb("bn_aff", [HO, 2, 2])
        tmp = sb("bn_tmp", [HO, 2])
        dev = sb("bn_dev", [HO, 2])
        gb_in = sem("bn_gb_in")
        step = sem("bn_step")
        rooted = sem("bn_rooted")
        h_ready = sem("h_ready")

        with nc.Block() as block:
            @block.sync
            def _(sp):
                for n, w in enumerate(("bn_gamma", "bn_beta")):
                    sp.dma_start(gb[:, n, :], d[w].rearrange("(h c) -> c h", h=2),
                                 allow_slow_non_contiguous=True).then_inc(gb_in, 16)

            @block.vector
            def _(dve):
                for h in range(2):
                    for q in range(NP):
                        last = dve.bn_stats(st[:, h, q, :], YT[:, h, q * (T // NP):(q + 1) * (T // NP)])
                last.then_inc(step, 1)
                dve.wait_ge(step, 1)
                for h in range(2):
                    last = dve.bn_aggr(mv[:, h, :], st[:, h, :, :].rearrange("c q s -> c (q s)"))
                last.then_inc(step, 1)
                dve.wait_ge(step, 2)
                dve.tensor_scalar(tmp[:, :], mv[:, :, 1], EPS, None, ALU.add).then_inc(step, 1)
                dve.wait_ge(rooted, 1)
                dve.reciprocal(tmp[:, :], dev[:, :]).then_inc(step, 1)
                dve.wait_ge(step, 4)
                dve.wait_ge(gb_in, 32)
                dve.tensor_tensor(aff[:, 0, :], tmp[:, :], gb[:, 0, :], ALU.mult).then_inc(step, 1)
                dve.wait_ge(step, 5)
                dve.tensor_tensor(tmp[:, :], mv[:, :, 0], aff[:, 0, :], ALU.mult).then_inc(step, 1)
                dve.wait_ge(step, 6)
                dve.tensor_tensor(aff[:, 1, :], gb[:, 1, :], tmp[:, :], ALU.subtract).then_inc(step, 1)

            @block.scalar
            def _(act):
                act.wait_ge(step, 3)
                act.activation(dev[:, :], tmp[:, :], ACT.Sqrt).then_inc(rooted, 1)
                act.wait_ge(step, 7)
                for h in range(2):
                    act.activation(HT[:, h, 0:T], YT[:, h, 0:T], ACT.Gelu, bias=aff[:, 1, h:h + 1],
                                   scale=aff[:, 0, h:h + 1]).then_inc(h_ready, 1)


def attention(nc, d, HT, OUTS, SSQ, W1, W2, ident, ones):
    with ExitStack() as ctx:
        def sb(name, shape, dt=F32):
            return ctx.enter_context(nc.sbuf_tensor(name, shape, dt))

        def sem(name):
            return ctx.enter_context(nc.semaphore(name))

        def ps(name, banks):
            return ctx.enter_context(nc.psum_tensor(name, [128, banks * 512], F32))

        wqkv = sb("wqkv", [HO, 3, 2, O])
        qk_bias = sb("qk_bias", [HO, 2, 2])
        q_bias = sb("q_bias", [HO, 2])
        bv_row = sb("bv_row", [1, O])
        bv_all = sb("bv_all", [128, O // 2])
        lam_in = sb("lam_in", [1, 4, HD])
        lam_pr = sb("lam_pr", [1, 2, HD])
        lam_sum = sb("lam_sum", [1, 2])
        lam_exp = sb("lam_exp", [1, 2])
        neg_lam = sb("neg_lam", [1, 1])
        head_sign = sb("head_sign", [128, 6, 2])
        head_mask = sb("head_mask", [HO, 6])
        kx_bias = sb("kx_bias", [HO, 2, 6])
        hp = [sb(f"hp{s}", [HO, 2, 128]) for s in range(2)]
        qT = [sb(f"qT{s}", [HO, 2, 128]) for s in range(2)]
        kx = [sb(f"kx{s}", [HO, 2, 2, 6, N]) for s in range(2)]
        vals = [sb(f"vals{s}", [128, 2, O // 2]) for s in range(2)]
        top = [sb(f"top{s}", [128, 12]) for s in range(2)]
        den = [sb(f"den{s}", [128, 12]) for s in range(2)]
        coef = [sb(f"coef{s}", [128, 12]) for s in range(2)]
        ex = [sb(f"ex{s}", [128, 12, N]) for s in range(2)]
        pm = [sb(f"pm{s}", [128, 2, 6, 64]) for s in range(2)]
        dT = [sb(f"dT{s}", [128, 3, 128]) for s in range(2)]
        sq = [sb(f"sq{s}", [128, O]) for s in range(2)]
        ssq = [sb(f"ssq{s}", [128, 6]) for s in range(2)]

        stage = [sb(f"stage_{n}", [128, 2 * H]) for n in ("fast", "slow", "h")]
        zero = sb("zero", [128, HROW])
        gates_row = sb("gates_row", [1, 2, E])
        gates = sb("gates", [128, 2, E])

        psQ = ps("psQ", 1)
        psK = ps("psK", 1)
        psV = ps("psV", 1)
        psA = ps("psA", 2)
        psD = ps("psD", 1)
        psX = ps("psX", 2)

        w_in = sem("a_w_in")
        b1_in = sem("b1_in")
        zero_ready = sem("zero_ready")
        slots_zero = sem("slots_zero")
        stage_in = sem("stage_in")
        stage_free = sem("stage_free")
        stage_step = sem("stage_step")
        stage_taken = sem("stage_taken")
        setup = sem("a_setup")
        mask_ready = sem("mask_ready")
        lam_ready = sem("lam_ready")
        lam_expd = sem("lam_expd")
        spread = sem("a_spread")
        hp_ready = sem("hp_ready")
        q_done = sem("q_done")
        k_done = sem("k_done")
        kx_ready = sem("kx_ready")
        v_done = sem("v_done")
        q_ready = sem("q_ready")
        v_ready = sem("v_ready")
        scored = sem("scored")
        top_ready = sem("top_ready")
        shifted = sem("shifted")
        exped = sem("exped")
        den_ready = sem("den_ready")
        coef_ready = sem("coef_ready")
        pm_ready = sem("pm_ready")
        diffed = sem("diffed")
        dT_ready = sem("dT_ready")
        weighing = sem("weighing")
        av_done = sem("av_done")
        sq_ready = sem("sq_ready")
        ssq_ready = sem("ssq_ready")
        out_ready = sem("out_ready")

        def paired(psum):
            return psum[:, :].rearrange("p (b c) -> p b c", b=2)[:, :, 0:6 * N].rearrange("p b (h k) -> p b h k", k=N)

        def by_head(tile):
            return strided(tile[:, :], 0, [[6, 2], [1, 6], [0, N]])

        def head_order(psum):
            return psum[:, :].rearrange("p (g c) -> p g c", g=2)[:, :, 0:O // 2].rearrange("p g (f v) -> p f g v", f=3)

        def exists(m):
            return not isinstance(m, int) or 0 <= m < PAIRS

        def reused(m):
            return not isinstance(m, int) or m >= 2

        def another(m):
            return not isinstance(m, int) or m >= 1

        with nc.Block() as block:
            @block.sync
            def _(sp):
                for n, w in enumerate(("Wq", "Wk", "Wv")):
                    sp.dma_start(wqkv[:, n, :, :], d[w].rearrange("(k c) o -> c k o", k=2)).then_inc(w_in, 16)
                for n, w in enumerate(("bq", "bk")):
                    sp.dma_start(qk_bias[:, n, :], d[w].rearrange("(h c) -> c h", h=2),
                                 allow_slow_non_contiguous=True).then_inc(w_in, 16)
                sp.dma_start(bv_row[:, :], d["bv"].rearrange("(a n) -> a n", a=1)).then_inc(w_in, 16)
                for n, w in enumerate(("lambda_q1", "lambda_q2", "lambda_k1", "lambda_k2")):
                    sp.dma_start(lam_in[:, n, :], d[w].rearrange("(a n) -> a n", a=1)).then_inc(w_in, 16)
                for n, w in enumerate(("m_gate1", "m_gate2")):
                    sp.dma_start(gates_row[:, n, :], d[w].rearrange("(a n) -> a n", a=1)).then_inc(w_in, 16)
                sp.dma_start(W1[HO:HO + 1, :].rearrange("a (e k h) -> a e k h", e=E, k=2)[:, :, 0, :],
                             d["b1"].rearrange("(a e) h -> a e h", a=1)).then_inc(b1_in, 16)
                sp.wait_ge(zero_ready, 1)
                sp.dma_start(d["xg"].rearrange("(p t) o -> p t o", p=128), strided(zero[:, :], 0, [[0, TILES], [1, HROW]]))\
                    .then_inc(slots_zero, 16)
                with sp.Fori(0, E) as e:
                    for n in range(2):
                        sp.wait_ge(stage_free, e * 2 + (n + 1))
                        for t, w in enumerate(("w_fast", "w_slow", "h_fast")):
                            src = d[w + "12"[n]].rearrange("e r c -> (e r) c")
                            if n == 0:
                                sp.dma_start(stage[t][0:HO, :].rearrange("c (k h) -> c k h", k=2),
                                             src[bass.ds(e * O, O), :].rearrange("(k c) h -> c k h", k=2))\
                                    .then_inc(stage_in, 16)
                            else:
                                sp.dma_start(stage[t][:, 0:H // 128 * O].rearrange("p (b o) -> p b o", o=O),
                                             src[bass.ds(e * H, H), :].rearrange("(b p) o -> p b o", p=128))\
                                    .then_inc(stage_in, 16)
                sp.wait_ge(b1_in, 16)
                sp.wait_ge(slots_zero, 16)

            @block.gpsimd
            def _(pool):
                pool.memset(head_mask[:, :], 1.0).then_inc(mask_ready, 1)
                pool.wait_ge(mask_ready, 1)
                pool.affine_select(out=head_mask[:, :], in_=head_mask[:, :], compare_op=ALU.is_ge, fill=0.0, base=0,
                                   pattern=[[-HD, 6]], channel_multiplier=1).then_inc(mask_ready, 1)
                pool.wait_ge(mask_ready, 2)
                pool.affine_select(out=head_mask[:, :], in_=head_mask[:, :], compare_op=ALU.is_ge, fill=0.0,
                                   base=HD - 1, pattern=[[HD, 6]], channel_multiplier=-1).then_inc(mask_ready, 1)
                pool.wait_ge(mask_ready, 3)

                def window(m, s):
                    if reused(m):
                        pool.wait_ge(v_done, m - 1)
                    view = HT[:, :, bass.ds(m * (2 * N), N + 64)]
                    pool.tensor_copy(hp[s][:, :, :].rearrange("c h (i t) -> c h i t", i=2),
                                     bass.AP(tensor=view.tensor, offset=view.offset,
                                             ap=[list(view.ap[0]), [TP, 2], [N, 2], [1, 64]])).then_inc(hp_ready, 1)

                window(0, 0)
                window(1, 1)

                def put_together(e, n, part):
                    rows, width, W = (HO, 2 * H, W1) if n == 0 else (128, H // 128 * O, W2)
                    at, size = part * (width // 2), width // 2
                    fast, slow, h = (t[0:rows, at:at + size] for t in stage)
                    dst = W[0:rows, bass.ds(e * width + at, size)]
                    gate = gates[0:rows, n, bass.ds(e, 1)]
                    steps = e * 12 + (6 * n + 3 * part)
                    pool.wait_ge(stage_in, e * (16 * 6) + 48 * (n + 1))
                    pool.sem_inc(stage_taken, 1)
                    pool.tensor_tensor(slow, slow, bass.AP(tensor=gate.tensor, offset=gate.offset,
                                                           ap=[list(gate.ap[0]), [0, size]]), ALU.mult)\
                        .then_inc(stage_step, 1)
                    pool.wait_ge(stage_step, steps + 1)
                    pool.tensor_tensor(slow, slow, fast, ALU.add).then_inc(stage_step, 1)
                    pool.wait_ge(stage_step, steps + 2)
                    pool.sem_inc(stage_taken, 1)
                    pool.tensor_tensor(dst, slow, h, ALU.add).then_inc(stage_step, 1)
                    if part == 1:
                        pool.wait_ge(stage_step, steps + 3)
                        pool.sem_inc(stage_free, 1)

                pool.wait_ge(setup, 6)
                pool.sem_inc(stage_free, 1)
                with pool.Fori(0, E - 1) as e:
                    for q in range(4):
                        window(e * 4 + (q + 2), q % 2)
                        put_together(e, q // 2, q % 2)
                for m in range(PAIRS - 2, PAIRS):
                    window(m, m % 2)
                for q in range(4):
                    put_together(E - 1, q // 2, q % 2)

            @block.vector
            def _(dve):
                dve.memset(zero[:, :], 0.0).then_inc(zero_ready, 1)
                for s in range(2):
                    last = dve.memset(pm[s][:, :, :, N:64], 0.0)
                dve.memset(head_sign[:, :, 0], 1.0).then_inc(setup, 1)
                dve.wait_ge(w_in, 16 * 12)
                dve.tensor_scalar(q_bias[:, :], qk_bias[:, 0, :], SCALE, None, ALU.mult).then_inc(setup, 1)
                dve.tensor_tensor(lam_pr[:, :, :], lam_in[:, 0:2, :], lam_in[:, 2:4, :], ALU.mult).then_inc(lam_ready, 1)
                dve.wait_ge(lam_ready, 1)
                dve.tensor_reduce(lam_sum[:, :], lam_pr[:, :, :], AX.X, ALU.add).then_inc(lam_ready, 1)
                dve.wait_ge(lam_expd, 1)
                dve.scalar_tensor_tensor(out=neg_lam[:, :], in0=lam_exp[:, 1:2], scalar=LAMBDA_INIT,
                                         in1=lam_exp[:, 0:1], op0=ALU.subtract, op1=ALU.subtract).then_inc(lam_ready, 1)
                dve.wait_ge(spread, 1)
                dve.tensor_copy(head_sign[:, :, 1], psD[:, 0:6]).then_inc(setup, 1)
                dve.tensor_copy(bv_all[:, :], psX[:, 0:O // 2]).then_inc(setup, 1)
                dve.tensor_copy(gates[:, :, :].rearrange("p a e -> p (a e)"), psD[:, 8:8 + 2 * E]).then_inc(setup, 1)
                dve.wait_ge(mask_ready, 3)
                dve.tensor_tensor(kx_bias[:, :, :], strided(head_mask[:, :], 0, [[0, 2], [1, 6]]),
                                  strided(qk_bias[:, :, :], 2, [[1, 2], [0, 6]]), ALU.mult).then_inc(setup, 1)
                dve.wait_ge(setup, 6)

                def values(m, s):
                    if not exists(m):
                        return
                    dve.wait_ge(v_done, m + 1)
                    if reused(m):
                        dve.wait_ge(av_done, m - 1)
                    dve.tensor_tensor(vals[s][:, :, :], psV[:, 0:O].rearrange("p (i v) -> p i v", i=2),
                                      strided(bv_all[:, :], 0, [[0, 2], [1, O // 2]]), ALU.add).then_inc(v_ready, 1)

                def shift(m, s):
                    if not exists(m):
                        return
                    dve.wait_ge(scored, m + 1)
                    if reused(m):
                        dve.wait_ge(pm_ready, m - 1)
                    dve.tensor_reduce(top[s][:, :], paired(psA), AX.X, ALU.max).then_inc(top_ready, 1)
                    dve.wait_ge(top_ready, m + 1)
                    dve.tensor_tensor(ex[s][:, :, :].rearrange("p (b h) k -> p b h k", b=2), paired(psA), by_head(top[s]),
                                      ALU.subtract).then_inc(shifted, 1)

                def maps(m, s):
                    if not exists(m):
                        return
                    dve.wait_ge(exped, m + 1)
                    dve.tensor_reduce(den[s][:, :], ex[s][:, :, :], AX.X, ALU.add).then_inc(den_ready, 1)
                    dve.wait_ge(den_ready, m * 2 + 1)
                    dve.reciprocal(den[s][:, :], den[s][:, :]).then_inc(den_ready, 1)
                    dve.wait_ge(den_ready, m * 2 + 2)
                    dve.tensor_tensor(coef[s][:, :], den[s][:, :], head_sign[:, :, :].rearrange("p e m -> p (e m)"),
                                      ALU.mult).then_inc(coef_ready, 1)
                    dve.wait_ge(coef_ready, m + 1)
                    if reused(m):
                        dve.wait_ge(diffed, m - 1)
                    for b in range(2):
                        last = dve.tensor_tensor(pm[s][:, :, 3 * b:3 * b + 3, 0:N].rearrange("p m e k -> p e m k"),
                                                 ex[s][:, 6 * b:6 * b + 6, :].rearrange("p (e m) k -> p e m k", m=2),
                                                 strided(coef[s][:, :], 6 * b, [[2, 3], [1, 2], [0, N]]), ALU.mult)
                    last.then_inc(pm_ready, 1)

                def outputs(m, s):
                    if not exists(m):
                        return
                    dve.wait_ge(sq_ready, m + 1)
                    dve.tensor_scalar(OUTS[:, bass.ds(m * HROW, O)].rearrange("p (f g v) -> p f g v", f=3, g=2), head_order(psX),
                                      1.0, None, ALU.mult).then_inc(out_ready, 1)
                    dve.tensor_reduce(ssq[s][:, :], sq[s][:, :].rearrange("p (e v) -> p e v", e=6), AX.X,
                                      ALU.add).then_inc(ssq_ready, 1)
                    dve.wait_ge(ssq_ready, m + 1)
                    dve.tensor_scalar(SSQ[:, bass.ds(m * 6, 6)], ssq[s][:, :], 1.0, None, ALU.mult)

                def step_of(i, s):
                    maps(i, s)
                    shift(i + 1, 1 - s)
                    values(i + 1, 1 - s)
                    outputs(i - 1, 1 - s)

                for i in range(-2, FIRST_STEP):
                    step_of(i, i % 2)
                with dve.Fori(0, (LAST_STEP - FIRST_STEP) // 2) as t:
                    for e in range(2):
                        step_of(t * 2 + (FIRST_STEP + e), e)
                for i in range(LAST_STEP, PAIRS + 1):
                    step_of(i, i % 2)

            @block.scalar
            def _(act):
                act.wait_ge(lam_ready, 2)
                act.activation(lam_exp[:, :], lam_sum[:, :], ACT.Exp).then_inc(lam_expd, 1)
                act.wait_ge(setup, 6)

                def keys(m, s):
                    if not exists(m):
                        return
                    act.wait_ge(k_done, m + 1)
                    if reused(m):
                        act.wait_ge(scored, m - 1)
                    for h in range(2):
                        kT = psK[0:HO, h * 128:(h + 1) * 128].rearrange("c (i t) -> c i t", i=2)[:, :, 0:N]
                        for e in range(6):
                            last = act.activation(kx[s][:, h, :, e, :], kT, ACT.Identity,
                                                  bias=kx_bias[:, h, e:e + 1], scale=head_mask[:, e:e + 1])
                    last.then_inc(kx_ready, 1)

                def queries(m, s):
                    if not exists(m):
                        return
                    act.wait_ge(q_done, m + 1)
                    for h in range(2):
                        last = act.activation(qT[s][:, h, :], psQ[0:HO, h * 128:(h + 1) * 128], ACT.Identity,
                                              bias=q_bias[:, h:h + 1], scale=SCALE)
                    last.then_inc(q_ready, 1)

                def exps(m, s):
                    if not exists(m):
                        return
                    act.wait_ge(shifted, m + 1)
                    act.activation(ex[s][:, :, :], ex[s][:, :, :], ACT.Exp).then_inc(exped, 1)

                def differences(m, s):
                    if not exists(m):
                        return
                    act.wait_ge(diffed, m + 1)
                    if reused(m):
                        act.wait_ge(av_done, m - 1)
                    act.activation(dT[s][:, :, :].rearrange("p f q -> p (f q)"), psD[:, 0:3 * 128],
                                   ACT.Copy).then_inc(dT_ready, 1)

                def squares(m, s):
                    if not exists(m):
                        return
                    act.wait_ge(av_done, m + 1)
                    if reused(m):
                        act.wait_ge(ssq_ready, m - 1)
                    act.activation(sq[s][:, :].rearrange("p (f g v) -> p f g v", f=3, g=2), head_order(psX),
                                   ACT.Square).then_inc(sq_ready, 1)

                def step_of(i, s):
                    keys(i + 2, s)
                    queries(i + 2, s)
                    exps(i + 1, 1 - s)
                    squares(i - 1, 1 - s)
                    differences(i, s)

                for i in range(-2, FIRST_STEP):
                    step_of(i, i % 2)
                with act.Fori(0, (LAST_STEP - FIRST_STEP) // 2) as t:
                    for e in range(2):
                        step_of(t * 2 + (FIRST_STEP + e), e)
                for i in range(LAST_STEP, PAIRS + 1):
                    step_of(i, i % 2)

            @block.tensor
            def _(pe):
                pe.wait_ge(lam_ready, 3)
                pe.matmul(psD[:, 0:6], ones[0:1, 0:128], neg_lam[:, 0:1].to_broadcast([1, 6]), start=True, stop=True)
                pe.matmul(psD[:, 8:8 + 2 * E], ones[0:1, 0:128], gates_row[:, :, :].rearrange("p a e -> p (a e)"),
                          start=True, stop=True)
                bv_view = bv_row[:, :].rearrange("p (f g v) -> p g f v", g=2, v=2 * HD)
                for g in range(2):
                    last = pe.matmul(psX[64 * g:64 * g + 64, 0:O // 2], ones[0:1, 0:64], bv_view[:, g, :, :],
                                     start=True, stop=True)
                last.then_inc(spread, 1)
                pe.wait_ge(setup, 6)

                def project(m, s, n, psum, copied, done):
                    if not exists(m):
                        return
                    pe.wait_ge(hp_ready, m + 1)
                    if another(m):
                        pe.wait_ge(copied, m)
                    for h in range(2):
                        for k in range(2):
                            last = pe.matmul(psum[0:HO, h * 128:(h + 1) * 128], wqkv[:, n, k, h * HO:(h + 1) * HO],
                                             hp[s][:, k, :], start=(k == 0), stop=(k == 1))
                    last.then_inc(done, 1)

                def project_values(m, s):
                    if not exists(m):
                        return
                    if another(m):
                        pe.wait_ge(v_ready, m)
                        pe.sem_inc(weighing, 1)
                    for i in range(2):
                        for g in range(2):
                            for k in range(2):
                                rhs = wqkv[:, 2, k, :].rearrange("c (f g v) -> c g f v", g=2, v=2 * HD)[:, g, :, :]
                                last = pe.matmul(psV[64 * g:64 * g + 64, i * HO:(i + 1) * HO],
                                                 hp[s][:, k, 64 * i:64 * i + 64], rhs, start=(k == 0), stop=(k == 1))
                    last.then_inc(v_done, 1)

                def scores(m, s):
                    if not exists(m):
                        return
                    pe.wait_ge(q_ready, m + 1)
                    pe.wait_ge(kx_ready, m + 1)
                    if another(m):
                        pe.wait_ge(shifted, m)
                    for i in range(2):
                        for h in range(2):
                            last = pe.matmul(psA[64 * i:64 * i + 64, h * 512:h * 512 + 6 * N],
                                             qT[s][:, h, 64 * i:64 * i + 64],
                                             kx[s][:, h, i, :, :].rearrange("c h k -> c (h k)"),
                                             start=True, stop=True)
                    last.then_inc(scored, 1)

                def turn_maps(m, s):
                    if not exists(m):
                        return
                    pe.wait_ge(pm_ready, m + 1)
                    if another(m):
                        pe.wait_ge(dT_ready, m)
                    for f in range(3):
                        for n in range(2):
                            last = pe.matmul(psD[:, f * 128:(f + 1) * 128],
                                             pm[s][:, n, 2 * f:2 * f + 2, :].rearrange("p e k -> p (e k)"),
                                             ident[:, :], is_transpose=True, start=(n == 0), stop=(n == 1))
                    last.then_inc(diffed, 1)

                def weigh_values(m, s):
                    if not exists(m):
                        return
                    pe.wait_ge(dT_ready, m + 1)
                    pe.wait_ge(v_ready, m + 1)
                    if another(m):
                        pe.wait_ge(out_ready, m)
                        pe.wait_ge(sq_ready, m)
                    pe.sem_inc(weighing, 1)
                    for i in range(2):
                        for f in range(3):
                            for g in range(2):
                                last = pe.matmul(psX[64 * i:64 * i + 64, g * 512 + f * 2 * HD:g * 512 + (f + 1) * 2 * HD],
                                                 dT[s][64 * g:64 * g + N, f, 64 * i:64 * i + 64],
                                                 vals[s][64 * g:64 * g + N, i, f * 2 * HD:(f + 1) * 2 * HD],
                                                 start=True, stop=True)
                    last.then_inc(av_done, 1)

                def step_of(i, s):
                    scores(i + 1, 1 - s)
                    project(i + 2, s, 1, psK, kx_ready, k_done)
                    project_values(i + 1, 1 - s)
                    project(i + 2, s, 0, psQ, q_ready, q_done)
                    turn_maps(i, s)
                    weigh_values(i - 1, 1 - s)

                for i in range(-2, FIRST_STEP):
                    step_of(i, i % 2)
                with pe.Fori(0, (LAST_STEP - FIRST_STEP) // 2) as t:
                    for e in range(2):
                        step_of(t * 2 + (FIRST_STEP + e), e)
                for i in range(LAST_STEP, PAIRS + 1):
                    step_of(i, i % 2)


def mix(nc, d, HT, H2, SSQ, RL, ident, ones):
    with ExitStack() as ctx:
        def sb(name, shape, dt=F32):
            return ctx.enter_context(nc.sbuf_tensor(name, shape, dt))

        def sem(name):
            return ctx.enter_context(nc.semaphore(name))

        def ps(name, banks):
            return ctx.enter_context(nc.psum_tensor(name, [128, banks * 512], F32))

        wo = sb("wo", [HO + 1, 2, O])
        nw = sb("nw", [HO, 1])
        eps = sb("eps", [128, 1])
        hw = [sb(f"hw{s}", [HO, 2, 128]) for s in range(2)]
        on = [sb(f"on{s}", [128, O]) for s in range(2)]
        oT = [sb(f"oT{s}", [HO + 1, 2, 128]) for s in range(2)]
        hn = [sb(f"hn{s}", [128, O]) for s in range(2)]
        hnT = [sb(f"hnT{s}", [HO + 1, 2, 128]) for s in range(2)]
        rms = sb("rms", [128, PAIRS * 6])
        st = [sb(f"ln_st{s}", [128, 6]) for s in range(2)]
        mv = [sb(f"ln_mv{s}", [128, 2]) for s in range(2)]
        dev = [sb(f"ln_dev{s}", [128, 1]) for s in range(2)]
        rstd = [sb(f"ln_rstd{s}", [128, 1]) for s in range(2)]
        rw = sb("rw", [E, O])
        pw = sb("pw", [DR, O])
        emb = sb("emb", [E, DR])
        emb2 = sb("emb2", [E, DR])
        embn = sb("embn", [E, DR])
        embT = sb("embT", [DR, E])
        gain = sb("gain", [E, 4])
        align = sb("align", [E, O])
        RW = sb("RW", [HO + 1, 2, RC])
        bias8 = sb("bias8", [HO + 1, 3, E])

        psO = [ps(f"m_psO{s}", 1) for s in range(2)]
        psM = [ps(f"m_psM{s}", 1) for s in range(2)]
        psN = [ps(f"m_psN{s}", 1) for s in range(2)]
        psR = [ps(f"m_psR{s}", 1) for s in range(2)]

        w_in = sem("m_w_in")
        eps_ready = sem("eps_ready")
        step = sem("m_step")
        rooted = sem("m_rooted")
        turned = sem("m_turned")
        wo_ready = sem("wo_ready")
        hw_ready = sem("hw_ready")
        on_ready = sem("on_ready")
        o_turned = sem("o_turned")
        oT_ready = sem("oT_ready")
        mixed = sem("mixed")
        stats_ready = sem("stats_ready")
        stats_waited = sem("stats_waited")
        mv_ready = sem("mv_ready")
        dev_ready = sem("dev_ready")
        rstd_ready = sem("rstd_ready")
        hn_ready = sem("hn_ready")
        hn_turned = sem("hn_turned")
        hnT_ready = sem("hnT_ready")
        routed = sem("routed")
        rl_ready = sem("rl_ready")

        def exists(m):
            return not isinstance(m, int) or 0 <= m < PAIRS

        def reused(m):
            return not isinstance(m, int) or m >= 2

        with nc.Block() as block:
            @block.sync
            def _(sp):
                sp.dma_start(wo[0:HO, :, :], d["Wo"].rearrange("(k c) o -> c k o", k=2)).then_inc(w_in, 16)
                for n in range(3):
                    sp.dma_start(nw[32 * n:32 * n + 32, :], d["norm_weight"].rearrange("(n a) -> n a", a=1)).then_inc(w_in, 16)
                sp.dma_start(wo[HO:HO + 1, 0, :], d["bo"].rearrange("(a n) -> a n", a=1)).then_inc(w_in, 16)
                sp.dma_start(rw[:, :], d["router_w"]).then_inc(w_in, 16)
                sp.dma_start(pw[:, :], d["probe_w"]).then_inc(w_in, 16)
                sp.dma_start(emb[:, :], d["router_emb"]).then_inc(w_in, 16)
                sp.dma_start(bias8[HO:HO + 1, 0, :], d["energy"].rearrange("(a n) -> a n", a=1)).then_inc(w_in, 16)
                sp.dma_start(bias8[HO:HO + 1, 1, :], d["fatigue"].rearrange("(a n) -> a n", a=1)).then_inc(w_in, 16)

            @block.gpsimd
            def _(pool):
                def window(m, s, first=False):
                    if not first:
                        pool.wait_ge(mixed, m - 1)
                    view = HT[:, :, bass.ds(m * (2 * N), N + 64)]
                    pool.tensor_copy(hw[s][:, :, :].rearrange("c h (i t) -> c h i t", i=2),
                                     bass.AP(tensor=view.tensor, offset=view.offset,
                                             ap=[list(view.ap[0]), [TP, 2], [N, 2], [1, 64]])).then_inc(hw_ready, 1)

                window(0, 0, first=True)
                window(1, 1, first=True)
                with pool.Fori(0, PAIRS // 2 - 1) as t:
                    for e in range(2):
                        window(t * 2 + (e + 2), e)

            @block.vector
            def _(dve):
                dve.memset(eps[:, :], EPS).then_inc(eps_ready, 1)
                for s in range(2):
                    dve.memset(oT[s][HO:HO + 1, 0, :], 1.0)
                    dve.memset(hnT[s][HO:HO + 1, 0, :], 1.0)
                dve.memset(RW[HO:HO + 1, 0, :], 0.0).then_inc(step, 1)
                dve.wait_ge(w_in, 16 * 10)
                dve.tensor_tensor(emb2[:, :], emb[:, :], emb[:, :], ALU.mult).then_inc(step, 1)
                dve.wait_ge(step, 2)
                dve.tensor_reduce(gain[:, 0:1], emb2[:, :], AX.X, ALU.add).then_inc(step, 1)
                dve.tensor_scalar(wo[0:HO, :, :], wo[0:HO, :, :], nw[:, 0:1], 1.0 - LAMBDA_INIT, ALU.mult,
                                  ALU.mult).then_inc(wo_ready, 1)
                dve.tensor_scalar(bias8[HO:HO + 1, 2, :], bias8[HO:HO + 1, 1, :], 0.1, None, ALU.mult).then_inc(step, 1)
                dve.wait_ge(step, 4)
                dve.scalar_tensor_tensor(out=RW[HO:HO + 1, 0, 0:E], in0=bias8[HO:HO + 1, 0, :], scalar=0.1,
                                         in1=bias8[HO:HO + 1, 2, :],
                                         op0=ALU.mult, op1=ALU.subtract).then_inc(step, 1)
                dve.wait_ge(rooted, 2)
                dve.tensor_scalar(gain[:, 2:3], gain[:, 1:2], 1e-12, None, ALU.max).then_inc(step, 1)
                dve.wait_ge(step, 6)
                dve.reciprocal(gain[:, 2:3], gain[:, 2:3]).then_inc(step, 1)
                dve.tensor_scalar(gain[:, 3:4], gain[:, 1:2], 0.02 / O, 0.02 / O, ALU.mult, ALU.add).then_inc(step, 1)
                dve.wait_ge(step, 8)
                dve.tensor_scalar(embn[:, :], emb[:, :], gain[:, 2:3], None, ALU.mult).then_inc(step, 1)
                dve.tensor_scalar(rw[:, :], rw[:, :], gain[:, 3:4], None, ALU.add).then_inc(step, 1)
                dve.wait_ge(turned, 1)
                dve.tensor_copy(embT[:, :], psR[0][0:DR, 0:E]).then_inc(step, 1)
                dve.wait_ge(turned, 2)
                dve.tensor_copy(align[:, :], psR[1][0:E, 0:O]).then_inc(step, 1)
                dve.wait_ge(turned, 3)
                dve.tensor_copy(RW[0:HO, :, :].rearrange("c k n -> c (k n)"), psR[0][0:HO, 0:2 * RC]).then_inc(step, 1)
                dve.reciprocal(rms[:, :], rms[:, :]).then_inc(step, 1)
                dve.wait_ge(step, 14)

                def normed(m, s):
                    if not exists(m):
                        return
                    if reused(m):
                        dve.wait_ge(o_turned, m - 1)
                    factor = rms[:, bass.ds(m * 6, 6)]
                    dve.tensor_tensor(on[s][:, :].rearrange("p (e v) -> p e v", e=6),
                                      H2[:, bass.ds(m * HROW, O)].rearrange("p (e v) -> p e v", e=6),
                                      bass.AP(tensor=factor.tensor, offset=factor.offset,
                                              ap=[list(factor.ap[0]), [1, 6], [0, 2 * HD]]), ALU.mult)\
                        .then_inc(on_ready, 1)

                def statistics(m, s):
                    if not exists(m):
                        return
                    dve.wait_ge(mixed, m + 1)
                    dve.bn_stats(st[s][:, :], psM[s][:, 0:O]).then_inc(stats_ready, 1)
                    dve.wait_ge(stats_ready, m + 1)
                    dve.sem_inc(stats_waited, 1)
                    dve.bn_aggr(mv[s][:, :], st[s][:, :]).then_inc(mv_ready, 1)

                def layer_norm(m, s):
                    if not exists(m):
                        return
                    dve.wait_ge(dev_ready, m + 1)
                    dve.reciprocal(rstd[s][:, :], dev[s][:, :]).then_inc(rstd_ready, 1)
                    dve.wait_ge(rstd_ready, m + 1)
                    if reused(m):
                        dve.wait_ge(hn_turned, m - 1)
                    dve.tensor_scalar(hn[s][:, :], psM[s][:, 0:O], mv[s][:, 0:1], rstd[s][:, 0:1],
                                      ALU.subtract, ALU.mult).then_inc(hn_ready, 1)

                def keep_rows(m, s):
                    if not exists(m):
                        return
                    dve.wait_ge(hn_ready, m + 1)
                    dve.tensor_scalar(H2[:, bass.ds(m * HROW, O)], hn[s][:, :], 1.0, None, ALU.mult)

                def keep_router(m, s):
                    if not exists(m):
                        return
                    dve.wait_ge(routed, m + 1)
                    dve.tensor_scalar(RL[:, bass.ds(m * RC, RC)], psR[s][:, 0:RC], 1.0, None, ALU.mult).then_inc(rl_ready, 1)

                def step_of(i, s):
                    layer_norm(i - 2, s)
                    normed(i + 1, 1 - s)
                    keep_rows(i - 2, s)
                    statistics(i - 1, 1 - s)
                    keep_router(i - 4, s)

                for i in range(-1, FIRST):
                    step_of(i, i % 2)
                with dve.Fori(0, (LAST - FIRST) // 2) as t:
                    for e in range(2):
                        step_of(t * 2 + (FIRST + e), e)
                for i in range(LAST, PAIRS + 4):
                    step_of(i, i % 2)

            @block.scalar
            def _(act):
                act.wait_ge(eps_ready, 1)
                act.activation(rms[:, :], SSQ[:, :], ACT.Sqrt, bias=eps[:, 0:1], scale=1.0 / (2 * HD)).then_inc(rooted, 1)
                act.wait_ge(step, 3)
                act.activation(gain[:, 1:2], gain[:, 0:1], ACT.Sqrt).then_inc(rooted, 1)

                def copy_oT(m, s):
                    if not exists(m):
                        return
                    act.wait_ge(o_turned, m + 1)
                    if reused(m):
                        act.wait_ge(mixed, m - 1)
                    act.activation(oT[s][0:HO, :, :].rearrange("c k t -> c (k t)"), psO[s][0:HO, 0:256],
                                   ACT.Copy).then_inc(oT_ready, 1)

                def deviations(m, s):
                    if not exists(m):
                        return
                    act.wait_ge(mv_ready, m + 1)
                    if reused(m):
                        act.wait_ge(rstd_ready, m - 1)
                    act.activation(dev[s][:, :], mv[s][:, 1:2], ACT.Sqrt, bias=eps[:, 0:1]).then_inc(dev_ready, 1)

                def copy_hnT(m, s):
                    if not exists(m):
                        return
                    act.wait_ge(hn_turned, m + 1)
                    if reused(m):
                        act.wait_ge(routed, m - 1)
                    act.activation(hnT[s][0:HO, :, :].rearrange("c k t -> c (k t)"), psN[s][0:HO, 0:256],
                                   ACT.Copy).then_inc(hnT_ready, 1)

                def step_of(i, s):
                    copy_oT(i, s)
                    copy_hnT(i - 3, 1 - s)
                    deviations(i - 1, 1 - s)

                for i in range(-1, FIRST):
                    step_of(i, i % 2)
                with act.Fori(0, (LAST - FIRST) // 2) as t:
                    for e in range(2):
                        step_of(t * 2 + (FIRST + e), e)
                for i in range(LAST, PAIRS + 4):
                    step_of(i, i % 2)

            @block.tensor
            def _(pe):
                pe.wait_ge(step, 10)
                pe.transpose(psR[0][0:DR, 0:E], embn[:, :], ident[0:E, 0:E]).then_inc(turned, 1)
                pe.wait_ge(step, 11)
                pe.matmul(psR[1][0:E, 0:O], embT[:, :], pw[:, :], start=True, stop=True).then_inc(turned, 1)
                pe.wait_ge(step, 12)
                for k in range(2):
                    for at, rows, w in ((0, E, rw), (E, E, align), (2 * E, DR, pw)):
                        last = pe.transpose(psR[0][0:HO, k * RC + at:k * RC + at + rows], w[:, k * HO:(k + 1) * HO],
                                            ident[0:rows, 0:rows])
                last.then_inc(turned, 1)
                pe.wait_ge(wo_ready, 1)

                def turn(m, src, psum, ready, copied, done):
                    if not exists(m):
                        return
                    pe.wait_ge(ready, m + 1)
                    if reused(m):
                        pe.wait_ge(copied, m - 1)
                    for k in range(2):
                        last = pe.transpose(psum[0:HO, k * 128:(k + 1) * 128], src[:, k * HO:(k + 1) * HO], ident[:, :])
                    last.then_inc(done, 1)

                def project(m, s):
                    if not exists(m):
                        return
                    pe.wait_ge(oT_ready, m + 1)
                    pe.wait_ge(hw_ready, m + 1)
                    if reused(m):
                        pe.wait_ge(hn_ready, m - 1)
                    for k in range(2):
                        rows = HO + 1 - k
                        pe.matmul(psM[s][:, 0:O], oT[s][0:rows, k, :], wo[0:rows, k, :], start=(k == 0), stop=False,
                                  skip_group_check=True)
                    for h in range(2):
                        last = pe.matmul(psM[s][:, h * HO:(h + 1) * HO], hw[s][:, h, :], ident[0:HO, 0:HO], start=False,
                                         stop=(h == 1), skip_group_check=True)
                    last.then_inc(mixed, 1)

                def route(m, s):
                    if not exists(m):
                        return
                    pe.wait_ge(hnT_ready, m + 1)
                    if reused(m):
                        pe.wait_ge(rl_ready, m - 1)
                    for k in range(2):
                        rows = HO + 1 - k
                        last = pe.matmul(psR[s][:, 0:RC], hnT[s][0:rows, k, :], RW[0:rows, k, :], start=(k == 0),
                                         stop=(k == 1))
                    last.then_inc(routed, 1)

                def step_of(i, s):
                    turn(i, on[s], psO[s], on_ready, oT_ready, o_turned)
                    project(i - 1, 1 - s)
                    turn(i - 3, hn[1 - s], psN[1 - s], hn_ready, hnT_ready, hn_turned)
                    route(i - 4, s)

                pe.wait_ge(step, 13)
                for i in range(-1, FIRST):
                    step_of(i, i % 2)
                with pe.Fori(0, (LAST - FIRST) // 2) as t:
                    for e in range(2):
                        step_of(t * 2 + (FIRST + e), e)
                for i in range(LAST, PAIRS + 4):
                    step_of(i, i % 2)


def experts(nc, d, out, H2, W1, W2, RL, ident, ones):
    with ExitStack() as ctx:
        def sb(name, shape, dt=F32):
            return ctx.enter_context(nc.sbuf_tensor(name, shape, dt))

        def sem(name):
            return ctx.enter_context(nc.semaphore(name))

        def ps(name, banks):
            return ctx.enter_context(nc.psum_tensor(name, [128, banks * 512], F32))

        rl = RL[:, :].rearrange("p (m r) -> p m r", r=RC)
        valid = sb("valid", [128, 1])
        nowhere = sb("nowhere", [128, 1])
        below = sb("below", [128, 128])
        rank_i = sb("rank_i", [128, E], I32)
        rank_e = sb("rank_e", [128, E])
        place_i = sb("place_i", [128, PAIRS], I32)
        tile_i = sb("tile_i", [128, TILES], I32)
        tile_f = sb("tile_f", [128, TILES])
        probe2 = sb("probe2", [128, PAIRS, DR])
        norm = sb("norm", [128, 2, PAIRS])
        logit = sb("logit", [128, PAIRS, E])
        cand = sb("cand", [128, PAIRS, E])
        best = sb("best", [128, 4, PAIRS])
        one_hot = [sb(f"one_hot{n}", [128, PAIRS, E]) for n in range(2)]
        gate = sb("gate", [128, 3, PAIRS])
        picked = sb("picked", [128, PAIRS, E])
        total = sb("total", [128, PAIRS, E])
        run = [sb(f"run{n}", [128, PAIRS, E]) for n in range(2)]
        count_i = sb("count_i", [128, E], I32)
        ends = [sb(f"ends{n}", [128, E]) for n in range(3)]
        slot = sb("slot", [128, 2, PAIRS])
        scat = sb("scat", [128, 2, PAIRS], U32)
        past = sb("past", [128, TILES, E])
        owner_f = sb("owner_f", [128, TILES])
        owner_rank = sb("owner_rank", [128, TILES])
        owner = sb("owner", [1, TILES], I32)
        b2_all = sb("b2_all", [128, E * O])
        xg = [sb(f"xg{s}", [RT, HROW]) for s in range(2)]
        second = [sb(f"second{s}", [RT, 1]) for s in range(2)]
        dest = [sb(f"dest{s}", [RT, 1], U32) for s in range(2)]
        xgT = [sb(f"xgT{s}", [HO + 1, 2, RT]) for s in range(2)]
        w1 = [sb(f"w1_{s}", [HO + 1, 2, H]) for s in range(2)]
        hidT = [sb(f"hidT{s}", [128, H // 128, RT]) for s in range(2)]
        yg = [sb(f"yg{s}", [RT, O]) for s in range(2)]
        back = [sb(f"back{s}", [128, 2, YG, O]) for s in range(YRING)]
        eps = sb("f_eps", [128, 1])
        st = sb("f_st", [128, PAIRS, 6])
        mv = sb("f_mv", [128, PAIRS, 2])
        dev = sb("f_dev", [128, PAIRS])
        rstd = sb("f_rstd", [128, PAIRS])

        psT = ps("f_psT", 1)
        psH = [ps(f"f_psH{s}", 2) for s in range(2)]
        psC = ps("f_psC", 2)
        psY = [ps("f_psY", 1), psC]

        const = sem("f_const")
        below_ready = sem("below_ready")
        b2_in = sem("b2_in")
        step = sem("f_step")
        rooted = sem("f_rooted")
        counted = sem("counted")
        slots_ready = sem("slots_ready")
        owner_ready = sem("owner_ready")
        scattered = sem("scattered")
        xg_in = [sem(f"xg_in{s}") for s in range(2)]
        xg_turned = sem("xg_turned")
        xgT_ready = sem("xgT_ready")
        hidden = sem("hidden")
        w1_ready = sem("w1_ready")
        rectified = sem("rectified")
        hidT_ready = sem("hidT_ready")
        y_done = sem("f_y_done")
        yg_ready = sem("yg_ready")
        y_stored = [sem(f"y_stored{s}") for s in range(2)]
        second_ready = sem("second_ready")
        dest_ready = sem("dest_ready")
        sending = sem("sending")
        back_clear = sem("back_clear")
        back_in = [sem(f"back_in{s}") for s in range(YRING)]
        scaled = sem("scaled")
        added = sem("added")
        final = sem("final")
        stored = sem("f_stored")

        def exists(j):
            return not isinstance(j, int) or 0 <= j < TILES

        def reused(j):
            return not isinstance(j, int) or j >= 2

        def expert_of(eng, j):
            return eng.value_load(owner[0:1, bass.ds(j, 1)], min_val=0, max_val=E - 1)

        with nc.Block() as block:
            @block.gpsimd
            def _(pool):
                pool.memset(below[:, :], 1.0).then_inc(below_ready, 1)
                pool.wait_ge(below_ready, 1)
                pool.affine_select(out=below[:, :], in_=below[:, :], compare_op=ALU.is_ge, fill=0.0, base=-1,
                                   pattern=[[1, 128]], channel_multiplier=-1).then_inc(below_ready, 1)
                pool.iota(rank_i[:, :], pattern=[[-1, E]], base=E, channel_multiplier=0).then_inc(const, 1)
                pool.iota(tile_i[:, :], pattern=[[1, TILES]], base=0, channel_multiplier=0).then_inc(const, 1)
                pool.iota(place_i[:, :], pattern=[[128, PAIRS]], base=0, channel_multiplier=1).then_inc(const, 1)
                pool.wait_ge(slots_ready, 1)
                for m in range(PAIRS):
                    for n in range(2):
                        pool.indirect_dma_start(out=d["xg"], out_offset=bass.IndirectOffsetOnAxis(
                            ap=scat[:, n, m:m + 1], axis=0), in_=H2[:, m * HROW:(m + 1) * HROW], in_offset=None,
                            bounds_check=SLOTS - 1, oob_is_err=False).then_inc(scattered, 16)

                def send(j, s):
                    pool.wait_ge(dest_ready, j + 1)
                    pool.wait_ge(yg_ready, j + 1)
                    pool.sem_inc(sending, 1)
                    pool.indirect_dma_start(out=d["yd"], out_offset=bass.IndirectOffsetOnAxis(ap=dest[s][:, 0:1], axis=0),
                                            in_=yg[s][:, :], in_offset=None, bounds_check=2 * ROWS - 1,
                                            oob_is_err=False).then_inc(y_stored[s], 16)

                with pool.Fori(0, TILES // 2) as t:
                    for e in range(2):
                        send(t * 2 + e, e)

            @block.vector
            def _(dve):
                links = [0]

                def link(ins):
                    links[0] += 1
                    ins.then_inc(step, 1)
                    dve.wait_ge(step, links[0])

                def over_experts(view):
                    return strided(view, 0, [[1, PAIRS], [0, E]])

                def over_pairs(view):
                    return strided(view, 0, [[0, PAIRS], [1, E]])

                dve.memset(valid[:, :], 0.0)
                dve.memset(eps[:, :], EPS)
                for s in range(2):
                    dve.memset(xgT[s][HO:HO + 1, 0, :], 1.0)
                link(dve.memset(nowhere[:, :], float(4 * SLOTS)))
                for i in range(2):
                    dve.memset(valid[64 * i:64 * i + N, :], 1.0)
                    last = dve.memset(nowhere[64 * i:64 * i + N, :], 0.0)
                link(last)
                dve.wait_ge(const, 3)
                dve.tensor_copy(rank_e[:, :], rank_i[:, :])
                dve.tensor_copy(tile_f[:, :], tile_i[:, :])
                link(dve.tensor_tensor(probe2[:, :, :], rl[:, :, 2 * E:RC], rl[:, :, 2 * E:RC], ALU.mult))
                link(dve.tensor_reduce(norm[:, 0, :], probe2[:, :, :], AX.X, ALU.add))
                dve.wait_ge(rooted, 1)
                link(dve.tensor_scalar(norm[:, 1, :], norm[:, 1, :], 1e-12, None, ALU.max))
                link(dve.reciprocal(norm[:, 1, :], norm[:, 1, :]))
                link(dve.tensor_tensor(cand[:, :, :], rl[:, :, E:2 * E], over_experts(norm[:, 1, :]), ALU.mult))
                link(dve.scalar_tensor_tensor(out=logit[:, :, :], in0=cand[:, :, :], scalar=0.02, in1=rl[:, :, 0:E],
                                              op0=ALU.mult, op1=ALU.add))
                for n in range(2):
                    link(dve.tensor_reduce(best[:, n, :], logit[:, :, :], AX.X, ALU.max))
                    link(dve.tensor_tensor(cand[:, :, :], logit[:, :, :], over_experts(best[:, n, :]), ALU.is_equal))
                    link(dve.tensor_tensor(cand[:, :, :], cand[:, :, :], over_pairs(rank_e[:, :]), ALU.mult))
                    link(dve.tensor_reduce(best[:, 2 + n, :], cand[:, :, :], AX.X, ALU.max))
                    link(dve.tensor_tensor(one_hot[n][:, :, :], over_pairs(rank_e[:, :]), over_experts(best[:, 2 + n, :]),
                                           ALU.is_equal))
                    if n == 0:
                        link(dve.scalar_tensor_tensor(out=logit[:, :, :], in0=one_hot[0][:, :, :], scalar=-3e38,
                                                      in1=logit[:, :, :], op0=ALU.mult, op1=ALU.add))
                link(dve.tensor_tensor(picked[:, :, :], one_hot[0][:, :, :], one_hot[1][:, :, :], ALU.add))
                link(dve.tensor_scalar(picked[:, :, :], picked[:, :, :], valid[:, 0:1], None, ALU.mult))
                assert links[0] == PICKED
                rows = H2[:, :].rearrange("p (m r) -> p m r", r=HROW)
                dve.tensor_scalar(rows[:, :, O], place_i[:, :], -1.0, float(FAR_ROW), ALU.mult, ALU.add)
                dve.tensor_scalar(rows[:, :, O + 1], best[:, 2, :], 1.0, None, ALU.mult)
                link(dve.tensor_tensor(gate[:, 2, :], best[:, 1, :], best[:, 0, :], ALU.subtract))
                dve.wait_ge(counted, 1)
                link(dve.tensor_copy(total[:, :, :], psC[:, 512:512 + PAIRS * E].rearrange("p (m e) -> p m e", e=E)))
                src = total
                for n in range(5):
                    dst, reach = run[n % 2], 1 << n
                    dve.tensor_copy(dst[:, 0:reach, :], src[:, 0:reach, :])
                    link(dve.tensor_tensor(dst[:, reach:PAIRS, :], src[:, reach:PAIRS, :], src[:, 0:PAIRS - reach, :],
                                           ALU.add))
                    src = dst
                link(dve.tensor_scalar(count_i[:, :], src[:, PAIRS - 1, :], float(RT - 1), None, ALU.add))
                link(dve.tensor_scalar(count_i[:, :], count_i[:, :], RT.bit_length() - 1, None, ALU.arith_shift_right))
                link(dve.tensor_copy(ends[0][:, :], count_i[:, :]))
                link(dve.tensor_tensor(run[1 - 0][:, :, :], src[:, :, :], total[:, :, :], ALU.subtract))
                eat = ends[0]
                for n in range(3):
                    dst, reach = ends[1 + n % 2], 1 << n
                    dve.tensor_copy(dst[:, 0:reach], eat[:, 0:reach])
                    link(dve.tensor_tensor(dst[:, reach:E], eat[:, reach:E], eat[:, 0:E - reach], ALU.add))
                    eat = dst
                link(dve.tensor_tensor(ends[0][:, :], eat[:, :], ends[0][:, :], ALU.subtract))
                link(dve.tensor_scalar(ends[0][:, :], ends[0][:, :], float(RT), None, ALU.mult))
                link(dve.tensor_tensor(run[1][:, :, :], run[1][:, :, :], over_pairs(ends[0][:, :]), ALU.add))
                link(dve.tensor_tensor(run[1][:, :, :], run[1][:, :, :],
                                       psC[:, 0:PAIRS * E].rearrange("p (m e) -> p m e", e=E), ALU.add))
                for n in range(2):
                    link(dve.tensor_tensor(cand[:, :, :], run[1][:, :, :], one_hot[n][:, :, :], ALU.mult))
                    link(dve.tensor_reduce(slot[:, n, :], cand[:, :, :], AX.X, ALU.add))
                for n in range(2):
                    last = dve.tensor_scalar(scat[:, n, :], slot[:, n, :], valid[:, 0:1], nowhere[:, 0:1], ALU.mult,
                                             ALU.add)
                last.then_inc(slots_ready, 1)
                link(dve.tensor_tensor(past[:, :, :], strided(tile_f[:, :], 0, [[1, TILES], [0, E]]),
                                       strided(eat[:, :], 0, [[0, TILES], [1, E]]), ALU.is_ge))
                link(dve.tensor_reduce(owner_f[:, :], past[:, :, :], AX.X, ALU.add))
                dve.tensor_scalar(owner_rank[:, :], owner_f[:, :], -1.0, float(E), ALU.mult, ALU.add)
                dve.tensor_scalar(owner[:, :], owner_f[0:1, :], float(E - 1), None, ALU.min).then_inc(owner_ready, 1)
                for s in range(YRING):
                    last = dve.memset(back[s][:, :, :, :], 0.0)
                last.then_inc(back_clear, 1)
                dve.wait_ge(rooted, 2)
                link(dve.tensor_scalar(gate[:, 0, :], gate[:, 2, :], 1.0, None, ALU.add))
                link(dve.reciprocal(gate[:, 0, :], gate[:, 0, :]))
                link(dve.tensor_tensor(gate[:, 1, :], gate[:, 2, :], gate[:, 0, :], ALU.mult))

                def stage(j, s):
                    if not exists(j):
                        return
                    e = expert_of(dve, j)
                    if reused(j):
                        dve.wait_ge(hidden, j - 1)
                    for k in range(2):
                        rows = HO + 1 - k
                        last = dve.tensor_copy(w1[s][0:rows, k, :], W1[0:rows, bass.ds(e * (2 * H) + k * H, H)])
                    last.then_inc(w1_ready, 1)

                def rectify(j, s):
                    if not exists(j):
                        return
                    dve.wait_ge(hidden, j + 1)
                    if reused(j):
                        dve.wait_ge(y_done, j - 1)
                    dve.tensor_scalar(hidT[s][:, :, :].rearrange("c b t -> c (b t)"), psH[s][:, 0:H], 0.0, None,
                                      ALU.max).then_inc(rectified, 1)

                def keep(j, s):
                    if not exists(j):
                        return
                    e = expert_of(dve, j)
                    dve.wait_ge(y_done, j + 1)
                    if reused(j):
                        dve.wait_ge(y_stored[s], j * 8 - 8 * s)
                    dve.tensor_tensor(yg[s][:, :], psY[s][:, 0:O], b2_all[:, bass.ds(e * O, O)], ALU.add)\
                        .then_inc(yg_ready, 1)

                def address(j, s):
                    if not exists(j):
                        return
                    dve.wait_ge(xg_in[s], j * 8 + (16 - 8 * s))
                    if reused(j):
                        dve.wait_ge(y_stored[s], j * 8 - 8 * s)
                    dve.tensor_scalar(second[s][:, :], xg[s][:, O + 1:O + 2], owner_rank[:, bass.ds(j, 1)], float(ROWS),
                                      ALU.not_equal, ALU.mult).then_inc(second_ready, 1)
                    dve.wait_ge(second_ready, j + 1)
                    dve.scalar_tensor_tensor(out=dest[s][:, :], in0=second[s][:, :], scalar=float(FAR_ROW),
                                             in1=xg[s][:, O:O + 1], op0=ALU.add, op1=ALU.subtract).then_inc(dest_ready, 1)

                def step_of(i, s):
                    stage(i + 2, s)
                    rectify(i + 1, 1 - s)
                    address(i + 1, 1 - s)
                    keep(i, s)

                dve.wait_ge(owner_ready, 1)
                dve.wait_ge(b2_in, 16)
                for i in range(-2, 2):
                    step_of(i, i % 2)
                with dve.Fori(0, TILES // 2 - 2) as t:
                    for e in range(2):
                        step_of(t * 2 + (2 + e), e)
                for i in range(TILES - 2, TILES):
                    step_of(i, i % 2)

                for q in range(PAIRS // YG):
                    rows4 = rows[:, q * YG:(q + 1) * YG, 0:O]
                    for n in range(2):
                        dve.wait_ge(scaled, 2 * YG * q + YG * (n + 1))
                        if n == 1:
                            dve.wait_ge(added, 2 * q + 1)
                        dve.tensor_tensor(rows4, rows4, back[q % YRING][:, n, :, :], ALU.add).then_inc(added, 1)
                    dve.wait_ge(added, 2 * q + 2)
                    for m in range(q * YG, (q + 1) * YG):
                        last = dve.bn_stats(st[:, m, :], H2[:, m * HROW:m * HROW + O])
                link(last)
                for m in range(PAIRS):
                    last = dve.bn_aggr(mv[:, m, :], st[:, m, :])
                link(last)
                assert links[0] == AGGREGATED
                dve.wait_ge(rooted, 3)
                link(dve.reciprocal(rstd[:, :], dev[:, :]))
                for m in range(PAIRS):
                    row = H2[:, m * HROW:m * HROW + O]
                    dve.tensor_scalar(row, row, mv[:, m, 0:1], rstd[:, m:m + 1], ALU.subtract, ALU.mult).then_inc(final, 1)

            @block.scalar
            def _(act):
                act.wait_ge(step, 4)
                act.activation(norm[:, 1, :], norm[:, 0, :], ACT.Sqrt).then_inc(rooted, 1)
                act.wait_ge(step, PICKED + 1)
                act.activation(gate[:, 2, :], gate[:, 2, :], ACT.Exp).then_inc(rooted, 1)

                def copy_xgT(j, s):
                    if not exists(j):
                        return
                    act.wait_ge(xg_turned, j + 1)
                    if reused(j):
                        act.wait_ge(hidden, j - 1)
                    act.activation(xgT[s][0:HO, :, :].rearrange("c k t -> c (k t)"), psT[0:HO, 0:2 * RT],
                                   ACT.Copy).then_inc(xgT_ready, 1)

                def square(j, s):
                    if not exists(j):
                        return
                    act.wait_ge(rectified, j + 1)
                    hid = hidT[s][:, :, :]
                    act.activation(hid, hid, ACT.Square).then_inc(hidT_ready, 1)

                def step_of(i, s):
                    copy_xgT(i + 2, s)
                    square(i + 1, 1 - s)

                for i in range(-2, 2):
                    step_of(i, i % 2)
                with act.Fori(0, TILES // 2 - 2) as t:
                    for e in range(2):
                        step_of(t * 2 + (2 + e), e)
                for i in range(TILES - 2, TILES):
                    step_of(i, i % 2)
                for q in range(PAIRS // YG):
                    act.wait_ge(back_in[q % YRING], 64 * (q // YRING + 1))
                    for n in range(2):
                        for at in range(YG):
                            result = back[q % YRING][:, n, at, :]
                            m = q * YG + at
                            act.activation(result, result, ACT.Copy, scale=gate[:, n, m:m + 1]).then_inc(scaled, 1)
                act.wait_ge(step, AGGREGATED)
                act.activation(dev[:, :], mv[:, :, 1], ACT.Sqrt, bias=eps[:, 0:1]).then_inc(rooted, 1)

            @block.tensor
            def _(pe):
                flat = picked[:, :, :].rearrange("p m e -> p (m e)")
                pe.wait_ge(below_ready, 2)
                pe.wait_ge(step, PICKED)
                pe.matmul(psC[:, 0:PAIRS * E], below[:, :], flat, start=True, stop=True)
                pe.matmul(psC[:, 512:512 + PAIRS * E], ones[:, :], flat, start=True, stop=True).then_inc(counted, 1)
                pe.wait_ge(owner_ready, 1)

                def turn(j, s):
                    if not exists(j):
                        return
                    pe.wait_ge(xg_in[s], j * 8 + (16 - 8 * s))
                    if not isinstance(j, int) or j >= 1:
                        pe.wait_ge(xgT_ready, j)
                    for k in range(2):
                        last = pe.transpose(psT[0:HO, k * RT:(k + 1) * RT], xg[s][:, k * HO:(k + 1) * HO], ident[:, :])
                    last.then_inc(xg_turned, 1)

                def widen(j, s):
                    if not exists(j):
                        return
                    pe.wait_ge(xgT_ready, j + 1)
                    pe.wait_ge(w1_ready, j + 1)
                    if reused(j):
                        pe.wait_ge(rectified, j - 1)
                    for b in range(H // 128):
                        for k in range(2):
                            rows = HO + 1 - k
                            last = pe.matmul(psH[s][:, b * RT:(b + 1) * RT], w1[s][0:rows, k, b * 128:(b + 1) * 128],
                                             xgT[s][0:rows, k, :], start=(k == 0), stop=(k == 1))
                    last.then_inc(hidden, 1)

                def narrow(j, s):
                    if not exists(j):
                        return
                    e = expert_of(pe, j)
                    pe.wait_ge(hidT_ready, j + 1)
                    if reused(j):
                        pe.wait_ge(yg_ready, j - 1)
                    for b in range(H // 128):
                        last = pe.matmul(psY[s][:, 0:O], hidT[s][:, b, :],
                                         W2[:, bass.ds(e * (H // 128 * O) + b * O, O)],
                                         start=(b == 0), stop=(b == H // 128 - 1))
                    last.then_inc(y_done, 1)

                def step_of(i, s):
                    widen(i + 1, 1 - s)
                    turn(i + 2, s)
                    narrow(i, s)

                for i in range(-2, 2):
                    step_of(i, i % 2)
                with pe.Fori(0, TILES // 2 - 2) as t:
                    for e in range(2):
                        step_of(t * 2 + (2 + e), e)
                for i in range(TILES - 2, TILES):
                    step_of(i, i % 2)

            @block.sync
            def _(sp):
                sp.dma_start(b2_all[:, :], d["b2"].rearrange("(a e) o -> a (e o)", a=1).to_broadcast([128, E * O])).then_inc(b2_in, 16)
                sp.wait_ge(scattered, 16 * 2 * PAIRS)

                def load(j, s, first=False):
                    if not first:
                        sp.wait_ge(xg_turned, j - 1)
                        sp.wait_ge(dest_ready, j - 1)
                    sp.dma_start(xg[s][:, :], d["xg"][bass.ds(j * RT, RT), :]).then_inc(xg_in[s], 16)

                load(0, 0, first=True)
                load(1, 1, first=True)
                with sp.Fori(0, TILES // 2 - 1) as t:
                    for e in range(2):
                        load(t * 2 + (e + 2), e)
                for s in range(2):
                    sp.wait_ge(y_stored[s], 16 * (TILES // 2))
                sp.wait_ge(back_clear, 1)
                for q in range(PAIRS // YG):
                    if q >= YRING:
                        sp.wait_ge(added, 2 * (q - YRING + 1))
                    for n in range(2):
                        src = d["yd"][n * ROWS + q * YG * 128:n * ROWS + (q + 1) * YG * 128, :]\
                            .rearrange("(m p) o -> p m o", p=128)
                        for i in range(2):
                            sp.dma_start(back[q % YRING][64 * i:64 * i + N, n, :, :], src[64 * i:64 * i + N])\
                                .then_inc(back_in[q % YRING], 16)
                rows = out.rearrange("(m i) n o -> i n m o", i=2)
                for m in range(0, PAIRS, 4):
                    sp.wait_ge(final, m + 4)
                    for i in range(2):
                        sp.dma_start(rows[i, :, m:m + 4, :],
                                     H2[64 * i:64 * i + N, m * HROW:(m + 4) * HROW].rearrange("p (m r) -> p m r", r=HROW)[:, :, 0:O])\
                            .then_inc(stored, 16)
                sp.wait_ge(stored, 16 * (PAIRS // 2))


def vit_kernel(nc, d, out):
    d["off_all"] = nc.dram_tensor("off_all", [G, STR, NP, 2 * K], F32, kind="Internal").ap()
    d["xg"] = nc.dram_tensor("xg_all", [SLOTS, HROW], F32, kind="Internal").ap()
    d["yd"] = nc.dram_tensor("y_all", [2 * ROWS, O], F32, kind="Internal").ap()
    with ExitStack() as ctx:
        def sb(name, shape):
            return ctx.enter_context(nc.sbuf_tensor(name, shape, F32))

        ident = sb("ident", [128, 128])
        ones = sb("ones", [128, 128])
        HT = sb("HT", [HO, 2, TP])
        with nc.sbuf_tensor("dwT", [128, BLK, O], F32) as dwT, nc.sbuf_tensor("far", [1, 1], I32) as far:
            tokenizer(nc, d, HT, dwT, far, ident, ones)
            far_taps(nc, d, HT, dwT, far, ident, ones)
            batch_norm(nc, d, HT, HT)
        H2 = sb("H2", [128, PAIRS * HROW])
        SSQ = sb("SSQ", [128, PAIRS * 6])
        RL = sb("RL", [128, PAIRS * RC])
        W1 = sb("W1", [128, E * 2 * H])
        W2 = sb("W2", [128, E * H // 128 * O])
        attention(nc, d, HT, H2, SSQ, W1, W2, ident, ones)
        mix(nc, d, HT, H2, SSQ, RL, ident, ones)
        experts(nc, d, out, H2, W1, W2, RL, ident, ones)


_INS = ['x', 'L0_tok_offset_w', 'L0_tok_offset_b', 'L0_tok_dconv_w', 'L0_tok_bn_gamma', 'L0_tok_bn_beta', 'L0_attn_Wq', 'L0_attn_bq', 'L0_attn_Wk', 'L0_attn_bk', 'L0_attn_Wv', 'L0_attn_bv', 'L0_attn_Wo', 'L0_attn_bo', 'L0_attn_lambda_q1', 'L0_attn_lambda_k1', 'L0_attn_lambda_q2', 'L0_attn_lambda_k2', 'L0_attn_norm_weight', 'L0_ffn_router_w', 'L0_ffn_probe_w', 'L0_ffn_router_emb', 'L0_ffn_fatigue', 'L0_ffn_energy', 'L0_ffn_w_fast1', 'L0_ffn_w_slow1', 'L0_ffn_h_fast1', 'L0_ffn_m_gate1', 'L0_ffn_b1', 'L0_ffn_w_fast2', 'L0_ffn_w_slow2', 'L0_ffn_h_fast2', 'L0_ffn_m_gate2', 'L0_ffn_b2']
_OUT = (64, 49, 192)


def kernel(**inputs):
    import numpy as _np
    import concourse.bacc as _bacc
    from concourse import mybir as _mybir
    from concourse.bass_utils import run_bass_kernel_spmd as _run

    nc = _bacc.Bacc("TRN2", target_bir_lowering=False, num_devices=1)
    arrays, views = {}, {}
    for name in _INS:
        a = _np.ascontiguousarray(inputs[name])
        arrays[f"in_{name}"] = a
        short = name.replace("L0_tok_", "").replace("L0_attn_", "").replace("L0_ffn_", "")
        views[short] = nc.dram_tensor(f"in_{name}", a.shape, _mybir.dt.from_np(a.dtype), kind="ExternalInput").ap()
    out = nc.dram_tensor("out_0", _OUT, _mybir.dt.float32, kind="ExternalOutput").ap()
    vit_kernel(nc, views, out)
    r = _run(nc, [arrays], core_ids=[0])
    return r.results[0]["out_0"]
```
